# Optimizing a Trainium2 kernel written in Bass

```python
import numpy as np
import jax
import jax.numpy as jnp

def _softmax(x, axis=-1):
    return jax.nn.softmax(x, axis=axis)

def _gelu(x):
    return jax.nn.gelu(x, approximate=True)

def _silu(x):
    return jax.nn.silu(x)

def _sigmoid(x):
    return jax.nn.sigmoid(x)

def _layernorm(x, axis=-1, eps=1e-05):
    m = jnp.mean(x, axis=axis, keepdims=True)
    v = jnp.var(x, axis=axis, keepdims=True)
    return (x - m) / jnp.sqrt(v + eps)

def _scatter_add(tgt, idx, src, axis=0):
    return tgt.at[idx].add(src)

def _segment_sum(src, seg, n):
    return jax.ops.segment_sum(src, seg, n)
kernel_name = 'mk_perceiver_d4_seqx_r8_930c6c'

def setup_inputs(seed: int=0):
    np.random.seed(seed)
    _w = jnp.asarray

    def _rec_inputs():
        import jax
        import jax.numpy as jnp
        _rk = jax.random.key(seed)
        x = 7.22e-05 + 1 * jax.random.normal(jax.random.fold_in(_rk, 1), (32, 32, 128), jnp.float32)
        _lenS = 32 - jax.random.randint(jax.random.fold_in(_rk, 7), (32,), 0, max(1, 32 // 4) + 1, jnp.int32)
        _lenS2 = 257 - jax.random.randint(jax.random.fold_in(_rk, 8), (32,), 0, max(1, 257 // 4) + 1, jnp.int32)
        _ctx_1024P = jax.random.normal(jax.random.fold_in(_rk, 11), (32, 16, 128), jnp.float32)
        _ctx_1024c = jax.random.dirichlet(jax.random.fold_in(_rk, 511), 0.3 * jnp.ones((16,), jnp.float32), (32, 257))
        _ctx_1024t = jnp.einsum('bsk,bkd->bsd', _ctx_1024c, _ctx_1024P)
        _ctx_1024t = _ctx_1024t * jax.lax.rsqrt(jnp.mean(jnp.square(_ctx_1024t)) + 1e-12) * 0.953939
        ctx_1024 = 4.13588e-05 + 0.999923 * (_ctx_1024t + 0.3 * jax.random.normal(jax.random.fold_in(_rk, 611), (32, 257, 128), jnp.float32))
        _validS = jnp.arange(32)[None, :] < _lenS[:, None]
        _validS2 = jnp.arange(257)[None, :] < _lenS2[:, None]
        _causal = jnp.tril(jnp.ones((32, 32), dtype=bool))
        mask_SxS2_bk0 = jnp.logical_not(jnp.broadcast_to(_validS2[0:1, :], (32, 257)))
        return (x, ctx_1024, mask_SxS2_bk0)
    x, ctx_1024, mask_SxS2_bk0 = _rec_inputs()

    def _L0_xattn_setup():
        import jax, jax.numpy as jnp
        import numpy as np
        B, S, D, G = (4, 256, 128, 8)
        DK = D // G
        key = jax.random.key(seed)
        ks = jax.random.split(key, 9)
        s_in = 1.0 / np.sqrt(D)
        return {'Q': jax.random.normal(ks[0], (B, S, D), jnp.float32), 'K': jax.random.normal(ks[1], (B, S, D), jnp.float32), 'V': jax.random.normal(ks[2], (B, S, D), jnp.float32), 'Wq_w': jax.random.normal(ks[3], (D, D), jnp.float32) * s_in, 'Wq_b': jax.random.normal(ks[4], (D,), jnp.float32) * 0.01, 'Wkv_w': jax.random.normal(ks[5], (G, D, 2 * DK), jnp.float32) * s_in, 'Wkv_b': jax.random.normal(ks[6], (G, 2 * DK), jnp.float32) * 0.01, 'Wo_w': jax.random.normal(ks[7], (D, D), jnp.float32) * s_in, 'Wo_b': jax.random.normal(ks[8], (D,), jnp.float32) * 0.01}
    _L0_xattn_all = _L0_xattn_setup()
    _L0_xattn_in = {k: v for k, v in _L0_xattn_all.items() if k in ('Wq_w', 'Wq_b', 'Wkv_w', 'Wkv_b', 'Wo_w', 'Wo_b')}
    del _L0_xattn_all

    def _L0_attn_setup():
        import jax, jax.numpy as jnp
        import numpy as np
        B, S, D, H = (2, 256, 128, 16)
        HD = D // H
        key = jax.random.key(seed)
        k0, k1, k2 = jax.random.split(key, 3)
        return {'x': jax.random.normal(k0, (B, S, D), jnp.float32), 'qkv_w': jax.random.normal(k1, (D, 3 * D), jnp.float32) / np.sqrt(D).astype(np.float32), 'qkv_b': jnp.zeros((3 * D,), jnp.float32), 'out_w': jax.random.normal(k2, (D, D), jnp.float32) / np.sqrt(D).astype(np.float32), 'out_b': jnp.zeros((D,), jnp.float32)}
    _L0_attn_all = _L0_attn_setup()
    _L0_attn_in = {k: v for k, v in _L0_attn_all.items() if k in ('qkv_w', 'qkv_b', 'out_w', 'out_b')}
    del _L0_attn_all

    def _L0_ffn_setup():
        import jax, jax.numpy as jnp
        import numpy as np
        INT8_MAX = 127.0

        def _absmax_scale(x, axes):
            amax = jnp.max(jnp.abs(x), axis=axes, keepdims=True)
            return jnp.maximum(amax, 1e-12) / INT8_MAX
        key = jax.random.key(seed)
        k1, k2 = jax.random.split(key)
        lhs = jax.random.normal(k1, (4, 1024, 128), dtype=jnp.float32)
        rhs = jax.random.normal(k2, (128, 128), dtype=jnp.float32)
        return {'lhs': lhs, 'rhs': rhs}
    _L0_ffn_all = _L0_ffn_setup()
    _L0_ffn_in = {k: v for k, v in _L0_ffn_all.items() if k in ('rhs',)}
    del _L0_ffn_all

    def _L1_xattn_setup():
        import jax, jax.numpy as jnp
        import numpy as np
        DIM = 128
        QK_DIM = 128
        V_DIM = 128
        HEADS = 16
        key = jax.random.key(seed)
        k1, k2, k3, k4 = jax.random.split(key, 4)
        x = jax.random.normal(k1, (4, 256, DIM), dtype=jnp.float32)
        context = jax.random.normal(k2, (4, 256, DIM), dtype=jnp.float32)
        Wq = jax.random.normal(k3, (DIM, QK_DIM), dtype=jnp.float32) / np.sqrt(DIM)
        Wkv = jax.random.normal(k4, (DIM, QK_DIM + V_DIM), dtype=jnp.float32) / np.sqrt(DIM)
        return {'x': x, 'context': context, 'Wq': Wq, 'Wkv': Wkv}
    _L1_xattn_all = _L1_xattn_setup()
    _L1_xattn_in = {k: v for k, v in _L1_xattn_all.items() if k in ('Wq', 'Wkv')}
    del _L1_xattn_all

    def _L1_attn_setup():
        import math
        import jax, jax.numpy as jnp
        import numpy as np
        DIM = 128
        DIM_QK = 128
        DIM_V = 128
        NUM_BUCKETS = 32
        MAX_DISTANCE = 128

        def _rel_pos_bucket_causal(seq_len):
            q = np.arange(seq_len)
            n = np.maximum(q[:, None] - q[None, :], 0)
            max_exact = NUM_BUCKETS // 2
            is_small = n < max_exact
            nf = np.maximum(n, 1).astype(np.float32)
            val_if_large = max_exact + (np.log(nf / max_exact) / math.log(MAX_DISTANCE / max_exact) * (NUM_BUCKETS - max_exact)).astype(np.int32)
            val_if_large = np.minimum(val_if_large, NUM_BUCKETS - 1)
            return jnp.asarray(np.where(is_small, n, val_if_large), dtype=jnp.int32)

        def laplacian_attn_fn(x):
            mu = math.sqrt(0.5)
            std = math.sqrt(0.25 * math.pi)
            return (1.0 + jax.lax.erf((x - mu) / (std * math.sqrt(2.0)))) * 0.5
        key = jax.random.key(seed)
        ks = jax.random.split(key, 8)
        B, S = (8, 256)
        x = jax.random.normal(ks[0], (B, S, DIM), dtype=jnp.float32)
        Wqk = jax.random.normal(ks[1], (DIM, DIM_QK), dtype=jnp.float32) * (1.0 / math.sqrt(DIM))
        bqk = jnp.zeros((DIM_QK,), dtype=jnp.float32)
        gamma = jax.random.normal(ks[2], (2, DIM_QK), dtype=jnp.float32) * 0.02
        beta = jnp.zeros((2, DIM_QK), dtype=jnp.float32)
        Wv = jax.random.normal(ks[3], (DIM, DIM_V), dtype=jnp.float32) * (1.0 / math.sqrt(DIM))
        bv = jnp.zeros((DIM_V,), dtype=jnp.float32)
        rel_emb = jax.random.normal(ks[4], (NUM_BUCKETS, 1), dtype=jnp.float32) * 0.02
        return {'x': x, 'Wqk': Wqk, 'bqk': bqk, 'gamma': gamma, 'beta': beta, 'Wv': Wv, 'bv': bv, 'rel_emb': rel_emb}
    _L1_attn_all = _L1_attn_setup()
    _L1_attn_in = {k: v for k, v in _L1_attn_all.items() if k in ('Wqk', 'bqk', 'gamma', 'beta', 'Wv', 'bv', 'rel_emb')}
    del _L1_attn_all

    def _L1_ffn_setup():
        import math
        import jax, jax.numpy as jnp
        import numpy as np
        B, S, D, H, E, F = (2, 128, 128, 16, 16, 512)
        HEAD = D // H
        MOE_TOKEN_DROPOUT = 0.2
        EPS = 1e-05

        def layer_norm(x, w, b):
            mu = x.mean(-1, keepdims=True)
            var = ((x - mu) ** 2).mean(-1, keepdims=True)
            return (x - mu) * jax.lax.rsqrt(var + EPS) * w + b
        key = jax.random.key(seed)
        ks = jax.random.split(key, 16)
        w = lambda k, shape: jax.random.normal(k, shape, jnp.float32) * 0.02
        return {'hidden_states': jax.random.normal(ks[0], (B, S, D), jnp.float32), 'ln1_w': jnp.ones((D,), jnp.float32), 'ln1_b': jnp.zeros((D,), jnp.float32), 'q_w': w(ks[1], (D, D)), 'q_b': jnp.zeros((D,), jnp.float32), 'k_w': w(ks[2], (D, D)), 'k_b': jnp.zeros((D,), jnp.float32), 'v_w': w(ks[3], (D, D)), 'v_b': jnp.zeros((D,), jnp.float32), 'o_w': w(ks[4], (D, D)), 'o_b': jnp.zeros((D,), jnp.float32), 'ln2_w': jnp.ones((D,), jnp.float32), 'ln2_b': jnp.zeros((D,), jnp.float32), 'router_w': w(ks[5], (D, E)), 'fc1_w': w(ks[6], (E, D, F)), 'fc1_b': jnp.zeros((E, F), jnp.float32), 'fc2_w': w(ks[7], (E, F, D)), 'fc2_b': jnp.zeros((E, D), jnp.float32)}
    _L1_ffn_all = _L1_ffn_setup()
    _L1_ffn_in = {k: v for k, v in _L1_ffn_all.items() if k in ('ln1_w', 'ln1_b', 'q_w', 'q_b', 'k_w', 'k_b', 'v_w', 'v_b', 'o_w', 'o_b', 'ln2_w', 'ln2_b', 'router_w', 'fc1_w', 'fc1_b', 'fc2_w', 'fc2_b')}
    del _L1_ffn_all

    def _L2_xattn_setup():
        import jax, jax.numpy as jnp
        import numpy as np
        key = jax.random.key(seed)
        ks = jax.random.split(key, 8)
        B, T, S = (32, 128, 128)
        Din, H, C = (128, 128, 128)
        s = 0.02
        return {'x': jax.random.normal(ks[0], (B, T, Din), jnp.float32), 'context': jax.random.normal(ks[1], (B, S, C), jnp.float32), 'W_ih': jax.random.normal(ks[2], (4 * H, Din + H), jnp.float32) * s, 'W_hh': jax.random.normal(ks[3], (4 * H, H), jnp.float32) * s, 'b_ih': jnp.zeros((4 * H,), jnp.float32), 'b_hh': jnp.zeros((4 * H,), jnp.float32), 'Wq': jax.random.normal(ks[4], (C, H), jnp.float32) * s, 'Wout': jax.random.normal(ks[5], (H, C + H), jnp.float32) * s, 'b_out': jnp.zeros((H,), jnp.float32)}
    _L2_xattn_all = _L2_xattn_setup()
    _L2_xattn_in = {k: v for k, v in _L2_xattn_all.items() if k in ('W_ih', 'W_hh', 'b_ih', 'b_hh', 'Wq', 'Wout', 'b_out')}
    del _L2_xattn_all

    def _L2_attn_setup():
        import jax, jax.numpy as jnp
        import numpy as np
        import math
        D_MODEL, D_C, D_R, NH = (128, 128, 32, 16)
        HD = D_MODEL // NH
        B, T = (2, 256)

        def _rope_tables(T, d_R):
            inv_freq = 1.0 / 10000.0 ** (jnp.arange(0, d_R, 2, dtype=jnp.float32) / d_R)
            t = jnp.arange(T, dtype=jnp.float32)
            freqs = jnp.outer(t, inv_freq)
            return (jnp.cos(freqs), jnp.sin(freqs))

        def _rotary_apply(x, cos, sin):
            d = x.shape[-1]
            x1, x2 = (x[..., :d // 2], x[..., d // 2:])
            return jnp.concatenate([x1 * cos - x2 * sin, x2 * cos + x1 * sin], axis=-1)
        key = jax.random.key(seed)
        ks = jax.random.split(key, 8)
        s = lambda fan_in: 1.0 / math.sqrt(fan_in)
        return {'x': jax.random.normal(ks[0], (B, T, D_MODEL), jnp.float32), 'W_kv_down': jax.random.normal(ks[1], (D_MODEL, D_C), jnp.float32) * s(D_MODEL), 'W_k_up': jax.random.normal(ks[2], (D_C, D_MODEL), jnp.float32) * s(D_C), 'W_v_up': jax.random.normal(ks[3], (D_C, D_MODEL), jnp.float32) * s(D_C), 'W_q': jax.random.normal(ks[4], (D_MODEL, D_MODEL), jnp.float32) * s(D_MODEL), 'W_q_rope': jax.random.normal(ks[5], (D_MODEL, D_R), jnp.float32) * s(D_MODEL), 'W_k_rope': jax.random.normal(ks[6], (D_C, D_R), jnp.float32) * s(D_C), 'W_o': jax.random.normal(ks[7], (D_MODEL, D_MODEL), jnp.float32) * s(D_MODEL)}
    _L2_attn_all = _L2_attn_setup()
    _L2_attn_in = {k: v for k, v in _L2_attn_all.items() if k in ('W_kv_down', 'W_k_up', 'W_v_up', 'W_q', 'W_q_rope', 'W_k_rope', 'W_o')}
    del _L2_attn_all

    def _L2_ffn_setup():
        import jax, jax.numpy as jnp
        import numpy as np
        D_MODEL = 128
        N_HEADS = 16
        HEAD_DIM = D_MODEL // N_HEADS
        FFN_DIM = 512
        N_EXPERTS = 8
        CAP_FRAC = 0.25
        MOE_TOKEN_DROPOUT = 0.2
        LN_EPS = 1e-05
        B, S = (4, 64)

        def _layer_norm(x, g, b):
            mu = x.mean(-1, keepdims=True)
            var = ((x - mu) ** 2).mean(-1, keepdims=True)
            return (x - mu) * jax.lax.rsqrt(var + LN_EPS) * g + b

        def _self_attention(x, wq, bq, wk, bk, wv, bv, wo, bo):
            b, s, d = x.shape
            q = ((x @ wq + bq) * HEAD_DIM ** (-0.5)).reshape(b, s, N_HEADS, HEAD_DIM)
            k = (x @ wk + bk).reshape(b, s, N_HEADS, HEAD_DIM)
            v = (x @ wv + bv).reshape(b, s, N_HEADS, HEAD_DIM)
            scores = jnp.einsum('bqhd,bkhd->bhqk', q, k)
            p = jax.nn.softmax(scores, axis=-1)
            o = jnp.einsum('bhqk,bkhd->bqhd', p, v).reshape(b, s, d)
            return o @ wo + bo

        def _moe_ffn(x, wr, w1, b1, w2, b2):
            T, D = x.shape
            C = int(np.ceil(CAP_FRAC * T))
            logits = x @ wr
            probs = jax.nn.softmax(logits, axis=-1)
            top1 = jnp.argmax(probs, axis=-1)
            m1 = jax.nn.one_hot(top1, N_EXPERTS, dtype=x.dtype)
            top2 = jnp.argmax(jnp.where(m1 > 0, -jnp.inf, logits), axis=-1)
            m2 = jax.nn.one_hot(top2, N_EXPERTS, dtype=x.dtype)
            loc1 = jnp.cumsum(m1, axis=0) - 1.0
            loc2 = jnp.cumsum(m2, axis=0) - 1.0 + m1.sum(0, keepdims=True)
            m1 = m1 * (loc1 < C)
            m2 = m2 * (loc2 < C)
            t1 = (probs * m1).sum(-1)
            t2 = (probs * m2).sum(-1)
            denom = jnp.maximum(t1 + t2, jnp.finfo(x.dtype).eps)
            t1, t2 = (t1 / denom, t2 / denom)
            tok = jnp.arange(T)
            s1 = loc1[tok, top1].astype(jnp.int32)
            s2 = loc2[tok, top2].astype(jnp.int32)
            v1 = m1[tok, top1] > 0
            v2 = m2[tok, top2] > 0
            s1 = jnp.where(v1, s1, C)
            s2 = jnp.where(v2, s2, C)
            buf = jnp.zeros((N_EXPERTS, C, D), x.dtype)
            buf = buf.at[top1, s1].set(x, mode='drop')
            buf = buf.at[top2, s2].set(x, mode='drop')
            h = jax.nn.relu(jnp.einsum('ecd,edf->ecf', buf, w1) + b1[:, None, :])
            y = (jnp.einsum('ecf,efd->ecd', h, w2) + b2[:, None, :]) * (1.0 - MOE_TOKEN_DROPOUT)
            y1 = y[top1, jnp.minimum(s1, C - 1)]
            y2 = y[top2, jnp.minimum(s2, C - 1)]
            g1 = t1 * v1
            g2 = t2 * v2
            return g1[:, None] * y1 + g2[:, None] * y2
        key = jax.random.key(seed)
        ks = jax.random.split(key, 20)

        def w(k, shape, scale=0.02):
            return jax.random.normal(k, shape, jnp.float32) * scale
        return {'x': jax.random.normal(ks[0], (B, S, D_MODEL), jnp.float32), 'wq': w(ks[1], (D_MODEL, D_MODEL)), 'bq': w(ks[2], (D_MODEL,)), 'wk': w(ks[3], (D_MODEL, D_MODEL)), 'bk': w(ks[4], (D_MODEL,)), 'wv': w(ks[5], (D_MODEL, D_MODEL)), 'bv': w(ks[6], (D_MODEL,)), 'wo': w(ks[7], (D_MODEL, D_MODEL)), 'bo': w(ks[8], (D_MODEL,)), 'ln1_g': 1.0 + w(ks[9], (D_MODEL,)), 'ln1_b': w(ks[10], (D_MODEL,)), 'ln2_g': 1.0 + w(ks[11], (D_MODEL,)), 'ln2_b': w(ks[12], (D_MODEL,)), 'wr': w(ks[13], (D_MODEL, N_EXPERTS)), 'w1': w(ks[14], (N_EXPERTS, D_MODEL, FFN_DIM)), 'b1': w(ks[15], (N_EXPERTS, FFN_DIM)), 'w2': w(ks[16], (N_EXPERTS, FFN_DIM, D_MODEL)), 'b2': w(ks[17], (N_EXPERTS, D_MODEL))}
    _L2_ffn_all = _L2_ffn_setup()
    _L2_ffn_in = {k: v for k, v in _L2_ffn_all.items() if k in ('wq', 'bq', 'wk', 'bk', 'wv', 'bv', 'wo', 'bo', 'ln1_g', 'ln1_b', 'ln2_g', 'ln2_b', 'wr', 'w1', 'b1', 'w2', 'b2')}
    del _L2_ffn_all

    def _L3_xattn_setup():
        import jax, jax.numpy as jnp
        import numpy as np
        B, S, D = (8, 256, 128)
        key = jax.random.key(seed)
        ks = jax.random.split(key, 9)
        scale = 1.0 / np.sqrt(D)
        inp = {'query': jax.random.normal(ks[0], (B, S, D), dtype=jnp.float32), 'key': jax.random.normal(ks[1], (B, S, D), dtype=jnp.float32), 'value': jax.random.normal(ks[2], (B, S, D), dtype=jnp.float32), 'mask': jnp.tril(jnp.ones((S, S), dtype=bool)), 'Wq': jax.random.normal(ks[3], (D, D), dtype=jnp.float32) * scale, 'bq': jax.random.normal(ks[4], (D,), dtype=jnp.float32) * 0.02, 'Wk': jax.random.normal(ks[5], (D, D), dtype=jnp.float32) * scale, 'bk': jax.random.normal(ks[6], (D,), dtype=jnp.float32) * 0.02, 'Wv': jax.random.normal(ks[7], (D, D), dtype=jnp.float32) * scale, 'bv': jax.random.normal(ks[8], (D,), dtype=jnp.float32) * 0.02}
        return inp
    _L3_xattn_all = _L3_xattn_setup()
    _L3_xattn_in = {k: v for k, v in _L3_xattn_all.items() if k in ('Wq', 'bq', 'Wk', 'bk', 'Wv', 'bv')}
    del _L3_xattn_all

    def _L3_attn_setup():
        import jax, jax.numpy as jnp
        import numpy as np
        D_MODEL = 128
        NUM_HEADS = 16
        HEAD_DIM = D_MODEL // NUM_HEADS
        THETA = 10000.0

        def apply_rope(x, positions):
            d = x.shape[-1]
            inv_freq = THETA ** (-jnp.arange(0, d, 2, dtype=jnp.float32) / d)
            angles = positions[:, None].astype(jnp.float32) * inv_freq[None, :]
            cos = jnp.cos(angles)
            sin = jnp.sin(angles)
            x1 = x[..., 0::2]
            x2 = x[..., 1::2]
            r1 = x1 * cos - x2 * sin
            r2 = x1 * sin + x2 * cos
            return jnp.stack([r1, r2], axis=-1).reshape(x.shape)
        key = jax.random.key(seed)
        ks = jax.random.split(key, 5)
        B, S = (2, 256)
        scale = 1.0 / np.sqrt(D_MODEL)
        return {'x': jax.random.normal(ks[0], (B, S, D_MODEL), dtype=jnp.float32), 'Wq': jax.random.normal(ks[1], (D_MODEL, D_MODEL), dtype=jnp.float32) * scale, 'Wk': jax.random.normal(ks[2], (D_MODEL, D_MODEL), dtype=jnp.float32) * scale, 'Wv': jax.random.normal(ks[3], (D_MODEL, D_MODEL), dtype=jnp.float32) * scale, 'Wo': jax.random.normal(ks[4], (D_MODEL, D_MODEL), dtype=jnp.float32) * scale}
    _L3_attn_all = _L3_attn_setup()
    _L3_attn_in = {k: v for k, v in _L3_attn_all.items() if k in ('Wq', 'Wk', 'Wv', 'Wo')}
    del _L3_attn_all

    def _L3_ffn_setup():
        import jax, jax.numpy as jnp
        import numpy as np
        B, T, D, H, E = (4, 256, 128, 256, 8)
        TOP_K = int(E * 0.25)
        key = jax.random.key(seed)
        ks = jax.random.split(key, 6)
        x = jax.random.normal(ks[0], (B, T, D), dtype=jnp.float32)
        gate = jax.random.normal(ks[1], (D, E), dtype=jnp.float32)
        W1 = jax.random.normal(ks[2], (E, D, H), dtype=jnp.float32) * D ** (-0.5)
        b1 = jnp.zeros((E, H), dtype=jnp.float32)
        W2 = jax.random.normal(ks[3], (E, H, D), dtype=jnp.float32) * H ** (-0.5)
        b2 = jnp.zeros((E, D), dtype=jnp.float32)
        return {'x': x, 'gate': gate, 'W1': W1, 'b1': b1, 'W2': W2, 'b2': b2}
    _L3_ffn_all = _L3_ffn_setup()
    _L3_ffn_in = {k: v for k, v in _L3_ffn_all.items() if k in ('gate', 'W1', 'b1', 'W2', 'b2')}
    del _L3_ffn_all
    return {'x': x, 'ctx_1024': ctx_1024, 'mask_SxS2_bk0': mask_SxS2_bk0, 'L0_xattn_Wq_w': _L0_xattn_in['Wq_w'], 'L0_xattn_Wq_b': _L0_xattn_in['Wq_b'], 'L0_xattn_Wkv_w': _L0_xattn_in['Wkv_w'], 'L0_xattn_Wkv_b': _L0_xattn_in['Wkv_b'], 'L0_xattn_Wo_w': _L0_xattn_in['Wo_w'], 'L0_xattn_Wo_b': _L0_xattn_in['Wo_b'], 'L0_attn_qkv_w': _L0_attn_in['qkv_w'], 'L0_attn_qkv_b': _L0_attn_in['qkv_b'], 'L0_attn_out_w': _L0_attn_in['out_w'], 'L0_attn_out_b': _L0_attn_in['out_b'], 'L0_ffn_rhs': _L0_ffn_in['rhs'], 'L1_xattn_Wq': _L1_xattn_in['Wq'], 'L1_xattn_Wkv': _L1_xattn_in['Wkv'], 'L1_attn_Wqk': _L1_attn_in['Wqk'], 'L1_attn_bqk': _L1_attn_in['bqk'], 'L1_attn_gamma': _L1_attn_in['gamma'], 'L1_attn_beta': _L1_attn_in['beta'], 'L1_attn_Wv': _L1_attn_in['Wv'], 'L1_attn_bv': _L1_attn_in['bv'], 'L1_attn_rel_emb': _L1_attn_in['rel_emb'], 'L1_ffn_ln1_w': _L1_ffn_in['ln1_w'], 'L1_ffn_ln1_b': _L1_ffn_in['ln1_b'], 'L1_ffn_q_w': _L1_ffn_in['q_w'], 'L1_ffn_q_b': _L1_ffn_in['q_b'], 'L1_ffn_k_w': _L1_ffn_in['k_w'], 'L1_ffn_k_b': _L1_ffn_in['k_b'], 'L1_ffn_v_w': _L1_ffn_in['v_w'], 'L1_ffn_v_b': _L1_ffn_in['v_b'], 'L1_ffn_o_w': _L1_ffn_in['o_w'], 'L1_ffn_o_b': _L1_ffn_in['o_b'], 'L1_ffn_ln2_w': _L1_ffn_in['ln2_w'], 'L1_ffn_ln2_b': _L1_ffn_in['ln2_b'], 'L1_ffn_router_w': _L1_ffn_in['router_w'], 'L1_ffn_fc1_w': _L1_ffn_in['fc1_w'], 'L1_ffn_fc1_b': _L1_ffn_in['fc1_b'], 'L1_ffn_fc2_w': _L1_ffn_in['fc2_w'], 'L1_ffn_fc2_b': _L1_ffn_in['fc2_b'], 'L2_xattn_W_ih': _L2_xattn_in['W_ih'], 'L2_xattn_W_hh': _L2_xattn_in['W_hh'], 'L2_xattn_b_ih': _L2_xattn_in['b_ih'], 'L2_xattn_b_hh': _L2_xattn_in['b_hh'], 'L2_xattn_Wq': _L2_xattn_in['Wq'], 'L2_xattn_Wout': _L2_xattn_in['Wout'], 'L2_xattn_b_out': _L2_xattn_in['b_out'], 'L2_attn_W_kv_down': _L2_attn_in['W_kv_down'], 'L2_attn_W_k_up': _L2_attn_in['W_k_up'], 'L2_attn_W_v_up': _L2_attn_in['W_v_up'], 'L2_attn_W_q': _L2_attn_in['W_q'], 'L2_attn_W_q_rope': _L2_attn_in['W_q_rope'], 'L2_attn_W_k_rope': _L2_attn_in['W_k_rope'], 'L2_attn_W_o': _L2_attn_in['W_o'], 'L2_ffn_wq': _L2_ffn_in['wq'], 'L2_ffn_bq': _L2_ffn_in['bq'], 'L2_ffn_wk': _L2_ffn_in['wk'], 'L2_ffn_bk': _L2_ffn_in['bk'], 'L2_ffn_wv': _L2_ffn_in['wv'], 'L2_ffn_bv': _L2_ffn_in['bv'], 'L2_ffn_wo': _L2_ffn_in['wo'], 'L2_ffn_bo': _L2_ffn_in['bo'], 'L2_ffn_ln1_g': _L2_ffn_in['ln1_g'], 'L2_ffn_ln1_b': _L2_ffn_in['ln1_b'], 'L2_ffn_ln2_g': _L2_ffn_in['ln2_g'], 'L2_ffn_ln2_b': _L2_ffn_in['ln2_b'], 'L2_ffn_wr': _L2_ffn_in['wr'], 'L2_ffn_w1': _L2_ffn_in['w1'], 'L2_ffn_b1': _L2_ffn_in['b1'], 'L2_ffn_w2': _L2_ffn_in['w2'], 'L2_ffn_b2': _L2_ffn_in['b2'], 'L3_xattn_Wq': _L3_xattn_in['Wq'], 'L3_xattn_bq': _L3_xattn_in['bq'], 'L3_xattn_Wk': _L3_xattn_in['Wk'], 'L3_xattn_bk': _L3_xattn_in['bk'], 'L3_xattn_Wv': _L3_xattn_in['Wv'], 'L3_xattn_bv': _L3_xattn_in['bv'], 'L3_attn_Wq': _L3_attn_in['Wq'], 'L3_attn_Wk': _L3_attn_in['Wk'], 'L3_attn_Wv': _L3_attn_in['Wv'], 'L3_attn_Wo': _L3_attn_in['Wo'], 'L3_ffn_gate': _L3_ffn_in['gate'], 'L3_ffn_W1': _L3_ffn_in['W1'], 'L3_ffn_b1': _L3_ffn_in['b1'], 'L3_ffn_W2': _L3_ffn_in['W2'], 'L3_ffn_b2': _L3_ffn_in['b2']}

def reference(x, ctx_1024, mask_SxS2_bk0, L0_xattn_Wq_w, L0_xattn_Wq_b, L0_xattn_Wkv_w, L0_xattn_Wkv_b, L0_xattn_Wo_w, L0_xattn_Wo_b, L0_attn_qkv_w, L0_attn_qkv_b, L0_attn_out_w, L0_attn_out_b, L0_ffn_rhs, L1_xattn_Wq, L1_xattn_Wkv, L1_attn_Wqk, L1_attn_bqk, L1_attn_gamma, L1_attn_beta, L1_attn_Wv, L1_attn_bv, L1_attn_rel_emb, L1_ffn_ln1_w, L1_ffn_ln1_b, L1_ffn_q_w, L1_ffn_q_b, L1_ffn_k_w, L1_ffn_k_b, L1_ffn_v_w, L1_ffn_v_b, L1_ffn_o_w, L1_ffn_o_b, L1_ffn_ln2_w, L1_ffn_ln2_b, L1_ffn_router_w, L1_ffn_fc1_w, L1_ffn_fc1_b, L1_ffn_fc2_w, L1_ffn_fc2_b, L2_xattn_W_ih, L2_xattn_W_hh, L2_xattn_b_ih, L2_xattn_b_hh, L2_xattn_Wq, L2_xattn_Wout, L2_xattn_b_out, L2_attn_W_kv_down, L2_attn_W_k_up, L2_attn_W_v_up, L2_attn_W_q, L2_attn_W_q_rope, L2_attn_W_k_rope, L2_attn_W_o, L2_ffn_wq, L2_ffn_bq, L2_ffn_wk, L2_ffn_bk, L2_ffn_wv, L2_ffn_bv, L2_ffn_wo, L2_ffn_bo, L2_ffn_ln1_g, L2_ffn_ln1_b, L2_ffn_ln2_g, L2_ffn_ln2_b, L2_ffn_wr, L2_ffn_w1, L2_ffn_b1, L2_ffn_w2, L2_ffn_b2, L3_xattn_Wq, L3_xattn_bq, L3_xattn_Wk, L3_xattn_bk, L3_xattn_Wv, L3_xattn_bv, L3_attn_Wq, L3_attn_Wk, L3_attn_Wv, L3_attn_Wo, L3_ffn_gate, L3_ffn_W1, L3_ffn_b1, L3_ffn_W2, L3_ffn_b2):
    import jax
    import jax.numpy as jnp

    def _L0_xattn_ref(Q, K, V, Wq_w, Wq_b, Wkv_w, Wkv_b, Wo_w, Wo_b):
        import jax, jax.numpy as jnp
        import numpy as np
        B, S, D, G = (4, 256, 128, 8)
        DK = D // G
        b, s, d = Q.shape
        g = Wkv_w.shape[0]
        dk = d // g
        q = (Q @ Wq_w + Wq_b).reshape(b, s, g, dk).transpose(0, 2, 1, 3)
        kv = jnp.einsum('bsd,gde->bgse', K, Wkv_w) + Wkv_b[None, :, None, :]
        k, v = (kv[..., :dk], kv[..., dk:])
        scale = jnp.float32(1.0) / jnp.sqrt(jnp.float32(dk))
        scores = jnp.einsum('bgqd,bgkd->bgqk', q, k) * scale
        attn = jax.nn.softmax(scores, axis=-1)
        ctx = jnp.einsum('bgqk,bgkd->bgqd', attn, v)
        combined = ctx.transpose(0, 2, 1, 3).reshape(b, s, d)
        return combined @ Wo_w + Wo_b

    def _L0_attn_ref(x, qkv_w, qkv_b, out_w, out_b):
        import jax, jax.numpy as jnp
        import numpy as np
        B, S, D, H = (2, 256, 128, 16)
        HD = D // H
        b, s, d = x.shape
        h, hd = (H, d // H)
        scale = 1.0 / np.sqrt(hd).astype(np.float32)
        qkv = (x @ qkv_w + qkv_b).reshape(b, s, 3, h, hd)
        q, k, v = (qkv[:, :, 0], qkv[:, :, 1], qkv[:, :, 2])
        logits = jnp.einsum('bqhd,bkhd->bhqk', q, k)
        causal_mask = jnp.triu(jnp.ones((s, s), bool), 1)
        logits = jnp.where(causal_mask, -jnp.inf, logits) * scale
        att = jax.nn.softmax(logits, axis=-1)
        out = jnp.einsum('bhqk,bkhd->bqhd', att, v).reshape(b, s, d)
        return out @ out_w + out_b

    def _L0_ffn_ref(lhs, rhs):
        import jax, jax.numpy as jnp
        import numpy as np
        INT8_MAX = 127.0

        def _absmax_scale(x, axes):
            amax = jnp.max(jnp.abs(x), axis=axes, keepdims=True)
            return jnp.maximum(amax, 1e-12) / INT8_MAX
        lhs_scale = _absmax_scale(lhs, (2,))
        rhs_scale = _absmax_scale(rhs, (0,))
        q_lhs = jnp.clip(jnp.round(lhs / lhs_scale), -INT8_MAX, INT8_MAX).astype(jnp.int8)
        q_rhs = jnp.clip(jnp.round(rhs / rhs_scale), -INT8_MAX, INT8_MAX).astype(jnp.int8)
        acc = jax.lax.dot_general(q_lhs, q_rhs, (((2,), (0,)), ((), ())), preferred_element_type=jnp.int32)
        return acc.astype(jnp.float32) * lhs_scale * rhs_scale

    def _L1_xattn_ref(x, context, Wq, Wkv):
        import jax, jax.numpy as jnp
        import numpy as np
        DIM = 128
        QK_DIM = 128
        V_DIM = 128
        HEADS = 16
        b, n, _ = x.shape
        j = context.shape[1]
        h = HEADS
        dqk = QK_DIM // h
        dv = V_DIM // h
        q = x @ Wq
        kv = context @ Wkv
        k, v = (kv[..., :QK_DIM], kv[..., QK_DIM:])
        q = q.reshape(b, n, h, dqk).transpose(0, 2, 1, 3)
        k = k.reshape(b, j, h, dqk).transpose(0, 2, 1, 3)
        v = v.reshape(b, j, h, dv).transpose(0, 2, 1, 3)
        scale = dqk ** (-0.5)
        scores = jnp.einsum('bhid,bhjd->bhij', q * scale, k)
        weights = jax.nn.softmax(scores, axis=-1)
        attn = jnp.einsum('bhij,bhjd->bhid', weights, v)
        out = attn.transpose(0, 2, 1, 3).reshape(b, n, h * dv)
        return out

    def _L1_attn_ref(x, Wqk, bqk, gamma, beta, Wv, bv, rel_emb):
        import math
        import jax, jax.numpy as jnp
        import numpy as np
        DIM = 128
        DIM_QK = 128
        DIM_V = 128
        NUM_BUCKETS = 32
        MAX_DISTANCE = 128

        def _rel_pos_bucket_causal(seq_len):
            q = np.arange(seq_len)
            n = np.maximum(q[:, None] - q[None, :], 0)
            max_exact = NUM_BUCKETS // 2
            is_small = n < max_exact
            nf = np.maximum(n, 1).astype(np.float32)
            val_if_large = max_exact + (np.log(nf / max_exact) / math.log(MAX_DISTANCE / max_exact) * (NUM_BUCKETS - max_exact)).astype(np.int32)
            val_if_large = np.minimum(val_if_large, NUM_BUCKETS - 1)
            return jnp.asarray(np.where(is_small, n, val_if_large), dtype=jnp.int32)

        def laplacian_attn_fn(x):
            mu = math.sqrt(0.5)
            std = math.sqrt(0.25 * math.pi)
            return (1.0 + jax.lax.erf((x - mu) / (std * math.sqrt(2.0)))) * 0.5
        B, S, _ = x.shape
        qk = jax.nn.swish(jnp.einsum('bsd,de->bse', x, Wqk) + bqk)
        q = qk * gamma[0] + beta[0]
        k = qk * gamma[1] + beta[1]
        v = jax.nn.swish(jnp.einsum('bsd,de->bse', x, Wv) + bv)
        scale = 1.0 / S
        sim = jnp.einsum('bid,bjd->bij', q, k) * scale
        buckets = _rel_pos_bucket_causal(S)
        bias = rel_emb[buckets, 0] * DIM_QK ** 0.5
        sim = sim + bias
        attn = laplacian_attn_fn(sim)
        i = jnp.arange(S)
        future = i[None, :] > i[:, None]
        attn = jnp.where(future, 0.0, attn)
        return jnp.einsum('bij,bjd->bid', attn, v)

    def _L1_ffn_ref(hidden_states, ln1_w, ln1_b, q_w, q_b, k_w, k_b, v_w, v_b, o_w, o_b, ln2_w, ln2_b, router_w, fc1_w, fc1_b, fc2_w, fc2_b):
        import math
        import jax, jax.numpy as jnp
        import numpy as np
        B, S, D, H, E, F = (2, 128, 128, 16, 16, 512)
        HEAD = D // H
        MOE_TOKEN_DROPOUT = 0.2
        EPS = 1e-05

        def layer_norm(x, w, b):
            mu = x.mean(-1, keepdims=True)
            var = ((x - mu) ** 2).mean(-1, keepdims=True)
            return (x - mu) * jax.lax.rsqrt(var + EPS) * w + b
        b, s, _ = hidden_states.shape
        T = b * s
        neg = jnp.finfo(jnp.float32).min
        resid = hidden_states
        x = layer_norm(hidden_states, ln1_w, ln1_b)
        q = (x @ q_w + q_b) / math.sqrt(HEAD)
        k = x @ k_w + k_b
        v = x @ v_w + v_b
        split = lambda t: t.reshape(b, s, H, HEAD).transpose(0, 2, 1, 3)
        q, k, v = (split(q), split(k), split(v))
        scores = jnp.einsum('bhqd,bhkd->bhqk', q, k)
        causal = jnp.tril(jnp.ones((s, s), bool))
        scores = jnp.where(causal, scores, neg)
        attn = jax.nn.softmax(scores, axis=-1)
        ctx = jnp.einsum('bhqk,bhkd->bhqd', attn, v)
        ctx = ctx.transpose(0, 2, 1, 3).reshape(b, s, D)
        hidden = resid + (ctx @ o_w + o_b)
        resid = hidden
        xt = layer_norm(hidden, ln2_w, ln2_b).reshape(T, D)
        logits = xt @ router_w
        probs = jax.nn.softmax(logits, axis=-1)
        top1 = jnp.argmax(probs, axis=-1)
        m1 = jax.nn.one_hot(top1, E, dtype=jnp.float32)
        logits_no1 = jnp.where(m1 > 0, -jnp.inf, logits)
        top2 = jnp.argmax(logits_no1, axis=-1)
        m2 = jax.nn.one_hot(top2, E, dtype=jnp.float32)
        loc1 = jnp.cumsum(m1, axis=0) - 1.0
        loc2 = jnp.cumsum(m2, axis=0) - 1.0 + m1.sum(axis=0, keepdims=True)
        C = 2 * math.ceil(T / E)
        m1 = m1 * (loc1 < C)
        m2 = m2 * (loc2 < C)
        g1 = (probs * m1).sum(-1)
        g2 = (probs * m2).sum(-1)
        denom = jnp.maximum(g1 + g2, jnp.finfo(jnp.float32).eps)
        g1, g2 = (g1 / denom, g2 / denom)
        slot1 = (loc1 * m1).sum(-1).astype(jnp.int32)
        slot2 = (loc2 * m2).sum(-1).astype(jnp.int32)
        d1 = m1[:, :, None] * jax.nn.one_hot(slot1, C, dtype=jnp.float32)[:, None, :]
        d2 = m2[:, :, None] * jax.nn.one_hot(slot2, C, dtype=jnp.float32)[:, None, :]
        dispatch = d1 + d2
        combine = g1[:, None, None] * d1 + g2[:, None, None] * d2
        xin = jnp.einsum('tec,td->ecd', dispatch, xt)
        h = jnp.einsum('ecd,edf->ecf', xin, fc1_w) + fc1_b[:, None, :]
        h = jax.nn.gelu(h, approximate=False)
        eout = jnp.einsum('ecf,efd->ecd', h, fc2_w) + fc2_b[:, None, :]
        eout = eout * (1.0 - MOE_TOKEN_DROPOUT)
        moe_out = jnp.einsum('tec,ecd->td', combine, eout).reshape(b, s, D)
        return resid + moe_out

    def _L2_xattn_ref(x, context, W_ih, W_hh, b_ih, b_hh, Wq, Wout, b_out):
        import jax, jax.numpy as jnp
        import numpy as np
        B, T, Din = x.shape
        H = W_hh.shape[1]

        def attend(h):
            q = h @ Wq.T
            scores = jnp.einsum('bc,bsc->bs', q, context)
            alpha = jax.nn.softmax(scores, axis=-1)
            ctx = jnp.einsum('bs,bsc->bc', alpha, context)
            return jnp.tanh(jnp.concatenate([ctx, h], axis=-1) @ Wout.T + b_out)

        def step(carry, x_t):
            h, c, attn = carry
            inp = jnp.concatenate([x_t, attn], axis=-1)
            gates = inp @ W_ih.T + b_ih + h @ W_hh.T + b_hh
            i, f, g, o = jnp.split(gates, 4, axis=-1)
            c = jax.nn.sigmoid(f) * c + jax.nn.sigmoid(i) * jnp.tanh(g)
            h = jax.nn.sigmoid(o) * jnp.tanh(c)
            out = attn_out = attend(h)
            return ((h, c, attn_out), out)
        h0 = jnp.zeros((B, H), x.dtype)
        init = (h0, h0, h0)
        xs = jnp.swapaxes(x, 0, 1)
        _, outs = jax.lax.scan(step, init, xs)
        return jnp.swapaxes(outs, 0, 1)

    def _L2_attn_ref(x, W_kv_down, W_k_up, W_v_up, W_q, W_q_rope, W_k_rope, W_o):
        import jax, jax.numpy as jnp
        import numpy as np
        import math
        D_MODEL, D_C, D_R, NH = (128, 128, 32, 16)
        HD = D_MODEL // NH
        B, T = (2, 256)

        def _rope_tables(T, d_R):
            inv_freq = 1.0 / 10000.0 ** (jnp.arange(0, d_R, 2, dtype=jnp.float32) / d_R)
            t = jnp.arange(T, dtype=jnp.float32)
            freqs = jnp.outer(t, inv_freq)
            return (jnp.cos(freqs), jnp.sin(freqs))

        def _rotary_apply(x, cos, sin):
            d = x.shape[-1]
            x1, x2 = (x[..., :d // 2], x[..., d // 2:])
            return jnp.concatenate([x1 * cos - x2 * sin, x2 * cos + x1 * sin], axis=-1)
        Bb, Tt, _ = x.shape
        cos, sin = _rope_tables(Tt, D_R)
        cos = cos[None]
        sin = sin[None]
        c_kv = x @ W_kv_down
        k_rope = _rotary_apply(c_kv @ W_k_rope, cos, sin)
        k = (c_kv @ W_k_up).reshape(Bb, Tt, NH, HD)
        v = (c_kv @ W_v_up).reshape(Bb, Tt, NH, HD)
        q = (x @ W_q).reshape(Bb, Tt, NH, HD)
        q_rope = _rotary_apply(x @ W_q_rope, cos, sin)
        scale = math.sqrt(HD + D_R)
        scores = jnp.einsum('bqhd,bkhd->bhqk', q, k)
        scores = scores + jnp.einsum('bqr,bkr->bqk', q_rope, k_rope)[:, None]
        scores = scores / scale
        causal = jnp.triu(jnp.ones((Tt, Tt), dtype=bool), k=1)
        scores = jnp.where(causal[None, None], -jnp.inf, scores)
        w = jax.nn.softmax(scores, axis=-1)
        attn = jnp.einsum('bhqk,bkhd->bqhd', w, v).reshape(Bb, Tt, D_MODEL)
        return attn @ W_o

    def _L2_ffn_ref(x, wq, bq, wk, bk, wv, bv, wo, bo, ln1_g, ln1_b, ln2_g, ln2_b, wr, w1, b1, w2, b2):
        import jax, jax.numpy as jnp
        import numpy as np
        D_MODEL = 128
        N_HEADS = 16
        HEAD_DIM = D_MODEL // N_HEADS
        FFN_DIM = 512
        N_EXPERTS = 8
        CAP_FRAC = 0.25
        MOE_TOKEN_DROPOUT = 0.2
        LN_EPS = 1e-05
        B, S = (4, 64)

        def _layer_norm(x, g, b):
            mu = x.mean(-1, keepdims=True)
            var = ((x - mu) ** 2).mean(-1, keepdims=True)
            return (x - mu) * jax.lax.rsqrt(var + LN_EPS) * g + b

        def _self_attention(x, wq, bq, wk, bk, wv, bv, wo, bo):
            b, s, d = x.shape
            q = ((x @ wq + bq) * HEAD_DIM ** (-0.5)).reshape(b, s, N_HEADS, HEAD_DIM)
            k = (x @ wk + bk).reshape(b, s, N_HEADS, HEAD_DIM)
            v = (x @ wv + bv).reshape(b, s, N_HEADS, HEAD_DIM)
            scores = jnp.einsum('bqhd,bkhd->bhqk', q, k)
            p = jax.nn.softmax(scores, axis=-1)
            o = jnp.einsum('bhqk,bkhd->bqhd', p, v).reshape(b, s, d)
            return o @ wo + bo

        def _moe_ffn(x, wr, w1, b1, w2, b2):
            T, D = x.shape
            C = int(np.ceil(CAP_FRAC * T))
            logits = x @ wr
            probs = jax.nn.softmax(logits, axis=-1)
            top1 = jnp.argmax(probs, axis=-1)
            m1 = jax.nn.one_hot(top1, N_EXPERTS, dtype=x.dtype)
            top2 = jnp.argmax(jnp.where(m1 > 0, -jnp.inf, logits), axis=-1)
            m2 = jax.nn.one_hot(top2, N_EXPERTS, dtype=x.dtype)
            loc1 = jnp.cumsum(m1, axis=0) - 1.0
            loc2 = jnp.cumsum(m2, axis=0) - 1.0 + m1.sum(0, keepdims=True)
            m1 = m1 * (loc1 < C)
            m2 = m2 * (loc2 < C)
            t1 = (probs * m1).sum(-1)
            t2 = (probs * m2).sum(-1)
            denom = jnp.maximum(t1 + t2, jnp.finfo(x.dtype).eps)
            t1, t2 = (t1 / denom, t2 / denom)
            tok = jnp.arange(T)
            s1 = loc1[tok, top1].astype(jnp.int32)
            s2 = loc2[tok, top2].astype(jnp.int32)
            v1 = m1[tok, top1] > 0
            v2 = m2[tok, top2] > 0
            s1 = jnp.where(v1, s1, C)
            s2 = jnp.where(v2, s2, C)
            buf = jnp.zeros((N_EXPERTS, C, D), x.dtype)
            buf = buf.at[top1, s1].set(x, mode='drop')
            buf = buf.at[top2, s2].set(x, mode='drop')
            h = jax.nn.relu(jnp.einsum('ecd,edf->ecf', buf, w1) + b1[:, None, :])
            y = (jnp.einsum('ecf,efd->ecd', h, w2) + b2[:, None, :]) * (1.0 - MOE_TOKEN_DROPOUT)
            y1 = y[top1, jnp.minimum(s1, C - 1)]
            y2 = y[top2, jnp.minimum(s2, C - 1)]
            g1 = t1 * v1
            g2 = t2 * v2
            return g1[:, None] * y1 + g2[:, None] * y2
        h = _layer_norm(x, ln1_g, ln1_b)
        h = _self_attention(h, wq, bq, wk, bk, wv, bv, wo, bo)
        x = x + h
        h = _layer_norm(x, ln2_g, ln2_b)
        b, s, d = h.shape
        moe = _moe_ffn(h.reshape(b * s, d), wr, w1, b1, w2, b2).reshape(b, s, d)
        return x + moe

    def _L3_xattn_ref(query, key, value, mask, Wq, bq, Wk, bk, Wv, bv):
        import jax, jax.numpy as jnp
        import numpy as np
        B, S, D = (8, 256, 128)
        dk = Wq.shape[1]
        q = jnp.einsum('bsd,de->bse', query, Wq) + bq
        k = jnp.einsum('bsd,de->bse', key, Wk) + bk
        v = jnp.einsum('bsd,de->bse', value, Wv) + bv
        scores = jnp.einsum('bqd,bkd->bqk', q, k) / jnp.sqrt(jnp.asarray(dk, q.dtype))
        scores = jnp.where(mask, scores, jnp.asarray(-jnp.inf, scores.dtype))
        attn = jax.nn.softmax(scores, axis=-1)
        return jnp.einsum('bqk,bkd->bqd', attn, v)

    def _L3_attn_ref(x, Wq, Wk, Wv, Wo):
        import jax, jax.numpy as jnp
        import numpy as np
        D_MODEL = 128
        NUM_HEADS = 16
        HEAD_DIM = D_MODEL // NUM_HEADS
        THETA = 10000.0

        def apply_rope(x, positions):
            d = x.shape[-1]
            inv_freq = THETA ** (-jnp.arange(0, d, 2, dtype=jnp.float32) / d)
            angles = positions[:, None].astype(jnp.float32) * inv_freq[None, :]
            cos = jnp.cos(angles)
            sin = jnp.sin(angles)
            x1 = x[..., 0::2]
            x2 = x[..., 1::2]
            r1 = x1 * cos - x2 * sin
            r2 = x1 * sin + x2 * cos
            return jnp.stack([r1, r2], axis=-1).reshape(x.shape)
        B, S, _ = x.shape
        q = jnp.einsum('bsd,ed->bse', x, Wq)
        k = jnp.einsum('bsd,ed->bse', x, Wk)
        v = jnp.einsum('bsd,ed->bse', x, Wv)
        q = q.reshape(B, S, NUM_HEADS, HEAD_DIM).transpose(0, 2, 1, 3)
        k = k.reshape(B, S, NUM_HEADS, HEAD_DIM).transpose(0, 2, 1, 3)
        v = v.reshape(B, S, NUM_HEADS, HEAD_DIM).transpose(0, 2, 1, 3)
        positions = jnp.arange(S)
        q = apply_rope(q, positions)
        k = apply_rope(k, positions)
        scale = 1.0 / jnp.sqrt(jnp.asarray(HEAD_DIM, dtype=x.dtype))
        scores = jnp.einsum('bhqd,bhkd->bhqk', q, k) * scale
        causal = jnp.tril(jnp.ones((S, S), dtype=bool))
        scores = jnp.where(causal, scores, -jnp.inf)
        att = jax.nn.softmax(scores, axis=-1)
        out = jnp.einsum('bhqk,bhkd->bhqd', att, v)
        out = out.transpose(0, 2, 1, 3).reshape(B, S, D_MODEL)
        return jnp.einsum('bsd,ed->bse', out, Wo)

    def _L3_ffn_ref(x, gate, W1, b1, W2, b2):
        import jax, jax.numpy as jnp
        import numpy as np
        B, T, D, H, E = (4, 256, 128, 256, 8)
        TOP_K = int(E * 0.25)
        raw_gate = jax.nn.softmax(jnp.einsum('btd,de->bte', x, gate), axis=-1)
        topk_scores, topk_idx = jax.lax.top_k(raw_gate, TOP_K)
        mask = jax.nn.one_hot(topk_idx, E, dtype=raw_gate.dtype).sum(axis=-2)
        gate_topk = mask * raw_gate
        gate_topk = gate_topk / jnp.maximum(gate_topk.sum(axis=-1, keepdims=True), 1e-12)
        h = jax.nn.relu(jnp.einsum('btd,edh->beth', x, W1) + b1[None, :, None, :])
        expert_out = jnp.einsum('beth,ehd->betd', h, W2) + b2[None, :, None, :]
        out = jnp.einsum('bte,betd->btd', gate_topk, expert_out)
        return out
    x = x + _L0_xattn_ref(_layernorm(x, axis=-1), ctx_1024, ctx_1024, L0_xattn_Wq_w, L0_xattn_Wq_b, L0_xattn_Wkv_w, L0_xattn_Wkv_b, L0_xattn_Wo_w, L0_xattn_Wo_b)
    x = x + _L0_attn_ref(_layernorm(x, axis=-1), L0_attn_qkv_w, L0_attn_qkv_b, L0_attn_out_w, L0_attn_out_b)
    x = x + _L0_ffn_ref(_layernorm(x, axis=-1), L0_ffn_rhs)
    x = x + _L1_xattn_ref(_layernorm(x, axis=-1), ctx_1024, L1_xattn_Wq, L1_xattn_Wkv)
    x = x + _L1_attn_ref(_layernorm(x, axis=-1), L1_attn_Wqk, L1_attn_bqk, L1_attn_gamma, L1_attn_beta, L1_attn_Wv, L1_attn_bv, L1_attn_rel_emb)
    x = x + _L1_ffn_ref(_layernorm(x, axis=-1), L1_ffn_ln1_w, L1_ffn_ln1_b, L1_ffn_q_w, L1_ffn_q_b, L1_ffn_k_w, L1_ffn_k_b, L1_ffn_v_w, L1_ffn_v_b, L1_ffn_o_w, L1_ffn_o_b, L1_ffn_ln2_w, L1_ffn_ln2_b, L1_ffn_router_w, L1_ffn_fc1_w, L1_ffn_fc1_b, L1_ffn_fc2_w, L1_ffn_fc2_b)
    x = x + _L2_xattn_ref(_layernorm(x, axis=-1), ctx_1024, L2_xattn_W_ih, L2_xattn_W_hh, L2_xattn_b_ih, L2_xattn_b_hh, L2_xattn_Wq, L2_xattn_Wout, L2_xattn_b_out)
    x = x + _L2_attn_ref(_layernorm(x, axis=-1), L2_attn_W_kv_down, L2_attn_W_k_up, L2_attn_W_v_up, L2_attn_W_q, L2_attn_W_q_rope, L2_attn_W_k_rope, L2_attn_W_o)
    x = x + _L2_ffn_ref(_layernorm(x, axis=-1), L2_ffn_wq, L2_ffn_bq, L2_ffn_wk, L2_ffn_bk, L2_ffn_wv, L2_ffn_bv, L2_ffn_wo, L2_ffn_bo, L2_ffn_ln1_g, L2_ffn_ln1_b, L2_ffn_ln2_g, L2_ffn_ln2_b, L2_ffn_wr, L2_ffn_w1, L2_ffn_b1, L2_ffn_w2, L2_ffn_b2)
    x = x + _L3_xattn_ref(_layernorm(x, axis=-1), ctx_1024, ctx_1024, mask_SxS2_bk0, L3_xattn_Wq, L3_xattn_bq, L3_xattn_Wk, L3_xattn_bk, L3_xattn_Wv, L3_xattn_bv)
    x = x + _L3_attn_ref(_layernorm(x, axis=-1), L3_attn_Wq, L3_attn_Wk, L3_attn_Wv, L3_attn_Wo)
    x = x + _L3_ffn_ref(_layernorm(x, axis=-1), L3_ffn_gate, L3_ffn_W1, L3_ffn_b1, L3_ffn_W2, L3_ffn_b2)
    return x

_drawn_inputs = setup_inputs


def setup_inputs(seed=0):
    import zlib

    import numpy as np

    out = dict(_drawn_inputs(seed))
    spreads = {'L0_attn_qkv_b': (0.0, 0.1),
     'L0_attn_out_b': (0.0, 0.1),
     'L1_attn_bqk': (0.0, 0.8),
     'L1_attn_beta': (0.0, 0.8),
     'L1_attn_bv': (0.0, 0.401),
     'L1_ffn_ln1_w': (1.0, 0.6),
     'L1_ffn_ln1_b': (0.0, 0.8),
     'L1_ffn_q_b': (0.0, 0.8),
     'L1_ffn_k_b': (0.0, 2.0),
     'L1_ffn_v_b': (0.0, 0.8),
     'L1_ffn_o_b': (0.0, 0.8),
     'L1_ffn_ln2_w': (1.0, 0.6),
     'L1_ffn_ln2_b': (0.0, 0.8),
     'L1_ffn_fc1_b': (0.0, 0.8),
     'L1_ffn_fc2_b': (0.0, 0.8),
     'L2_xattn_b_ih': (0.0, 0.8),
     'L2_xattn_b_hh': (0.0, 0.8),
     'L2_xattn_b_out': (0.0, 0.8),
     'L3_ffn_b1': (0.0, 2.0),
     'L3_ffn_b2': (0.0, 2.0)}
    factors = {'L0_xattn_Wq_b': 8.0,
     'L0_xattn_Wkv_b': 5.438,
     'L0_xattn_Wo_b': 4.189,
     'L1_xattn_Wq': 3.059,
     'L1_attn_Wqk': 8.0,
     'L1_attn_gamma': 8.0,
     'L1_attn_rel_emb': 4.341,
     'L1_ffn_q_w': 8.0,
     'L1_ffn_k_w': 8.0,
     'L1_ffn_v_w': 8.0,
     'L1_ffn_o_w': 8.0,
     'L1_ffn_router_w': 8.0,
     'L1_ffn_fc1_w': 8.0,
     'L1_ffn_fc2_w': 8.0,
     'L2_xattn_W_ih': 8.0,
     'L2_xattn_W_hh': 8.0,
     'L2_xattn_Wq': 8.0,
     'L2_xattn_Wout': 6.178,
     'L2_attn_W_k_up': 6.918,
     'L2_attn_W_q': 6.89,
     'L2_attn_W_q_rope': 3.718,
     'L2_attn_W_k_rope': 3.662,
     'L2_ffn_wq': 8.0,
     'L2_ffn_bq': 8.0,
     'L2_ffn_wk': 8.0,
     'L2_ffn_bk': 200.0,
     'L2_ffn_wv': 8.0,
     'L2_ffn_bv': 8.0,
     'L2_ffn_wo': 8.0,
     'L2_ffn_bo': 8.0,
     'L2_ffn_ln1_g': 8.0,
     'L2_ffn_ln1_b': 8.0,
     'L2_ffn_ln2_g': 8.0,
     'L2_ffn_ln2_b': 8.0,
     'L2_ffn_wr': 8.0,
     'L2_ffn_w1': 8.0,
     'L2_ffn_b1': 60.67,
     'L2_ffn_w2': 8.0,
     'L2_ffn_b2': 64.0,
     'L3_xattn_Wq': 8.375,
     'L3_xattn_bq': 200.0,
     'L3_xattn_Wk': 8.595,
     'L3_xattn_bk': 200.0,
     'L3_xattn_bv': 64.0,
     'L3_attn_Wq': 14.598,
     'L3_attn_Wk': 4.801,
     'L3_attn_Wv': 3.042,
     'L3_attn_Wo': 3.055,
     'L3_ffn_W1': 4.164,
     'L3_ffn_W2': 2.896}
    for name, (base, spread) in spreads.items():
        noise = np.random.default_rng([zlib.crc32(name.encode()), seed]).standard_normal(out[name].shape)
        drawn = base * np.exp(spread * noise) if base else spread * noise
        out[name] = jnp.asarray(drawn.astype(out[name].dtype))
    for name, factor in factors.items():
        out[name] = (out[name] * factor).astype(out[name].dtype)
    return out
```

```python
from contextlib import ExitStack

import numpy as np

import concourse.bass as bass
from concourse import mybir

F32 = mybir.dt.float32
BF16 = mybir.dt.bfloat16
ALU = mybir.AluOpType
ACT = mybir.ActivationFunctionType
AX = mybir.AxisListType

P = 128
D = 128
BATCH = 32
SEQ = 32
KEYS = 257
TOKENS = BATCH * SEQ
TILES = TOKENS // P
PER_TILE = P // SEQ
BANK = 512
GROUP = BANK // P
GROUPS = TILES // GROUP
KCH = 86
KSIZES = (86, 86, 85)
MASKED = -1e30
LN_EPS = 1e-5
QMAX = 127.0
ROUND = 12582912.0
DROP = 0.8

FIRST_SEM, LAST_SEM = 110, 250
MOST_SEMS = 40
FIRST = 1
LOADED = 16


def constants():
    p = np.arange(P)
    c = {}
    c["ident"] = np.eye(P)
    c["ones"] = np.ones((P, P))
    c["upto"] = (p[:, None] <= p[None, :])
    for dk in (8, 16):
        rows = 4 * dk
        c[f"spread{dk}"] = ((p[:, None] % rows) // dk == np.arange(4)[None, :])
        c[f"own_head{dk}"] = (p[:, None] // SEQ == np.arange(rows)[None, :] // dk)
    c["block_of"] = (p[:, None] // SEQ == np.arange(4)[None, :])
    c["fold"] = (p[:, None] % SEQ == np.arange(SEQ)[None, :])
    c["causal"] = np.where(np.arange(SEQ)[None, :] > p[:, None] % SEQ, MASKED, 0.0)
    same = p[:, None] // SEQ == p[None, :] // SEQ
    c["past"] = same & (p[:, None] <= p[None, :])
    c["first_wins"] = np.broadcast_to(16.0 - np.arange(16), (P, 16))
    c["minus_half"] = np.full((P, TILES), -0.5)
    c["own_row"] = np.broadcast_to(np.eye(8).reshape(1, 64), (P, 64))
    c["batch_of_row"] = (p[:, None] == (32 * (np.arange(BATCH) // 8) + np.arange(BATCH) % 8)[None, :])
    t = np.arange(SEQ, dtype=np.float32)
    inv = (1.0 / 10000.0 ** (np.arange(0, 32, 2, dtype=np.float32) / 32)).astype(np.float32)
    ang = (inv[(p % 32) % 16][:, None] * t[None, :]).astype(np.float32)
    c["cos_half"] = np.cos(ang)
    c["sin_half"] = np.sin(ang) * np.where((p % 32) < 16, -1.0, 1.0)[:, None]
    inv = (10000.0 ** (-np.arange(0, 8, 2, dtype=np.float32) / 8)).astype(np.float32)
    ang = (inv[(p % 8) // 2][:, None] * t[None, :]).astype(np.float32)
    c["cos_pair"] = np.cos(ang)
    c["sin_pair"] = np.sin(ang) * np.where(p % 2 == 0, -1.0, 1.0)[:, None]
    return {k: np.ascontiguousarray(v, dtype=np.float32) for k, v in c.items()}


def bucket_rows():
    n = np.maximum(np.arange(SEQ)[:, None] - np.arange(SEQ)[None, :], 0)
    nf = np.maximum(n, 1).astype(np.float32)
    large = 16 + (np.log(nf / 16) / np.log(8.0) * 16).astype(np.int32)
    b = np.where(n < 16, n, np.minimum(large, 31))
    hot = b[None] == np.arange(32)[:, None, None]
    return np.ascontiguousarray(np.tile(hot, (1, 1, PER_TILE)).reshape(32, SEQ * P), dtype=np.float32)


HALF_SWAP = np.concatenate([np.arange(16, 32), np.arange(16)])
PAIR_SWAP = np.arange(P) ^ 1


def packed_weights(w):
    def mat(a):
        return np.asarray(a)

    def col(a):
        return mat(a).reshape(-1, P).T

    def row(a):
        return np.broadcast_to(mat(a).reshape(1, -1), (P, mat(a).size))

    c = {}
    kv = mat(w["L0_xattn_Wkv_w"])
    kvb = mat(w["L0_xattn_Wkv_b"])
    c["L0x_q"] = mat(w["L0_xattn_Wq_w"])
    c["L0x_k"] = kv[:, :, :16].transpose(1, 0, 2).reshape(D, D)
    c["L0x_v"] = kv[:, :, 16:].transpose(1, 0, 2).reshape(D, D)
    c["L0x_o"] = mat(w["L0_xattn_Wo_w"])
    c["L0x_qb"] = col(w["L0_xattn_Wq_b"])
    c["L0x_kb"] = kvb[:, :16].reshape(D, 1)
    c["L0x_vbc"] = kvb[:, 16:].reshape(D, 1)
    c["L0x_ob"] = row(w["L0_xattn_Wo_b"])
    qkv, qkvb = mat(w["L0_attn_qkv_w"]), mat(w["L0_attn_qkv_b"])
    for i, n in enumerate("qkv"):
        c["L0a_" + n] = qkv[:, i * D:(i + 1) * D]
    c["L0a_qb"], c["L0a_kb"], c["L0a_vb"] = col(qkvb[:D]), col(qkvb[D:2 * D]), row(qkvb[2 * D:])
    c["L0a_o"], c["L0a_ob"] = mat(w["L0_attn_out_w"]), row(w["L0_attn_out_b"])
    c["L0f_T"] = mat(w["L0_ffn_rhs"]).T
    c["L1x_q"] = mat(w["L1_xattn_Wq"])
    c["L1x_k"], c["L1x_v"] = mat(w["L1_xattn_Wkv"])[:, :D], mat(w["L1_xattn_Wkv"])[:, D:]
    c["L1a_qk"], c["L1a_qkb"] = mat(w["L1_attn_Wqk"]), col(w["L1_attn_bqk"])
    c["L1a_gamma"], c["L1a_beta"] = mat(w["L1_attn_gamma"]).T, mat(w["L1_attn_beta"]).T
    c["L1a_v"], c["L1a_vb"] = mat(w["L1_attn_Wv"]), row(w["L1_attn_bv"])
    c["L1a_rel"] = np.concatenate([mat(w["L1_attn_rel_emb"]), np.zeros((P - 32, 1), np.float32)])
    for n in "qkvo":
        c["L1f_" + n] = mat(w[f"L1_ffn_{n}_w"])
        c[f"L1f_{n}b"] = (col if n in "qk" else row)(w[f"L1_ffn_{n}_b"])
        c["L2f_" + n] = mat(w[f"L2_ffn_w{n}"])
        c[f"L2f_{n}b"] = (col if n in "qk" else row)(w[f"L2_ffn_b{n}"])
    for i in "12":
        c[f"L1f_ln{i}w"], c[f"L1f_ln{i}b"] = col(w[f"L1_ffn_ln{i}_w"]), col(w[f"L1_ffn_ln{i}_b"])
        c[f"L2f_ln{i}w"], c[f"L2f_ln{i}b"] = col(w[f"L2_ffn_ln{i}_g"]), col(w[f"L2_ffn_ln{i}_b"])
    c["L1f_r"], c["L2f_r"], c["L3f_r"] = mat(w["L1_ffn_router_w"]), mat(w["L2_ffn_wr"]), mat(w["L3_ffn_gate"])
    for n, a in (("L1f_b2", "L1_ffn_fc2_b"), ("L2f_b2", "L2_ffn_b2"), ("L3f_b2", "L3_ffn_b2")):
        b2 = mat(w[a])
        c[n] = np.concatenate([b2, np.zeros((P - b2.shape[0], D), np.float32)])
    order = np.concatenate([np.arange(0, 256), np.arange(384, 512), np.arange(256, 384)])
    c["L2x_ihx"] = mat(w["L2_xattn_W_ih"])[order, :D].T
    c["L2x_iha"] = mat(w["L2_xattn_W_ih"])[order, D:].T
    c["L2x_hh"] = mat(w["L2_xattn_W_hh"])[order].T
    c["L2x_bih"], c["L2x_bhh"] = col(mat(w["L2_xattn_b_ih"])[order]), col(mat(w["L2_xattn_b_hh"])[order])
    c["L2x_q"] = mat(w["L2_xattn_Wq"])
    c["L2x_oc"], c["L2x_oh"] = mat(w["L2_xattn_Wout"])[:, :D].T, mat(w["L2_xattn_Wout"])[:, D:].T
    c["L2x_ob"] = col(w["L2_xattn_b_out"])
    c["L2a_down"], c["L2a_k"], c["L2a_v"] = (mat(w["L2_attn_" + n]) for n in ("W_kv_down", "W_k_up", "W_v_up"))
    c["L2a_q"], c["L2a_o"] = mat(w["L2_attn_W_q"]), mat(w["L2_attn_W_o"])
    for n, a in (("qr", "L2_attn_W_q_rope"), ("kr", "L2_attn_W_k_rope")):
        c["L2a_" + n] = np.tile(mat(w[a]), (1, 4))
        c[f"L2a_{n}s"] = np.tile(mat(w[a])[:, HALF_SWAP], (1, 4))
    for n in "qkv":
        c["L3x_" + n] = mat(w[f"L3_xattn_W{n}"])
        c[f"L3x_{n}b"] = (row if n == "v" else col)(w[f"L3_xattn_b{n}"])
        c["L3a_" + n] = mat(w[f"L3_attn_W{n}"]).T
    for n in "qk":
        c[f"L3a_{n}s"] = mat(w[f"L3_attn_W{n}"]).T[:, PAIR_SWAP]
    c["L3a_o"] = mat(w["L3_attn_Wo"]).T
    return c


def packed_experts(w1, b1, w2):
    w1, b1, w2 = np.asarray(w1), np.asarray(b1), np.asarray(w2)
    e, _, f = w1.shape
    n = f // P
    w2 = w2.reshape(e, n, P, D).transpose(0, 2, 1, 3).reshape(e, P, n * D)
    return np.concatenate([w1, w2, b1.reshape(e, n, P).transpose(0, 2, 1)], axis=2)


class Env:

    def __init__(self, nc, stack):
        self.nc, self.stack, self.n, self.next_sem = nc, stack, 0, FIRST_SEM

    def sb(self, stack, name, shape, dt=F32):
        self.n += 1
        return stack.enter_context(self.nc.sbuf_tensor(f"{name}_{self.n}", shape, dt))

    def sem(self, stack, name):
        self.n += 1
        self.next_sem += 1
        return stack.enter_context(self.nc.semaphore(f"{name}_{self.n}", num=self.next_sem - 1))

    def stage(self):
        if self.next_sem > LAST_SEM - MOST_SEMS:
            with self.nc.Block() as block:
                @block.sync
                def _(sp):
                    sp.sem_clear(range(FIRST_SEM, LAST_SEM))
            self.next_sem = FIRST_SEM

    def w(self, name):
        a, b = self.wcols[name]
        return self.W[:, a:b]

    def c(self, name):
        a, b = self.ccols[name]
        return self.C[:, a:b]

    def bank(self, b, n=BANK):
        return self.PS[:, b, 0:n]


def head_start(env, semaphores):
    with env.nc.Block() as block:
        @block.sync
        def _(sp):
            for sem in semaphores:
                sp.sem_inc(sem, FIRST)


def over(ap, axis, shape):
    return ap.unsqueeze(axis).broadcast_to(shape)


def norm_transpose(env, src, turned, keep=None, scale=None, shift=None):
    nc = env.nc
    env.stage()
    with ExitStack() as s:
        z = keep if keep is not None else env.sb(s, "normed", [P, TILES, D])
        stats = env.sb(s, "stats", [P, TILES, 6])
        mv = env.sb(s, "mean_var", [P, TILES, 2])
        var_eps = env.sb(s, "var_eps", [P, TILES])
        rstd = env.sb(s, "rstd", [P, TILES])
        have_var = env.sem(s, "have_var")
        have_rstd = env.sem(s, "have_rstd")
        tile_normed = env.sem(s, "tile_normed")
        tile_turned = env.sem(s, "tile_turned")
        with nc.Block() as block:
            @block.vector
            def _(dve):
                for t in range(TILES):
                    nc.vector.bn_stats(stats[:, t, :], src[:, t, :])
                dve.drain()
                for t in range(TILES):
                    nc.vector.bn_aggr(mv[:, t, :], stats[:, t, :])
                dve.drain()
                nc.vector.tensor_scalar(var_eps[:, :], mv[:, :, 1], LN_EPS, None, ALU.add).then_inc(have_var, 1)
                dve.wait_ge(have_rstd, 1)
                for t in range(TILES):
                    nc.vector.tensor_scalar(z[:, t, :], src[:, t, :], mv[:, t, 0:1], rstd[:, t:t + 1],
                                            ALU.subtract, ALU.mult).then_inc(tile_normed, 1)

            @block.gpsimd
            def _(pool):
                pool.wait_ge(have_var, 1)
                nc.gpsimd.tensor_tensor(rstd[:, :], var_eps[:, :], env.c("minus_half"),
                                        ALU.pow).then_inc(have_rstd, 1)

            @block.tensor
            def _(pe):
                for t in range(TILES):
                    pe.wait_ge(tile_normed, t + 1)
                    nc.tensor.transpose(env.PS[:, t // 4, (t % 4) * P:(t % 4 + 1) * P], z[:, t, :],
                                        env.c("ident")).then_inc(tile_turned, 1)

            @block.scalar
            def _(act):
                for h in range(2):
                    act.wait_ge(tile_turned, 4 * (h + 1))
                    if scale is None:
                        nc.scalar.copy(turned[:, h * BANK:(h + 1) * BANK], env.bank(h))
                    else:
                        nc.scalar.activation(turned[:, h * BANK:(h + 1) * BANK], env.bank(h), ACT.Identity,
                                             bias=shift, scale=scale)


def project(env, out, weight, src, bias=None):
    nc = env.nc
    env.stage()
    with ExitStack() as s:
        half_done = env.sem(s, "half_projected")
        with nc.Block() as block:
            @block.tensor
            def _(pe):
                for h in range(2):
                    nc.tensor.matmul(env.bank(h), weight, src[:, h * BANK:(h + 1) * BANK],
                                     start=True, stop=True).then_inc(half_done, 1)

            @block.scalar
            def _(act):
                for h in range(2):
                    act.wait_ge(half_done, h + 1)
                    nc.scalar.activation(out[:, h * BANK:(h + 1) * BANK], env.bank(h), ACT.Identity,
                                         bias=0.0 if bias is None else bias)


def self_attention(env, layer, R, qsrc, kvsrc, scale, causal=False, biases=True, rope=None, qk_rope=False):
    nc = env.nc
    env.stage()
    nb = GROUP * PER_TILE
    w = lambda n: env.w(layer + n)
    spread, block_of, ident = env.c("spread8"), env.c("block_of"), env.c("ident")
    PS = env.PS
    with ExitStack() as s:
        two = range(GROUPS)
        q = [env.sb(s, f"q{g}", [P, BANK]) for g in two]
        kbd = [env.sb(s, f"k_spread{g}", [P, nb, 4, SEQ]) for g in two]
        kb4 = env.sb(s, "k_bias_spread", [P, 4])
        v = [env.sb(s, f"v_own{g}", [P, GROUP, PER_TILE, 4, 4, 8]) for g in two]
        sc = [env.sb(s, f"scores{g}", [P, 4, GROUP, 4, SEQ]) for g in two]
        probsT = [env.sb(s, f"probsT{g}", [P, 4, GROUP, P]) for g in two]
        top = [env.sb(s, f"top{g}", [P, 4, GROUP, 4]) for g in two]
        total = [env.sb(s, f"total{g}", [P, 4, GROUP, 4]) for g in two]
        att = [env.sb(s, f"att{g}", [P, GROUP, D]) for g in two]
        attT = [env.sb(s, f"attT{g}", [P, BANK]) for g in two]
        if rope or qk_rope:
            rot = env.sb(s, "rot", [P, nb, SEQ])
            rot2 = env.sb(s, "rot2", [P, nb, SEQ])
            krot = env.sb(s, "k_rotated", [P, nb, SEQ])
        if qk_rope:
            qr = [env.sb(s, f"q_rope{g}", [P, BANK]) for g in two]
            kr = [env.sb(s, f"k_rope{g}", [P, nb, 4, SEQ]) for g in two]
        names = ("kb_spread", "projected", "q_ready", "k_rotated", "k_ready", "v_projected", "v_ready", "scored",
                 "shifted", "exped", "turned", "probsT_ready", "weighed", "att_ready", "att_turned", "attT_ready",
                 "out_projected", "rope_projected", "rope_ready")
        S = {n: env.sem(s, n) for n in names}

        def banked(b):
            return PS[:, b, :].rearrange("p (b q) -> p b q", q=SEQ)

        with nc.Block() as block:
            @block.tensor
            def _(pe):
                def project_group(g):
                    cols = slice(g * BANK, (g + 1) * BANK)
                    nc.tensor.matmul(PS[:, 4 * g, :], w("q"), qsrc[:, cols], start=True, stop=True)
                    last = nc.tensor.matmul(PS[:, 4 * g + 1, :], w("k"), kvsrc[:, cols], start=True, stop=True)
                    if rope:
                        nc.tensor.matmul(PS[:, 4 * g + 2, :], w("qs"), qsrc[:, cols], start=True, stop=True)
                        last = nc.tensor.matmul(PS[:, 4 * g + 3, :], w("ks"), kvsrc[:, cols], start=True, stop=True)
                    last.then_inc(S["projected"], 1)

                def rope_group(g):
                    cols = slice(g * BANK, (g + 1) * BANK)
                    pe.wait_ge(S["q_ready"], g + 1)
                    pe.wait_ge(S["k_ready"], g + 1)
                    for i, (name, src) in enumerate((("qr", qsrc), ("qrs", qsrc), ("kr", kvsrc), ("krs", kvsrc))):
                        last = nc.tensor.matmul(PS[:, 4 * g + i, :], w(name), src[:, cols], start=True, stop=True)
                    last.then_inc(S["rope_projected"], 1)

                def values(g):
                    mine = w("v").rearrange("p (c h e) -> p h c e", c=4, h=4)
                    for n in range(nb):
                        at = g * BANK + n * SEQ
                        for h in range(4):
                            last = nc.tensor.matmul(PS[32 * h:32 * h + 32, 4 + g, n * 32:(n + 1) * 32],
                                                    kvsrc[:, at:at + SEQ], mine[:, h, :, :], start=True, stop=True)
                    last.then_inc(S["v_projected"], 1)

                def scores(g):
                    pe.wait_ge(S["q_ready"], g + 1)
                    pe.wait_ge(S["k_ready"], g + 1)
                    if qk_rope:
                        pe.wait_ge(S["rope_ready"], g + 1)
                    for t in range(GROUP):
                        for c in range(4):
                            r = slice(32 * c, 32 * c + 32)
                            for b in range(PER_TILE):
                                n = t * PER_TILE + b
                                o = PS[32 * b:32 * b + 32, 4 * g + c, t * P:(t + 1) * P]
                                last = nc.tensor.matmul(o, q[g][r, n * SEQ:(n + 1) * SEQ], kbd[g][r, n, :, :],
                                                        start=True, stop=not qk_rope)
                                if qk_rope:
                                    last = nc.tensor.matmul(o, qr[g][r, n * SEQ:(n + 1) * SEQ], kr[g][r, n, :, :],
                                                            start=False, stop=True)
                    last.then_inc(S["scored"], 1)

                def weigh(g):
                    pe.wait_ge(S["exped"], g + 1)
                    for c in range(4):
                        for t in range(GROUP):
                            last = nc.tensor.transpose(PS[:, 4 * g + c, t * P:(t + 1) * P], sc[g][:, c, t, :, :],
                                                       ident)
                        last.then_inc(S["turned"], 1)
                    pe.wait_ge(S["probsT_ready"], 2 * (g + 1))
                    for t in range(GROUP):
                        for c in range(4):
                            for b in range(PER_TILE):
                                last = nc.tensor.matmul(PS[32 * b:32 * b + 32, 4 * g, t * P + 32 * c:t * P + 32 * c + 32],
                                                        probsT[g][:, c, t, 32 * b:32 * b + 32], v[g][:, t, b, c, :, :],
                                                        start=True, stop=True)
                    last.then_inc(S["weighed"], 1)

                def finish(g):
                    pe.wait_ge(S["att_ready"], g + 1)
                    for t in range(GROUP):
                        last = nc.tensor.transpose(PS[:, 4 * g + 1, t * P:(t + 1) * P], att[g][:, t, :], ident)
                    last.then_inc(S["att_turned"], 1)
                    pe.wait_ge(S["attT_ready"], g + 1)
                    for t in range(GROUP):
                        last = nc.tensor.matmul(PS[:, 4 * g + 2, t * P:(t + 1) * P], attT[g][:, t * P:(t + 1) * P],
                                                w("o"), start=True, stop=True)
                    last.then_inc(S["out_projected"], 1)

                project_group(0)
                values(0)
                values(1)
                if qk_rope:
                    rope_group(0)
                scores(0)
                pe.wait_ge(S["v_ready"], 2)
                project_group(1)
                if qk_rope:
                    rope_group(1)
                scores(1)
                weigh(0)
                finish(0)
                weigh(1)
                finish(1)

            @block.scalar
            def _(act):
                def keys(g):
                    if rope:
                        act.wait_ge(S["k_rotated"], g + 1)
                    else:
                        act.wait_ge(S["projected"], g + 1)
                    for j in range(4):
                        last = nc.scalar.activation(kbd[g][:, :, j, :], krot[:, :, :] if rope else banked(4 * g + 1),
                                                    ACT.Identity, scale=spread[:, j:j + 1],
                                                    bias=kb4[:, j:j + 1] if biases else 0.0)
                    last.then_inc(S["k_ready"], 1)

                def values(g):
                    act.wait_ge(S["v_projected"], g + 1)
                    for j in range(4):
                        last = nc.scalar.activation(v[g][:, :, :, :, j, :].rearrange("p t b c e -> p (t b c) e"),
                                                    PS[:, 4 + g, :].rearrange("p (n e) -> p n e", e=8),
                                                    ACT.Copy, scale=block_of[:, j:j + 1])
                    last.then_inc(S["v_ready"], 1)

                def exp(g):
                    act.wait_ge(S["shifted"], g + 1)
                    nc.scalar.activation(sc[g][:, :, :, :, :], sc[g][:, :, :, :, :], ACT.Exp, scale=scale
                                         ).then_inc(S["exped"], 1)

                def turned(g):
                    act.wait_ge(S["turned"], 4 * g + 2)
                    nc.scalar.copy(probsT[g][:, 0:2, :, :],
                                   PS[:, 4 * g:4 * g + 2, :].rearrange("p c (t r) -> p c t r", t=GROUP)
                                   ).then_inc(S["probsT_ready"], 1)
                    act.wait_ge(S["turned"], 4 * g + 4)
                    nc.scalar.copy(probsT[g][:, 2:4, :, :],
                                   PS[:, 4 * g + 2:4 * g + 4, :].rearrange("p c (t r) -> p c t r", t=GROUP)
                                   ).then_inc(S["probsT_ready"], 1)

                def finish(g):
                    act.wait_ge(S["att_turned"], g + 1)
                    nc.scalar.copy(attT[g][:, :], PS[:, 4 * g + 1, :]).then_inc(S["attT_ready"], 1)

                if biases:
                    act.wait_ge(S["kb_spread"], 1)
                keys(0)
                values(0)
                values(1)
                keys(1)
                exp(0)
                turned(0)
                exp(1)
                finish(0)
                turned(1)
                finish(1)

            @block.vector
            def _(dve):
                def rotate(out, plain, swapped, cos, sin):
                    nc.vector.tensor_tensor(rot[:, :, :], banked(plain), over(env.c(cos), 1, [P, nb, SEQ]), ALU.mult)
                    nc.vector.tensor_tensor(rot2[:, :, :], banked(swapped), over(env.c(sin), 1, [P, nb, SEQ]),
                                            ALU.mult)
                    dve.drain()
                    return nc.vector.tensor_tensor(out, rot[:, :, :], rot2[:, :, :], ALU.add)

                def queries(g):
                    dve.wait_ge(S["projected"], g + 1)
                    if rope:
                        if g > 0:
                            dve.wait_ge(S["k_ready"], g)
                        rotate(krot[:, :, :], 4 * g + 1, 4 * g + 3, "cos_pair", "sin_pair").then_inc(S["k_rotated"], 1)
                        dve.drain()
                        rotate(q[g][:, :].rearrange("p (b q) -> p b q", q=SEQ), 4 * g, 4 * g + 2,
                               "cos_pair", "sin_pair").then_inc(S["q_ready"], 1)
                    elif biases:
                        nc.vector.tensor_scalar(q[g][:, :], PS[:, 4 * g, :], w("qb"), None, ALU.add
                                                ).then_inc(S["q_ready"], 1)
                    else:
                        nc.vector.tensor_copy(q[g][:, :], PS[:, 4 * g, :]).then_inc(S["q_ready"], 1)
                    if qk_rope:
                        dve.wait_ge(S["rope_projected"], g + 1)
                        rotate(qr[g][:, :].rearrange("p (b q) -> p b q", q=SEQ), 4 * g, 4 * g + 1,
                               "cos_half", "sin_half")
                        dve.drain()
                        rotate(krot[:, :, :], 4 * g + 2, 4 * g + 3, "cos_half", "sin_half")
                        dve.drain()
                        nc.vector.tensor_copy(kr[g][:, :, :, :], over(krot[:, :, :], 2, [P, nb, 4, SEQ])
                                              ).then_inc(S["rope_ready"], 1)

                def softmax(g):
                    dve.wait_ge(S["scored"], g + 1)
                    raw = PS[:, 4 * g:4 * g + 4, :].rearrange("p c (t h k) -> p (c t) h k", h=4, k=SEQ)
                    mine = sc[g][:, :, :, :, :].rearrange("p c t h k -> p (c t) h k")
                    if causal:
                        nc.vector.tensor_tensor(sc[g][:, :, :, :, :].rearrange("p c t h k -> p (c t h) k"),
                                                PS[:, 4 * g:4 * g + 4, :].rearrange("p c (n k) -> p (c n) k", k=SEQ),
                                                over(env.c("causal"), 1, [P, 16 * GROUP, SEQ]), ALU.add)
                        dve.drain()
                        raw = mine
                    tops = top[g][:, :, :, :].rearrange("p c t h -> p (c t) h")
                    nc.vector.tensor_reduce(tops, raw, AX.X, ALU.max)
                    dve.drain()
                    nc.vector.tensor_tensor(mine, raw, over(tops, 3, [P, 4 * GROUP, 4, SEQ]), ALU.subtract
                                            ).then_inc(S["shifted"], 1)

                def sums(g):
                    dve.wait_ge(S["exped"], g + 1)
                    nc.vector.tensor_reduce(total[g][:, :, :, :], sc[g][:, :, :, :, :], AX.X, ALU.add)
                    dve.drain()
                    nc.vector.reciprocal(total[g][:, :, :, :], total[g][:, :, :, :])

                def normalise(g):
                    dve.drain()
                    dve.wait_ge(S["weighed"], g + 1)
                    for c in range(4):
                        last = nc.vector.tensor_tensor(
                            att[g][:, :, 32 * c:32 * c + 32].rearrange("p t (h e) -> p t h e", h=4),
                            PS[:, 4 * g, :].rearrange("p (t c h e) -> p t c h e", t=GROUP, c=4, h=4)[:, :, c, :, :],
                            over(total[g][:, c, :, :], 3, [P, GROUP, 4, 8]), ALU.mult)
                    if biases:
                        dve.drain()
                        last = nc.vector.tensor_tensor(att[g][:, :, :], att[g][:, :, :],
                                                       over(w("vb"), 1, [P, GROUP, D]), ALU.add)
                    last.then_inc(S["att_ready"], 1)

                def add(g):
                    dve.wait_ge(S["out_projected"], g + 1)
                    here = R[:, g * GROUP:(g + 1) * GROUP, :]
                    nc.vector.tensor_tensor(here, here, PS[:, 4 * g + 2, :].rearrange("p (t d) -> p t d", t=GROUP),
                                            ALU.add)
                    if biases:
                        dve.drain()
                        nc.vector.tensor_tensor(here, here, over(w("ob"), 1, [P, GROUP, D]), ALU.add)

                if biases:
                    nc.vector.tensor_scalar(kb4[:, :], spread, w("kb"), None, ALU.mult).then_inc(S["kb_spread"], 1)
                queries(0)
                softmax(0)
                queries(1)
                sums(0)
                softmax(1)
                normalise(0)
                sums(1)
                add(0)
                normalise(1)
                add(1)


def cross_attention(env, layer, X, ctxT, qT, dk, scale, biases):
    nc = env.nc
    env.stage()
    rows = 4 * dk
    n_c = D // rows
    per_batch = n_c // 2
    units = PER_TILE * per_batch
    w = lambda n: env.w(layer + n)
    spread, own, fold, ident = env.c(f"spread{dk}"), env.c(f"own_head{dk}"), env.c("fold"), env.c("ident")
    PS = env.PS
    KT, V, PT, REST = 6, 7, 4, 5
    OT_COLS, RT_COLS, OUT_COLS = slice(256, 384), slice(384, 416), slice(KEYS, KEYS + D)
    with ExitStack() as s:
        one = env.sb(s, "ctx_batch", [P, KEYS])
        kT = env.sb(s, "kT", [P, KEYS])
        v = [env.sb(s, f"v{i}", [KCH, 3, D]) for i in range(2)]
        qbd = [env.sb(s, f"q_spread{i}", [P, 4, SEQ]) for i in range(2)]
        probs = [env.sb(s, f"probs{i}", [P, 2, KEYS]) for i in range(2)]
        probsT = env.sb(s, "probsT", [KCH, 3, 2 * P])
        top = env.sb(s, "top", [P, 2])
        ntop = [env.sb(s, f"minus_top{i}", [P, 2]) for i in range(2)]
        total = [env.sb(s, f"total{i}", [P, n_c]) for i in range(2)]
        inv = env.sb(s, "inv", [P, n_c])
        inv_own = env.sb(s, "inv_own", [P, n_c, rows])
        oh = env.sb(s, "own_out", [P, 4, SEQ])
        o = env.sb(s, "unscaled", [P, SEQ])
        attT = env.sb(s, "attT", [P, P])
        names = ("ctx_copied", "kv_projected", "kT_ready", "q_ready", "v_ready", "scored", "top_ready", "exped",
                 "turned", "probsT_ready", "weighed", "inv_ready", "inv_turned", "batch_read", "attT_ready",
                 "out_projected", "tile_added")
        S = {n: env.sem(s, n) for n in names}
        head_start(env, [S[n] for n in ("kv_projected", "tile_added", "batch_read")])

        def unit(t, i):
            return t * units + i, t * PER_TILE + i // per_batch, i // per_batch % PER_TILE, i % per_batch

        with nc.Block() as block:
            @block.gpsimd
            def _(pool):
                with pool.Fori(0, BATCH) as k:
                    pool.wait_ge(S["kv_projected"], FIRST + k)
                    nc.gpsimd.tensor_copy(one[:, :], ctxT[:, k, :]).then_inc(S["ctx_copied"], 1)

            @block.tensor
            def _(pe):
                def keys_values(k):
                    pe.wait_ge(S["ctx_copied"], k + 1)
                    nc.tensor.matmul(PS[:, KT, 0:KEYS], w("k"), one[:, :], start=True, stop=True)
                    for i in range(3):
                        last = nc.tensor.matmul(PS[0:KSIZES[i], V, i * P:(i + 1) * P],
                                                one[:, i * KCH:i * KCH + KSIZES[i]], w("v"), start=True, stop=True)
                    last.then_inc(S["kv_projected"], 1)

                def scores(k, j, u, parity):
                    if u == 0:
                        pe.wait_ge(S["kT_ready"], k + 1)
                        pe.wait_ge(S["q_ready"], k + 1)
                    for c in range(2):
                        r = slice(rows * (2 * u + c), rows * (2 * u + c + 1))
                        last = nc.tensor.matmul(PS[:, 2 * parity + c, 0:KEYS], qbd[j % 2][r, :, :], kT[r, :],
                                                start=True, stop=True)
                    last.then_inc(S["scored"], 1)

                def turn(n, k, u, parity):
                    pe.wait_ge(S["exped"], n * 2 + 2)
                    if u == 0:
                        pe.wait_ge(S["batch_read"], FIRST + k)
                    for i in range(3):
                        for c in range(2):
                            o_cols = (i % 2) * 2 * P + c * P
                            last = nc.tensor.transpose(PS[0:KSIZES[i], PT + i // 2, o_cols:o_cols + P],
                                                       probs[parity][:, c, i * KCH:i * KCH + KSIZES[i]], ident)
                        if i > 0:
                            last.then_inc(S["turned"], 1)

                def weigh(n, k, j, u):
                    if u == 0:
                        pe.wait_ge(S["v_ready"], k + 1)
                    pe.wait_ge(S["probsT_ready"], n * 2 + 2)
                    for i in range(3):
                        for c in range(2):
                            r = slice(rows * (2 * u + c), rows * (2 * u + c + 1))
                            last = nc.tensor.matmul(PS[r, REST, OT_COLS], v[j % 2][0:KSIZES[i], i, r],
                                                    probsT[0:KSIZES[i], i, c * P:(c + 1) * P],
                                                    start=i == 0, stop=i == 2)
                    last.then_inc(S["weighed"], 1)
                    if u == per_batch - 1:
                        pe.wait_ge(S["inv_ready"], k + 1)
                        for c in range(n_c):
                            last = nc.tensor.matmul(PS[rows * c:rows * (c + 1), REST, RT_COLS], inv_own[:, c, :], fold,
                                                    start=True, stop=True)
                        last.then_inc(S["inv_turned"], 1)

                def step(t, i, ahead=True):
                    n, k, j, u = unit(t, i)
                    if ahead:
                        _, nk, nj, nu = unit(t, i + 1)
                        if nu == 0:
                            pe.wait_ge(S["v_ready"], nk)
                            if i == 1:
                                pe.wait_ge(S["tile_added"], FIRST + t)
                            keys_values(nk)
                    turn(n, k, u, i % 2)
                    if ahead:
                        scores(nk, nj, nu, (i + 1) % 2)
                    if i == units:
                        finish(t)
                    weigh(n, k, j, u)

                def finish(t):
                    pe.wait_ge(S["attT_ready"], t + 1)
                    if biases:
                        out = nc.tensor.matmul(PS[:, KT, OUT_COLS], attT[:, :], w("o"), start=True, stop=True)
                    else:
                        out = nc.tensor.transpose(PS[:, KT, OUT_COLS], attT[:, :], ident)
                    out.then_inc(S["out_projected"], 1)

                keys_values(0)
                scores(0, 0, 0, 0)
                step(0, 0)
                with pe.Fori(0, TILES - 1) as t:
                    for i in range(1, units + 1):
                        step(t, i)
                for i in range(1, units):
                    step(TILES - 1, i, ahead=i < units - 1)
                finish(TILES - 1)

            @block.scalar
            def _(act):
                def keys(k):
                    act.wait_ge(S["kv_projected"], FIRST + k + 1)
                    nc.scalar.activation(kT[:, :], PS[:, KT, 0:KEYS], ACT.Identity,
                                         bias=w("kb") if biases else 0.0).then_inc(S["kT_ready"], 1)

                def exp(n, j, u, parity):
                    act.wait_ge(S["top_ready"], n + 1)
                    for c in range(2):
                        nc.scalar.activation(probs[parity][:, c, :], PS[:, 2 * parity + c, 0:KEYS], ACT.Exp,
                                             bias=ntop[parity][:, c:c + 1], scale=scale,
                                             accum_out=total[j % 2][:, 2 * u + c:2 * u + c + 1]
                                             ).then_inc(S["exped"], 1)

                def step(t, i, ahead=True):
                    n = unit(t, i)[0]
                    if ahead:
                        _, nk, nj, nu = unit(t, i + 1)
                        if nu == 0:
                            keys(nk)
                    act.wait_ge(S["turned"], n * 2 + 2)
                    nc.scalar.copy(probsT[0:KSIZES[2], 2, :], PS[0:KSIZES[2], REST, 0:2 * P]
                                   ).then_inc(S["probsT_ready"], 1)
                    if ahead:
                        exp(n + 1, nj, nu, (i + 1) % 2)

                keys(0)
                exp(0, 0, 0, 0)
                step(0, 0)
                with act.Fori(0, TILES - 1) as t:
                    for i in range(1, units + 1):
                        step(t, i)
                for i in range(1, units):
                    step(TILES - 1, i, ahead=i < units - 1)

            @block.vector
            def _(dve):
                def queries(k, j):
                    nc.vector.tensor_tensor(qbd[j % 2][:, :, :], over(qT[:, bass.ds(k * SEQ, SEQ)], 1, [P, 4, SEQ]),
                                            over(spread, 2, [P, 4, SEQ]), ALU.mult).then_inc(S["q_ready"], 1)

                def values(k, j):
                    dve.wait_ge(S["kv_projected"], FIRST + k + 1)
                    for n, i0, i1 in ((KCH, 0, 2), (KSIZES[2], 2, 3)):
                        last = nc.vector.tensor_copy(v[j % 2][0:n, i0:i1, :],
                                                     PS[0:n, V, i0 * P:i1 * P].rearrange("p (i d) -> p i d", d=D))
                    dve.drain()
                    dve.sem_inc(S["v_ready"], 1)

                def maximum(n, parity):
                    dve.wait_ge(S["scored"], n + 1)
                    nc.vector.tensor_reduce(top[:, :], PS[:, 2 * parity:2 * parity + 2, 0:KEYS], AX.X, ALU.max)
                    dve.drain()
                    nc.vector.tensor_scalar(ntop[parity][:, :], top[:, :], -scale, None, ALU.mult
                                            ).then_inc(S["top_ready"], 1)

                def step(t, i, ahead=True):
                    n, k, j, u = unit(t, i)
                    ends = u == per_batch - 1
                    if ahead:
                        _, nk, nj, nu = unit(t, i + 1)
                        if nu == 0:
                            queries(nk, nj)
                            values(nk, nj)
                    if ends:
                        dve.wait_ge(S["exped"], n * 2 + 2)
                        nc.vector.reciprocal(inv[:, :], total[j % 2][:, :])
                    dve.wait_ge(S["turned"], n * 2 + 1)
                    nc.vector.tensor_copy(probsT[:, 0:2, :], PS[0:KCH, PT, :].rearrange("p (i r) -> p i r", i=2)
                                          ).then_inc(S["probsT_ready"], 1)
                    if ends:
                        dve.drain()
                        nc.vector.tensor_tensor(inv_own[:, :, :], over(inv[:, :], 2, [P, n_c, rows]),
                                                over(own, 1, [P, n_c, rows]), ALU.mult).then_inc(S["inv_ready"], 1)
                    if ahead:
                        maximum(n + 1, (i + 1) % 2)
                    if i == units:
                        add(t)
                    if ends:
                        dve.wait_ge(S["weighed"], n + 1)
                        dve.wait_ge(S["inv_turned"], k + 1)
                        nc.vector.tensor_tensor(oh[:, :, :], PS[:, REST, OT_COLS].rearrange("p (h q) -> p h q", h=4),
                                                over(spread, 2, [P, 4, SEQ]), ALU.mult)
                        dve.drain()
                        nc.vector.tensor_reduce(o[:, :], oh[:, :, :].rearrange("p h q -> p q h"), AX.X, ALU.add)
                        dve.drain()
                        nc.vector.tensor_tensor(attT[:, j * SEQ:(j + 1) * SEQ], PS[:, REST, RT_COLS], o[:, :],
                                                ALU.mult).then_inc(S["batch_read"], 1)
                        if j == PER_TILE - 1:
                            dve.drain()
                            if biases:
                                nc.vector.tensor_scalar(attT[:, :], attT[:, :], w("vbc"), None, ALU.add)
                                dve.drain()
                            dve.sem_inc(S["attT_ready"], 1)

                def add(t):
                    here = X[:, t, :] if isinstance(t, int) else X[:, bass.ds(t, 1), :].rearrange("p o d -> p (o d)")
                    dve.wait_ge(S["out_projected"], t + 1)
                    nc.vector.tensor_tensor(here, here, PS[:, KT, OUT_COLS], ALU.add)
                    dve.drain()
                    dve.sem_inc(S["tile_added"], 1)
                    if biases:
                        nc.vector.tensor_tensor(here, here, w("ob"), ALU.add)

                queries(0, 0)
                values(0, 0)
                maximum(0, 0)
                step(0, 0)
                with dve.Fori(0, TILES - 1) as t:
                    for i in range(1, units + 1):
                        step(t, i)
                for i in range(1, units):
                    step(TILES - 1, i, ahead=i < units - 1)
                add(TILES - 1)


def single_cross_attention(env, layer, X, ctxT, qT, mask, scale):
    nc = env.nc
    env.stage()
    w = lambda n: env.w(layer + n)
    ident = env.c("ident")
    PS = env.PS
    with ExitStack() as s:
        one = env.sb(s, "ctx_batch", [P, KEYS])
        kT = env.sb(s, "kT", [P, KEYS])
        q = env.sb(s, "q_tile", [P, P])
        v = env.sb(s, "v", [KCH, PER_TILE, 3, D])
        sc = env.sb(s, "scores", [P, KEYS])
        probs = env.sb(s, "probs", [P, KEYS])
        probsT = env.sb(s, "probsT", [KCH, 3, P])
        stat = env.sb(s, "stat", [P, 4])
        names = ("ctx_copied", "q_copied", "kv_projected", "kT_ready", "v_ready", "scored", "top_ready", "exped",
                 "turned", "probsT_ready", "weighed", "tile_added")
        S = {n: env.sem(s, n) for n in names}
        head_start(env, [S[n] for n in ("kv_projected", "tile_added", "kT_ready", "v_ready", "scored")])
        with nc.Block() as block:
            @block.gpsimd
            def _(pool):
                with pool.Fori(0, BATCH) as k:
                    pool.wait_ge(S["kv_projected"], FIRST + k)
                    nc.gpsimd.tensor_copy(one[:, :], ctxT[:, k, :]).then_inc(S["ctx_copied"], 1)

            @block.tensor
            def _(pe):
                with pe.Fori(0, TILES) as t:
                    pe.wait_ge(S["tile_added"], FIRST + t)
                    for j in range(PER_TILE):
                        k = t * PER_TILE + j
                        pe.wait_ge(S["ctx_copied"], k + 1)
                        pe.wait_ge(S["kT_ready"], FIRST + k)
                        pe.wait_ge(S["v_ready"], FIRST + k)
                        nc.tensor.matmul(PS[:, 4, 0:KEYS], w("k"), one[:, :], start=True, stop=True)
                        for i in range(3):
                            last = nc.tensor.matmul(PS[0:KSIZES[i], 5, i * P:(i + 1) * P],
                                                    one[:, i * KCH:i * KCH + KSIZES[i]], w("v"),
                                                    start=True, stop=True)
                        last.then_inc(S["kv_projected"], 1)
                        pe.wait_ge(S["kT_ready"], FIRST + k + 1)
                        if j == 0:
                            pe.wait_ge(S["q_copied"], t + 1)
                        nc.tensor.matmul(PS[32 * j:32 * j + 32, 0, 0:KEYS], q[:, 32 * j:32 * j + 32], kT[:, :],
                                         start=True, stop=True).then_inc(S["scored"], 1)
                    pe.wait_ge(S["exped"], t + 1)
                    for i in range(3):
                        last = nc.tensor.transpose(PS[0:KSIZES[i], 6, i * P:(i + 1) * P],
                                                   probs[:, i * KCH:i * KCH + KSIZES[i]], ident)
                    last.then_inc(S["turned"], 1)
                    pe.wait_ge(S["probsT_ready"], t + 1)
                    pe.wait_ge(S["v_ready"], FIRST + (t + 1) * PER_TILE)
                    for j in range(PER_TILE):
                        for i in range(3):
                            last = nc.tensor.matmul(PS[32 * j:32 * j + 32, 7, 0:D],
                                                    probsT[0:KSIZES[i], i, 32 * j:32 * j + 32],
                                                    v[0:KSIZES[i], j, i, :], start=i == 0, stop=i == 2)
                    last.then_inc(S["weighed"], 1)

            @block.scalar
            def _(act):
                with act.Fori(0, TILES) as t:
                    for j in range(PER_TILE):
                        k = t * PER_TILE + j
                        act.wait_ge(S["kv_projected"], FIRST + k + 1)
                        act.wait_ge(S["scored"], FIRST + k)
                        nc.scalar.activation(kT[:, :], PS[:, 4, 0:KEYS], ACT.Identity,
                                             bias=w("kb")).then_inc(S["kT_ready"], 1)
                    act.wait_ge(S["top_ready"], t + 1)
                    nc.scalar.activation(probs[:, :], sc[:, :], ACT.Exp, bias=stat[:, 1:2], scale=scale,
                                         accum_out=stat[:, 2:3]).then_inc(S["exped"], 1)

            @block.vector
            def _(dve):
                with dve.Fori(0, TILES) as t:
                    nc.vector.tensor_copy(q[:, :], qT[:, bass.ts(t, P)]).then_inc(S["q_copied"], 1)
                    for j in range(PER_TILE):
                        dve.wait_ge(S["kv_projected"], FIRST + t * PER_TILE + j + 1)
                        for n, i0, i1 in ((KCH, 0, 2), (KSIZES[2], 2, 3)):
                            nc.vector.tensor_tensor(v[0:n, j, i0:i1, :],
                                                    PS[0:n, 5, i0 * P:i1 * P].rearrange("p (i d) -> p i d", d=D),
                                                    over(w("vb")[0:n], 1, [n, i1 - i0, D]), ALU.add)
                        dve.drain()
                        dve.sem_inc(S["v_ready"], 1)
                    dve.wait_ge(S["scored"], FIRST + (t + 1) * PER_TILE)
                    nc.vector.tensor_tensor(sc[:, :], PS[:, 0, 0:KEYS], mask[:, :], ALU.add)
                    dve.drain()
                    nc.vector.tensor_reduce(stat[:, 0:1], sc[:, :], AX.X, ALU.max)
                    dve.drain()
                    nc.vector.tensor_scalar(stat[:, 1:2], stat[:, 0:1], -scale, None, ALU.mult
                                            ).then_inc(S["top_ready"], 1)
                    dve.wait_ge(S["exped"], t + 1)
                    nc.vector.reciprocal(stat[:, 3:4], stat[:, 2:3])
                    dve.wait_ge(S["turned"], t + 1)
                    nc.vector.tensor_copy(probsT[:, 0:2, :],
                                          PS[0:KCH, 6, 0:2 * P].rearrange("p (i r) -> p i r", r=P))
                    nc.vector.tensor_copy(probsT[0:KSIZES[2], 2, :], PS[0:KSIZES[2], 6, 2 * P:3 * P])
                    dve.drain()
                    dve.sem_inc(S["probsT_ready"], 1)
                    dve.wait_ge(S["weighed"], t + 1)
                    nc.vector.scalar_tensor_tensor(X[:, t, :], PS[:, 7, 0:D], stat[:, 3:4], X[:, t, :],
                                                   ALU.mult, ALU.add)
                    dve.drain()
                    dve.sem_inc(S["tile_added"], 1)


def int8_matmul(env, X, z):
    nc = env.nc
    env.stage()
    PS = env.PS
    WT = env.w("L0f_T")
    ident = env.c("ident")
    with ExitStack() as s:
        qz = env.sb(s, "z_rounded", [P, TILES, D])
        zs = env.sb(s, "z_scale", [P, TILES])
        zi = env.sb(s, "z_inverse", [P, TILES])
        qw = env.sb(s, "w_rounded", [P, D])
        ws = env.sb(s, "w_scale", [P, 2])
        diag = env.sb(s, "w_scale_diag", [P, P])
        wrow = env.sb(s, "w_scale_row", [P, P])
        qwT = env.sb(s, "w_turned", [P, D], BF16)
        qzT = env.sb(s, "z_turned", [P, TOKENS], BF16)
        prod = env.sb(s, "product", [P, TILES, D])
        names = ("w_rounded", "w_turned", "z_rounded", "z_turned", "copied", "multiplied")
        S = {n: env.sem(s, n) for n in names}
        with nc.Block() as block:
            @block.vector
            def _(dve):
                def rounded(out, values, inverse):
                    nc.vector.tensor_tensor(out, values, inverse, ALU.mult)
                    dve.drain()
                    nc.vector.tensor_scalar(out, out, ROUND, ROUND, ALU.add, ALU.subtract)
                    dve.drain()
                    return nc.vector.tensor_scalar(out, out, QMAX, -QMAX, ALU.min, ALU.max)

                nc.vector.tensor_reduce(ws[:, 0:1], WT, AX.X, ALU.max, apply_absolute_value=True)
                nc.vector.tensor_reduce(zs[:, :], z[:, :, :], AX.X, ALU.max, apply_absolute_value=True)
                dve.drain()
                nc.vector.tensor_scalar(ws[:, 0:1], ws[:, 0:1], 1e-12, 1.0 / QMAX, ALU.max, ALU.mult)
                nc.vector.tensor_scalar(zs[:, :], zs[:, :], 1e-12, 1.0 / QMAX, ALU.max, ALU.mult)
                dve.drain()
                nc.vector.reciprocal(ws[:, 1:2], ws[:, 0:1])
                nc.vector.reciprocal(zi[:, :], zs[:, :])
                nc.vector.tensor_scalar(diag[:, :], ident, ws[:, 0:1], None, ALU.mult)
                dve.drain()
                rounded(qw[:, :], WT, ws[:, 1:2].broadcast_to([P, D])).then_inc(S["w_rounded"], 1)
                rounded(qz[:, :, :], z[:, :, :], over(zi[:, :], 2, [P, TILES, D])).then_inc(S["z_rounded"], 1)
                dve.wait_ge(S["w_turned"], 1)
                nc.vector.tensor_copy(wrow[:, :], PS[:, 4, 0:P])
                nc.vector.tensor_copy(qwT[:, :], PS[:, 4, P:2 * P]).then_inc(S["copied"], 1)
                dve.drain()
                for h in range(2):
                    dve.wait_ge(S["multiplied"], h + 1)
                    half = slice(4 * h, 4 * h + 4)
                    nc.vector.tensor_tensor(prod[:, half, :], PS[:, 2 + h, :].rearrange("p (t d) -> p t d", t=4),
                                            over(zs[:, half], 2, [P, 4, D]), ALU.mult)
                dve.drain()
                nc.vector.tensor_tensor(prod[:, :, :], prod[:, :, :], over(wrow[:, :], 1, [P, TILES, D]), ALU.mult)
                dve.drain()
                nc.vector.tensor_tensor(X[:, :, :], X[:, :, :], prod[:, :, :], ALU.add)

            @block.tensor
            def _(pe):
                pe.wait_ge(S["w_rounded"], 1)
                nc.tensor.matmul(PS[:, 4, 0:P], env.c("ones"), diag[:, :], start=True, stop=True)
                nc.tensor.transpose(PS[:, 4, P:2 * P], qw[:, :], ident).then_inc(S["w_turned"], 1)
                pe.wait_ge(S["z_rounded"], 1)
                for t in range(TILES):
                    nc.tensor.transpose(PS[:, t // 4, (t % 4) * P:(t % 4 + 1) * P], qz[:, t, :], ident
                                        ).then_inc(S["z_turned"], 1)
                for t in range(TILES):
                    if t % 4 == 0:
                        pe.wait_ge(S["copied"], 2 + t // 4)
                    last = nc.tensor.matmul(PS[:, 2 + t // 4, (t % 4) * P:(t % 4 + 1) * P],
                                            qzT[:, t * P:(t + 1) * P], qwT[:, :], start=True, stop=True)
                    if t % 4 == 3:
                        last.then_inc(S["multiplied"], 1)

            @block.scalar
            def _(act):
                act.wait_ge(S["copied"], 1)
                for h in range(2):
                    act.wait_ge(S["z_turned"], 4 * (h + 1))
                    nc.scalar.copy(qzT[:, h * BANK:(h + 1) * BANK], env.bank(h)).then_inc(S["copied"], 1)


def laplacian_attention(env, X, zT, bucket_dram):
    nc = env.nc
    env.stage()
    PS = env.PS
    mu, std = float(np.sqrt(0.5)), float(np.sqrt(0.25 * np.pi))
    w = lambda n: env.w("L1a_" + n)
    with ExitStack() as s:
        hot = env.sb(s, "buckets", [32, SEQ, P])
        bias = env.sb(s, "bias", [P, SEQ])
        qk = env.sb(s, "qk", [P, TOKENS])
        q = env.sb(s, "q", [P, TOKENS])
        k = env.sb(s, "k", [P, TOKENS])
        v = env.sb(s, "v", [P, TILES, D])
        sim = env.sb(s, "sim", [P, TILES, P])
        near = env.sb(s, "near_zero", [P, TILES, P])
        cum = env.sb(s, "gelu", [P, TILES, P])
        names = ("buckets_loaded", "bias_summed", "qk_projected", "qk_swished", "q_ready", "v_projected",
                 "v_biased", "v_ready", "scored", "sim_ready", "gelu_ready", "weights_ready", "weighed")
        S = {n: env.sem(s, n) for n in names}
        with nc.Block() as block:
            @block.sync
            def _(sp):
                sp.dma_start(hot[:, :, :], bucket_dram.rearrange("n (q p) -> n q p", q=SEQ)
                             ).then_inc(S["buckets_loaded"], 16)

            @block.tensor
            def _(pe):
                for h in range(2):
                    nc.tensor.matmul(env.bank(h), w("qk"), zT[:, h * BANK:(h + 1) * BANK], start=True, stop=True
                                     ).then_inc(S["qk_projected"], 1)
                for t in range(TILES):
                    last = nc.tensor.matmul(PS[:, 2 + t // 4, (t % 4) * P:(t % 4 + 1) * P],
                                            zT[:, t * P:(t + 1) * P], w("v"), start=True, stop=True)
                last.then_inc(S["v_projected"], 1)
                pe.wait_ge(S["buckets_loaded"], LOADED)
                for i in range(SEQ):
                    last = nc.tensor.matmul(PS[:, 4, i:i + 1], hot[:, i, :], w("rel")[0:32], start=True, stop=True)
                last.then_inc(S["bias_summed"], 1)
                pe.wait_ge(S["q_ready"], 1)
                for t in range(TILES):
                    last = nc.tensor.matmul(PS[:, 6 + t // 4, (t % 4) * P:(t % 4 + 1) * P],
                                            k[:, t * P:(t + 1) * P], q[:, t * P:(t + 1) * P], start=True, stop=True)
                last.then_inc(S["scored"], 1)
                pe.wait_ge(S["weights_ready"], 1)
                pe.wait_ge(S["v_ready"], 1)
                for t in range(TILES):
                    last = nc.tensor.matmul(PS[:, t // 4, (t % 4) * P:(t % 4 + 1) * P], sim[:, t, :], v[:, t, :],
                                            start=True, stop=True)
                last.then_inc(S["weighed"], 1)

            @block.scalar
            def _(act):
                for h in range(2):
                    act.wait_ge(S["qk_projected"], h + 1)
                    nc.scalar.activation(qk[:, h * BANK:(h + 1) * BANK], env.bank(h), ACT.Silu, bias=w("qkb")
                                         ).then_inc(S["qk_swished"], 1)
                act.wait_ge(S["v_biased"], 1)
                nc.scalar.activation(v[:, :, :], v[:, :, :], ACT.Silu).then_inc(S["v_ready"], 1)
                act.wait_ge(S["sim_ready"], 1)
                nc.scalar.activation(cum[:, :, :], near[:, :, :], ACT.Gelu).then_inc(S["gelu_ready"], 1)

            @block.vector
            def _(dve):
                dve.wait_ge(S["v_projected"], 1)
                nc.vector.tensor_tensor(v[:, :, :], PS[:, 2:4, :].rearrange("p h (t d) -> p (h t) d", t=4),
                                        over(w("vb"), 1, [P, TILES, D]), ALU.add).then_inc(S["v_biased"], 1)
                dve.wait_ge(S["qk_swished"], 2)
                for out, i in ((q, 0), (k, 1)):
                    nc.vector.tensor_scalar(out[:, :], qk[:, :], w("gamma")[:, i:i + 1], w("beta")[:, i:i + 1],
                                            ALU.mult, ALU.add)
                dve.drain()
                dve.sem_inc(S["q_ready"], 1)
                dve.wait_ge(S["bias_summed"], 1)
                nc.vector.tensor_scalar(bias[:, :], PS[:, 4, 0:SEQ], float(D ** 0.5), -mu, ALU.mult, ALU.add)
                dve.drain()
                dve.wait_ge(S["scored"], 1)
                nc.vector.scalar_tensor_tensor(sim[:, :, :].rearrange("p t (b q) -> p (t b) q", q=SEQ),
                                               PS[:, 6:8, :].rearrange("p h (b q) -> p (h b) q", q=SEQ), 1.0 / SEQ,
                                               over(bias[:, :], 1, [P, BATCH, SEQ]), ALU.mult, ALU.add)
                dve.drain()
                nc.vector.tensor_scalar(sim[:, :, :], sim[:, :, :], 1.0 / std, None, ALU.mult)
                dve.drain()
                nc.vector.tensor_scalar(near[:, :, :], sim[:, :, :], 0.0, 1e-20, ALU.is_equal, ALU.mult)
                dve.drain()
                nc.vector.tensor_tensor(near[:, :, :], near[:, :, :], sim[:, :, :], ALU.add
                                        ).then_inc(S["sim_ready"], 1)
                dve.drain()
                nc.vector.reciprocal(sim[:, :, :], near[:, :, :])
                dve.wait_ge(S["gelu_ready"], 1)
                dve.drain()
                nc.vector.tensor_tensor(sim[:, :, :], sim[:, :, :], cum[:, :, :], ALU.mult)
                dve.drain()
                nc.vector.tensor_tensor(sim[:, :, :], sim[:, :, :], over(env.c("past"), 1, [P, TILES, P]), ALU.mult
                                        ).then_inc(S["weights_ready"], 1)
                dve.wait_ge(S["weighed"], 1)
                nc.vector.tensor_tensor(X[:, :, :], X[:, :, :], PS[:, 0:2, :].rearrange("p h (t d) -> p (h t) d", t=4),
                                        ALU.add)


def route(env, gates, gatesT, zT, router, n_experts, capacity, floor, factor):
    nc = env.nc
    env.stage()
    PS = env.PS
    E = n_experts
    full = [P, TILES, E]
    with ExitStack() as s:
        lg = env.sb(s, "logits", full)
        tmp = env.sb(s, "masked_logits", full)
        m = env.sb(s, "best_two", [P, 2, TILES, E])
        pr = env.sb(s, "probs", full)
        st = env.sb(s, "stats", [P, TILES, 6])
        run = env.sb(s, "running", [P, 2, 2 * TILES, E])
        names = ("logits_done", "shifted", "exped", "hot_ready", "summed", "gates_ready", "gates_turned")
        S = {n: env.sem(s, n) for n in names}
        with nc.Block() as block:
            @block.tensor
            def _(pe):
                for t in range(TILES):
                    last = nc.tensor.matmul(PS[:, 0, t * E:(t + 1) * E], zT[:, t * P:(t + 1) * P], router,
                                            start=True, stop=True)
                last.then_inc(S["logits_done"], 1)
                if capacity is not None:
                    pe.wait_ge(S["hot_ready"], 1)
                    flat = m[:, :, :, :].rearrange("p n t e -> p (n t e)")
                    nc.tensor.matmul(PS[:, 1, 0:2 * TILES * E], env.c("upto"), flat, start=True, stop=True)
                    nc.tensor.matmul(PS[:, 2, 0:2 * TILES * E], env.c("ones"), flat, start=True, stop=True
                                     ).then_inc(S["summed"], 1)
                pe.wait_ge(S["gates_ready"], 1)
                for t in range(TILES):
                    last = nc.tensor.transpose(PS[0:E, 3 + t // 4, (t % 4) * P:(t % 4 + 1) * P], gates[:, t, :],
                                               env.c("ident"))
                last.then_inc(S["gates_turned"], 1)

            @block.scalar
            def _(act):
                act.wait_ge(S["shifted"], 1)
                nc.scalar.activation(pr[:, :, :], pr[:, :, :], ACT.Exp).then_inc(S["exped"], 1)

            @block.vector
            def _(dve):
                def st_over(i):
                    return st[:, :, i:i + 1].broadcast_to(full)

                def best(out, values):
                    nc.vector.tensor_reduce(st[:, :, 0], values, AX.X, ALU.max)
                    dve.drain()
                    nc.vector.tensor_tensor(out, values, st_over(0), ALU.is_equal)
                    dve.drain()
                    nc.vector.tensor_tensor(out, out, over(env.c("first_wins")[:, 0:E], 1, full), ALU.mult)
                    dve.drain()
                    nc.vector.tensor_reduce(st[:, :, 1], out, AX.X, ALU.max)
                    dve.drain()
                    nc.vector.tensor_tensor(out, out, st_over(1), ALU.is_equal)
                    dve.drain()

                dve.wait_ge(S["logits_done"], 1)
                nc.vector.tensor_copy(lg[:, :, :], PS[:, 0, 0:TILES * E].rearrange("p (t e) -> p t e", e=E))
                dve.drain()
                best(m[:, 0, :, :], lg[:, :, :])
                nc.vector.tensor_tensor(pr[:, :, :], lg[:, :, :], st_over(0), ALU.subtract).then_inc(S["shifted"], 1)
                nc.vector.scalar_tensor_tensor(tmp[:, :, :], m[:, 0, :, :], MASKED, lg[:, :, :], ALU.mult, ALU.add)
                dve.drain()
                best(m[:, 1, :, :], tmp[:, :, :])
                dve.sem_inc(S["hot_ready"], 1)
                dve.wait_ge(S["exped"], 1)
                nc.vector.tensor_reduce(st[:, :, 2], pr[:, :, :], AX.X, ALU.add)
                dve.drain()
                nc.vector.reciprocal(st[:, :, 3], st[:, :, 2])
                dve.drain()
                nc.vector.tensor_tensor(pr[:, :, :], pr[:, :, :], st_over(3), ALU.mult)
                if capacity is not None:
                    n = 2 * TILES
                    dve.wait_ge(S["summed"], 1)
                    totals = PS[:, 2, 0:n * E].rearrange("p (n e) -> p n e", e=E)
                    nc.vector.memset(run[:, 0, 0:1, :], 0.0)
                    nc.vector.tensor_copy(run[:, 0, 1:n, :], totals[:, 0:n - 1, :])
                    src = 0
                    for shift in (1, 2, 4, 8):
                        dve.drain()
                        nc.vector.tensor_copy(run[:, 1 - src, 0:shift, :], run[:, src, 0:shift, :])
                        nc.vector.tensor_tensor(run[:, 1 - src, shift:n, :], run[:, src, shift:n, :],
                                                run[:, src, 0:n - shift, :], ALU.add)
                        src = 1 - src
                    dve.drain()
                    nc.vector.tensor_tensor(run[:, src, :, :], run[:, src, :, :],
                                            PS[:, 1, 0:n * E].rearrange("p (n e) -> p n e", e=E), ALU.add)
                    dve.drain()
                    hot = m[:, :, :, :].rearrange("p n t e -> p (n t) e")
                    nc.vector.scalar_tensor_tensor(hot, run[:, src, :, :], float(capacity), hot,
                                                   ALU.is_le, ALU.mult)
                dve.drain()
                nc.vector.tensor_tensor(tmp[:, :, :], m[:, 0, :, :], m[:, 1, :, :], ALU.add)
                dve.drain()
                nc.vector.tensor_tensor(pr[:, :, :], pr[:, :, :], tmp[:, :, :], ALU.mult)
                dve.drain()
                nc.vector.tensor_reduce(st[:, :, 4], pr[:, :, :], AX.X, ALU.add)
                dve.drain()
                nc.vector.tensor_scalar(st[:, :, 4], st[:, :, 4], floor, None, ALU.max)
                dve.drain()
                nc.vector.reciprocal(st[:, :, 5], st[:, :, 4])
                dve.drain()
                nc.vector.scalar_tensor_tensor(gates[:, :, :], pr[:, :, :], factor, st_over(5), ALU.mult, ALU.mult
                                               ).then_inc(S["gates_ready"], 1)
                dve.wait_ge(S["gates_turned"], 1)
                nc.vector.tensor_copy(gatesT[0:E, :], PS[0:E, 3:5, :].rearrange("p h c -> p (h c)"))


def experts(env, acc, zT, gates, gatesT, dram, b2, n_experts, hidden, func):
    nc = env.nc
    env.stage()
    PS = env.PS
    n_f = hidden // P
    cols = hidden + n_f * D + n_f
    units = 2 * n_f
    with ExitStack() as s:
        wt = [env.sb(s, f"expert{i}", [P, cols]) for i in range(2)]
        h = [env.sb(s, f"hidden{i}", [P, n_f, TOKENS]) for i in range(2)]
        gc = [env.sb(s, f"gate_col{i}", [P, TILES]) for i in range(2)]
        names = ("b2_done", "acc_begun", "fc1_done", "hidden_ready", "fc2_done", "added", "gate_copied")
        S = {n: env.sem(s, n) for n in names}
        loaded = [env.sem(s, f"expert_loaded{i}") for i in range(2)]
        head_start(env, [S[n] for n in ("fc2_done", "hidden_ready", "added")])
        with nc.Block() as block:
            @block.sync
            def _(sp):
                with sp.Fori(0, n_experts // 2) as i:
                    for x in range(2):
                        sp.wait_ge(S["fc2_done"], FIRST + i * 2 * TILES)
                        sp.dma_start(wt[x][:, :], dram[i * 2 + x, :, :]).then_inc(loaded[x], 16)

            @block.tensor
            def _(pe):
                for t in range(TILES):
                    last = nc.tensor.matmul(PS[:, 4 + t // 4, (t % 4) * P:(t % 4 + 1) * P],
                                            gatesT[0:n_experts, t * P:(t + 1) * P], b2[0:n_experts],
                                            start=True, stop=True)
                last.then_inc(S["b2_done"], 1)
                pe.wait_ge(S["acc_begun"], 1)
                with pe.Fori(0, n_experts // 2) as i:
                    for x in range(2):
                        e = i * 2 + x
                        pe.wait_ge(loaded[x], i * 16 + 16)
                        for u in range(units):
                            f, half = u // 2, u % 2
                            if u >= 4:
                                pe.wait_ge(S["hidden_ready"], FIRST + e * units + u - 3)
                            elif x == 0:
                                pe.wait_ge(S["hidden_ready"], FIRST + i * 2 * units)
                            else:
                                pe.wait_ge(S["hidden_ready"], FIRST + (i * 2 + 1) * units - 3 + u)
                            nc.tensor.matmul(PS[:, u % 4, :], wt[x][:, f * P:(f + 1) * P],
                                             zT[:, half * BANK:(half + 1) * BANK], start=True, stop=True
                                             ).then_inc(S["fc1_done"], 1)
                        pe.wait_ge(S["hidden_ready"], FIRST + (e + 1) * units)
                        for t in range(TILES):
                            if t >= 4:
                                pe.wait_ge(S["added"], FIRST + e * TILES + t - 3)
                            else:
                                pe.wait_ge(S["added"], FIRST + e * TILES)
                            for f in range(n_f):
                                last = nc.tensor.matmul(PS[:, 4 + t % 4, 0:D], h[x][:, f, t * P:(t + 1) * P],
                                                        wt[x][:, hidden + f * D:hidden + (f + 1) * D],
                                                        start=f == 0, stop=f == n_f - 1)
                            last.then_inc(S["fc2_done"], 1)

            @block.scalar
            def _(act):
                with act.Fori(0, n_experts // 2) as i:
                    for x in range(2):
                        e = i * 2 + x
                        act.wait_ge(loaded[x], i * 16 + 16)
                        act.wait_ge(S["fc2_done"], FIRST + i * 2 * TILES)
                        for u in range(units):
                            f, half = u // 2, u % 2
                            act.wait_ge(S["fc1_done"], e * units + u + 1)
                            nc.scalar.activation(h[x][:, f, half * BANK:(half + 1) * BANK], PS[:, u % 4, :], func,
                                                 bias=wt[x][:, hidden + n_f * D + f:hidden + n_f * D + f + 1]
                                                 ).then_inc(S["hidden_ready"], 1)

            @block.gpsimd
            def _(pool):
                with pool.Fori(0, n_experts // 2) as i:
                    for x in range(2):
                        pool.wait_ge(S["added"], FIRST + i * 2 * TILES)
                        nc.gpsimd.tensor_copy(gc[x][:, :], gates[:, :, bass.ds(i * 2 + x, 1)].rearrange("p t o -> p (t o)")
                                              ).then_inc(S["gate_copied"], 1)

            @block.vector
            def _(dve):
                dve.wait_ge(S["b2_done"], 1)
                nc.vector.tensor_copy(acc[:, :, :], PS[:, 4:6, :].rearrange("p h (t d) -> p (h t) d", t=4)
                                      ).then_inc(S["acc_begun"], 1)
                dve.drain()
                with dve.Fori(0, n_experts // 2) as i:
                    for x in range(2):
                        e = i * 2 + x
                        dve.wait_ge(S["gate_copied"], e + 1)
                        for t in range(TILES):
                            dve.wait_ge(S["fc2_done"], FIRST + e * TILES + t + 1)
                            nc.vector.scalar_tensor_tensor(acc[:, t, :], PS[:, 4 + t % 4, 0:D], gc[x][:, t:t + 1],
                                                           acc[:, t, :], ALU.mult, ALU.add).then_inc(S["added"], 1)
                        dve.drain()


def add_to(env, X, others):
    nc = env.nc
    with nc.Block() as block:
        @block.vector
        def _(dve):
            for o in others:
                nc.vector.tensor_tensor(X[:, :, :], X[:, :, :], o[:, :, :], ALU.add)
                dve.drain()


def context_lstm(env, X, zT, ctxT):
    nc = env.nc
    env.stage()
    PS = env.PS
    w = lambda n: env.w("L2x_" + n)
    ident = env.c("ident")
    own_row = env.c("own_row").rearrange("p (i m) -> p i m", i=8)
    batch_of_row = env.c("batch_of_row")
    GATES, CTX, OUT = (0, 7), 5, 6
    TURNED, SCORES = (1, 2), (3, 4)
    HALF = 4
    with ExitStack() as s:
        keysT = env.sb(s, "scored_ctxT", [P, BATCH, KEYS])
        rows = env.sb(s, "projected_ctx", [P, BATCH, 2, D])
        lastrow = env.sb(s, "projected_ctx_last", [P, D])
        gx = env.sb(s, "gates_of_x", [P, SEQ + 1, 4, BATCH])
        w_a = env.sb(s, "w_attn", [P, 4 * P])
        w_h = env.sb(s, "w_hidden", [P, 4 * P])
        w_o = env.sb(s, "w_out_hidden", [P, P])
        gb = env.sb(s, "gate_bias", [P, 4])
        outs = env.sb(s, "outs", [P, BATCH, SEQ])
        attn = env.sb(s, "attn", [P, BATCH])
        h2 = env.sb(s, "h2", [P, BATCH])
        c2 = env.sb(s, "c2", [P, BATCH])
        gt = env.sb(s, "gates_tanh", [P, 4, BATCH])
        u = env.sb(s, "in_part", [P, BATCH])
        f = env.sb(s, "kept_part", [P, BATCH])
        tc = env.sb(s, "tanh_c", [P, BATCH])
        gate_spread = env.sb(s, "out_gate_spread", [P, 4, 8, 8])
        hbd = env.sb(s, "h_spread", [P, 4, 8, 8])
        ntop = [env.sb(s, f"minus_top{x}", [P, 1]) for x in range(2)]
        total = [env.sb(s, f"total{x}", [P, 1]) for x in range(2)]
        inv = [env.sb(s, f"inv{x}", [P, 1]) for x in range(2)]
        probs = [env.sb(s, f"probs{x}", [P, KEYS]) for x in range(2)]
        pT = [env.sb(s, f"probsT_spread{x}", [P, 2, 4, HALF, 8]) for x in range(2)]
        share = env.sb(s, "inv_of_row", [P, 4, 8])
        last_share = env.sb(s, "last_prob_of_row", [P, 4, 8])
        cx = env.sb(s, "ctx_sum", [P, D])
        names = ("weights_ready", "gx_done", "gx_ready", "keys_done", "keys_ready", "rows_done", "rows_ready",
                 "gates_done", "tanh_ready", "c_ready", "tanh_c_ready", "h_ready", "h_spread", "scored",
                 "top_ready", "exped", "turned", "pT_ready", "summed", "cx_ready", "share_ready",
                 "out_done", "attn_ready", "outs_turned")
        S = {n: env.sem(s, n) for n in names}
        head_start(env, [S["attn_ready"]])
        with nc.Block() as block:
            @block.vector
            def _(dve):
                nc.vector.tensor_scalar(w_h[:, 0:3 * P], w("hh")[:, 0:3 * P], 0.25, None, ALU.mult)
                nc.vector.tensor_scalar(w_h[:, 3 * P:4 * P], w("hh")[:, 3 * P:4 * P], 0.5, None, ALU.mult)
                nc.vector.tensor_scalar(w_a[:, 0:3 * P], w("iha")[:, 0:3 * P], 0.5, None, ALU.mult)
                nc.vector.tensor_copy(w_a[:, 3 * P:4 * P], w("iha")[:, 3 * P:4 * P])
                nc.vector.tensor_scalar(w_o[:, :], w("oh"), 0.5, None, ALU.mult)
                nc.vector.tensor_tensor(gb[:, :], w("bih"), w("bhh"), ALU.add)
                dve.drain()
                nc.vector.tensor_scalar(gb[:, 0:3], gb[:, 0:3], 0.5, None, ALU.mult).then_inc(S["weights_ready"], 1)
                nc.vector.memset(attn[:, :], 0.0)
                nc.vector.memset(h2[:, :], 0.0)
                nc.vector.memset(c2[:, :], 0.0)
                nc.vector.memset(gx[:, SEQ, :, :], 0.0)
                nc.vector.memset(PS[:, SCORES[0], :], 0.0)
                nc.vector.memset(PS[:, SCORES[1], :], 0.0)
                nc.vector.memset(PS[:, CTX, :], 0.0)
                dve.drain()
                dve.sem_inc(S["rows_ready"], 1)
                for n in range(BATCH // 2):
                    dve.wait_ge(S["rows_done"], n + 1)
                    nc.vector.tensor_copy(rows[:, 2 * n:2 * n + 2, :, :].rearrange("p b c d -> p (b c d)"),
                                          PS[:, 6 + n % 2, :]).then_inc(S["rows_ready"], 1)
                dve.wait_ge(S["rows_done"], BATCH // 2 + 1)
                nc.vector.tensor_copy(lastrow[:, :], PS[:, CTX, 0:D])

            @block.tensor
            def _(pe):
                for n in range(BATCH // 2):
                    for b in (2 * n, 2 * n + 1):
                        if b >= 3:
                            pe.wait_ge(S["keys_ready"], b - 2)
                        nc.tensor.matmul(PS[:, b % 3, 0:KEYS], w("q"), ctxT[:, b, :], start=True, stop=True
                                         ).then_inc(S["keys_done"], 1)
                    if n >= 2:
                        pe.wait_ge(S["rows_ready"], n)
                    for x in range(4):
                        last = nc.tensor.matmul(PS[:, 6 + n % 2, x * D:(x + 1) * D],
                                                ctxT[:, 2 * n + x // 2, x % 2 * P:(x % 2 + 1) * P], w("oc"),
                                                start=True, stop=True)
                    last.then_inc(S["rows_done"], 1)
                for j in range(4):
                    last = nc.tensor.matmul(PS[32 * j:32 * j + 8, CTX, 0:D], ctxT[:, 8 * j:8 * j + 8, KEYS - 1],
                                            w("oc"), start=True, stop=True)
                last.then_inc(S["rows_done"], 1)
                pe.wait_ge(S["keys_ready"], BATCH)
                for i in range(4):
                    for half in range(2):
                        n = 2 * i + half
                        if n >= 3:
                            pe.wait_ge(S["gx_ready"], n - 2)
                        nc.tensor.matmul(PS[:, n % 3, :], w("ihx")[:, i * P:(i + 1) * P],
                                         zT[:, half * BANK:(half + 1) * BANK], start=True, stop=True
                                         ).then_inc(S["gx_done"], 1)

            @block.scalar
            def _(act):
                for b in range(BATCH):
                    act.wait_ge(S["keys_done"], b + 1)
                    nc.scalar.activation(keysT[:, b, :], PS[:, b % 3, 0:KEYS], ACT.Copy, scale=0.5
                                         ).then_inc(S["keys_ready"], 1)
                act.wait_ge(S["weights_ready"], 1)
                for i in range(4):
                    for half in range(2):
                        n = 2 * i + half
                        b = slice(half * BATCH // 2, (half + 1) * BATCH // 2)
                        act.wait_ge(S["gx_done"], n + 1)
                        nc.scalar.activation(gx[:, 0:SEQ, i, b].rearrange("p t b -> p b t"),
                                             PS[:, n % 3, :].rearrange("p (b t) -> p b t", t=SEQ), ACT.Identity,
                                             bias=gb[:, i:i + 1], scale=0.5 if i < 3 else 1.0
                                             ).then_inc(S["gx_ready"], 1)

        STEPS = 4

        def steps_of(turn):
            return [turn * STEPS + i for i in range(STEPS)]

        with nc.Block() as block:
            @block.tensor
            def _(pe):
                def gates_of_x(t, bank):
                    nc.tensor.matmul(PS[:, bank, 0:4 * BATCH], ident,
                                     gx[:, bass.ds(t, 1), :, :].rearrange("p o g b -> p (o g b)"),
                                     start=True, stop=False)

                def gates_of(weights, state, i, bank, last=False):
                    return nc.tensor.matmul(PS[:, bank, i * BATCH:(i + 1) * BATCH], weights[:, i * P:(i + 1) * P],
                                            state[:, :], start=False, stop=last)

                gates_of_x(0, GATES[0])
                for i in range(4):
                    gates_of(w_h, h2, i, GATES[0])
                with pe.Fori(0, SEQ // STEPS) as turn:
                    for t, (now, then) in zip(steps_of(turn), (GATES, GATES[::-1]) * (STEPS // 2)):
                        pe.wait_ge(S["attn_ready"], FIRST + t)
                        for i in range(4):
                            last = gates_of(w_a, attn, i, now, last=i == 3)
                        last.then_inc(S["gates_done"], 1)
                        gates_of_x(t + 1, then)
                        nc.tensor.matmul(PS[:, TURNED[0], :], ident, zT[:, 0:BANK],
                                         start=True, stop=True)
                        for x in range(2):
                            pe.wait_ge(S["h_spread"], t * 2 + x + 1)
                            for i in range(HALF):
                                for j in range(4):
                                    last = nc.tensor.matmul(PS[32 * j:32 * j + 8, SCORES[x], 0:KEYS],
                                                            hbd[:, j, HALF * x + i, :],
                                                            keysT[:, 8 * j + HALF * x + i, :],
                                                            start=i == 0, stop=i == HALF - 1)
                            last.then_inc(S["scored"], 1)
                        for x in range(2):
                            pe.wait_ge(S["exped"], t * 2 + x + 1)
                            for c in range(2):
                                last = nc.tensor.transpose(PS[:, TURNED[x], c * P:(c + 1) * P],
                                                           probs[x][:, c * P:(c + 1) * P], ident)
                            last.then_inc(S["turned"], 1)
                            if x == 0:
                                pe.wait_ge(S["h_ready"], t + 1)
                            gates_of(w_h, h2, 2 * x, then)
                            gates_of(w_h, h2, 2 * x + 1, then)
                            if x == 0:
                                nc.tensor.matmul(PS[:, OUT, 0:BATCH], w_o[:, :], h2[:, :], start=True, stop=False)
                            for c in range(2):
                                pe.wait_ge(S["pT_ready"], t * 4 + 2 * x + c + 1)
                                for i in range(HALF):
                                    for j in range(4):
                                        last = nc.tensor.matmul(PS[32 * j:32 * j + 8, CTX, 0:D], pT[x][:, c, j, i, :],
                                                                rows[:, 8 * j + HALF * x + i, c, :],
                                                                start=x + i + c == 0, stop=x * c * i == HALF - 1)
                        last.then_inc(S["summed"], 1)
                        pe.wait_ge(S["share_ready"], t + 1)
                        nc.tensor.matmul(PS[:, OUT, 0:BATCH], lastrow[:, :],
                                         last_share[:, :, :].rearrange("p j i -> p (j i)"), start=False, stop=False)
                        pe.wait_ge(S["cx_ready"], t + 1)
                        nc.tensor.matmul(PS[:, OUT, 0:BATCH], cx[:, :], share[:, :, :].rearrange("p j i -> p (j i)"),
                                         start=False, stop=True).then_inc(S["out_done"], 1)
                nc.tensor.matmul(PS[:, GATES[0], 0:1], ident, gx[:, SEQ, 0, 0:1], start=False, stop=True)

            @block.scalar
            def _(act):
                with act.Fori(0, SEQ // STEPS) as turn:
                    for t, now in zip(steps_of(turn), GATES * (STEPS // 2)):
                        act.wait_ge(S["gates_done"], t + 1)
                        nc.scalar.activation(gt[:, :, :].rearrange("p g b -> p (g b)"), PS[:, now, 0:4 * BATCH], ACT.Tanh
                                             ).then_inc(S["tanh_ready"], 1)
                        act.wait_ge(S["c_ready"], t + 1)
                        nc.scalar.activation(tc[:, :], c2[:, :], ACT.Tanh, scale=0.5).then_inc(S["tanh_c_ready"], 1)
                        for x in range(2):
                            act.wait_ge(S["top_ready"], t * 2 + x + 1)
                            nc.scalar.activation(probs[x][:, :], PS[:, SCORES[x], 0:KEYS], ACT.Exp, bias=ntop[x][:, :],
                                                 accum_out=total[x][:, :]).then_inc(S["exped"], 1)
                        act.wait_ge(S["out_done"], t + 1)
                        nc.scalar.activation(attn[:, :], PS[:, OUT, 0:BATCH], ACT.Tanh, bias=w("ob")
                                             ).then_inc(S["attn_ready"], 1)
                        act.drain()
                        nc.scalar.copy(outs[:, :, bass.ds(t, 1)].rearrange("p b o -> p (b o)"), attn[:, :])

            @block.vector
            def _(dve):
                def by_row(values):
                    return values.rearrange("p (j i) -> p j i", i=8)

                def spread_rows(out, values, x):
                    mine = own_row[:, HALF * x:HALF * (x + 1), :]
                    return nc.vector.tensor_tensor(out, values.unsqueeze(3).broadcast_to([P, 4, HALF, 8]),
                                                   over(mine, 1, [P, 4, HALF, 8]), ALU.mult)

                with dve.Fori(0, SEQ // STEPS) as turn:
                    for t in steps_of(turn):
                        dve.wait_ge(S["tanh_ready"], t + 1)
                        nc.vector.scalar_tensor_tensor(u[:, :], gt[:, 0, :], 1.0, gt[:, 3, :], ALU.add, ALU.mult)
                        nc.vector.scalar_tensor_tensor(f[:, :], gt[:, 1, :], 1.0, c2[:, :], ALU.add, ALU.mult)
                        dve.drain()
                        nc.vector.scalar_tensor_tensor(c2[:, :], f[:, :], 0.5, u[:, :], ALU.mult, ALU.add
                                                       ).then_inc(S["c_ready"], 1)
                        nc.vector.scalar_tensor_tensor(gate_spread[:, :, :, :], by_row(gt[:, 2, :]).unsqueeze(3)
                                                       .broadcast_to([P, 4, 8, 8]), 1.0,
                                                       over(own_row, 1, [P, 4, 8, 8]), ALU.add, ALU.mult)
                        dve.drain()
                        dve.wait_ge(S["tanh_c_ready"], t + 1)
                        for x in range(2):
                            i = slice(HALF * x, HALF * (x + 1))
                            nc.vector.tensor_tensor(hbd[:, :, i, :], gate_spread[:, :, i, :],
                                                    by_row(tc[:, :])[:, :, i].unsqueeze(3)
                                                    .broadcast_to([P, 4, HALF, 8]), ALU.mult
                                                    ).then_inc(S["h_spread"], 1)
                        nc.vector.scalar_tensor_tensor(h2[:, :], gt[:, 2, :], 1.0, tc[:, :], ALU.add, ALU.mult
                                                       ).then_inc(S["h_ready"], 1)
                        for x in range(2):
                            dve.wait_ge(S["scored"], t * 2 + x + 1)
                            nc.vector.tensor_reduce(ntop[x][:, :], PS[:, SCORES[x], 0:KEYS], AX.X, ALU.max, negate=True
                                                    ).then_inc(S["top_ready"], 1)
                        for x in range(2):
                            dve.wait_ge(S["turned"], t * 2 + x + 1)
                            for c in range(2):
                                cols = PS[:, TURNED[x], c * P:(c + 1) * P].rearrange("p (j i) -> p j i", i=32)
                                spread_rows(pT[x][:, c, :, :, :], cols[:, :, HALF * x:HALF * (x + 1)], x
                                            ).then_inc(S["pT_ready"], 1)
                            nc.vector.reciprocal(inv[x][:, :], total[x][:, :])
                            dve.drain()
                            i = slice(HALF * x, HALF * (x + 1))
                            of_row = batch_of_row.rearrange("p (j i) -> p j i", i=8)[:, :, i]
                            nc.vector.tensor_scalar(share[:, :, i], of_row, inv[x][:, :], None, ALU.mult)
                            dve.drain()
                            last = nc.vector.tensor_scalar(last_share[:, :, i], share[:, :, i],
                                                           probs[x][:, KEYS - 1:KEYS], None, ALU.mult)
                        last.then_inc(S["share_ready"], 1)
                        dve.wait_ge(S["summed"], t + 1)
                        nc.vector.tensor_copy(cx[:, :], PS[:, CTX, 0:D]).then_inc(S["cx_ready"], 1)

        with nc.Block() as block:
            @block.tensor
            def _(pe):
                flat = outs[:, :, :].rearrange("p b t -> p (b t)")
                for t in range(TILES):
                    last = nc.tensor.transpose(PS[:, 6 + t // 4, (t % 4) * P:(t % 4 + 1) * P],
                                               flat[:, t * P:(t + 1) * P], ident)
                last.then_inc(S["outs_turned"], 1)

            @block.vector
            def _(dve):
                dve.wait_ge(S["outs_turned"], 1)
                nc.vector.tensor_tensor(X[:, :, :], X[:, :, :], PS[:, 6:8, :].rearrange("p h (t d) -> p (h t) d", t=4),
                                        ALU.add)


STOP = 99


def perceiver(nc, dram, wcols, ccols, x_in, out):
    with ExitStack() as top:
        env = Env(nc, top)
        env.wcols, env.ccols = wcols, ccols
        env.W = env.sb(top, "weights", [P, dram["weights"].shape[1]])
        env.C = env.sb(top, "constants", [P, dram["constants"].shape[1]])
        env.PS = top.enter_context(nc.psum_tensor("banks", [P, 8, BANK], F32))
        X = env.sb(top, "X", [P, TILES, D])
        zT = env.sb(top, "zT", [P, TOKENS])
        ctxT = env.sb(top, "ctxT", [P, BATCH, KEYS])
        mask_in = env.sb(top, "mask_words", [P, KEYS, 2], mybir.dt.int32)
        mask = env.sb(top, "mask", [P, KEYS])
        x_loaded, rest_loaded, stored = (top.enter_context(nc.semaphore(n)) for n in ("x_loaded", "rest_loaded", "stored"))

        with nc.Block() as block:
            @block.sync
            def _(sp):
                sp.dma_start(X[:, :, :], x_in.rearrange("(t b) s d -> (b s) t d", b=PER_TILE)).then_inc(x_loaded, 16)
                sp.dma_start(env.C[:, :], dram["constants"]).then_inc(x_loaded, 16)
                sp.dma_start(env.W[:, :], dram["weights"]).then_inc(x_loaded, 16)
                for j in range(PER_TILE):
                    sp.dma_start(mask_in[32 * j:32 * j + 32, :, :].rearrange("p k w -> p (k w)"),
                                 dram["mask"].bitcast(mybir.dt.int32)).then_inc(rest_loaded, 16)
                sp.wait_ge(x_loaded, 3 * LOADED)

            @block.scalar
            def _(act):
                act.dma_start(ctxT[:, :, :], dram["ctxT"]).then_inc(rest_loaded, 16)
                act.wait_ge(rest_loaded, 5 * LOADED)

        with nc.Block() as block:
            @block.vector
            def _(dve):
                nc.vector.tensor_scalar(mask[:, :], mask_in[:, :, 0], -1.0, -MASKED, ALU.add, ALU.mult)

        def level0():
            norm_transpose(env, X, zT)
            with ExitStack() as s:
                qT = env.sb(s, "qT", [P, TOKENS])
                project(env, qT, env.w("L0x_q"), zT, env.w("L0x_qb"))
                cross_attention(env, "L0x_", X, ctxT, qT, 16, 16 ** -0.5, True)
            yield
            norm_transpose(env, X, zT)
            self_attention(env, "L0a_", X, zT, zT, 8 ** -0.5, causal=True)
            yield
            with ExitStack() as s:
                z = env.sb(s, "z", [P, TILES, D])
                norm_transpose(env, X, zT, keep=z)
                int8_matmul(env, X, z)
            yield

        def level1():
            norm_transpose(env, X, zT)
            with ExitStack() as s:
                qT = env.sb(s, "qT", [P, TOKENS])
                project(env, qT, env.w("L1x_q"), zT)
                cross_attention(env, "L1x_", X, ctxT, qT, 8, 8 ** -0.5, False)
            yield
            norm_transpose(env, X, zT)
            laplacian_attention(env, X, zT, dram["buckets"])
            yield
            mixture("L1f_", 16, 512, 2 * TOKENS // 16, ACT.Gelu, 8 ** -0.5, True)
            yield

        def mixture(layer, n, hidden, capacity, func, scale, causal):
            eps = float(np.finfo(np.float32).eps)
            with ExitStack() as s:
                Y = env.sb(s, "Y", [P, TILES, D])
                acc = env.sb(s, "acc", [P, TILES, D])
                gates = env.sb(s, "gates", [P, TILES, n])
                gatesT = env.sb(s, "gatesT", [n, TOKENS])
                norm_transpose(env, X, zT, keep=Y)
                norm_transpose(env, Y, zT, scale=env.w(layer + "ln1w"), shift=env.w(layer + "ln1b"))
                self_attention(env, layer, Y, zT, zT, scale, causal=causal)
                norm_transpose(env, Y, zT, scale=env.w(layer + "ln2w"), shift=env.w(layer + "ln2b"))
                route(env, gates, gatesT, zT, env.w(layer + "r"), n, capacity, eps, DROP)
                experts(env, acc, zT, gates, gatesT, dram[layer + "experts"], env.w(layer + "b2"), n, hidden, func)
                add_to(env, X, (Y, acc))

        def level2():
            norm_transpose(env, X, zT)
            context_lstm(env, X, zT, ctxT)
            yield
            with ExitStack() as s:
                latent = env.sb(s, "latentT", [P, TOKENS])
                norm_transpose(env, X, zT)
                project(env, latent, env.w("L2a_down"), zT)
                self_attention(env, "L2a_", X, zT, latent, 40 ** -0.5, causal=True, biases=False, qk_rope=True)
            yield
            mixture("L2f_", 8, 512, TOKENS // 4, ACT.Relu, 8 ** -0.5, False)
            yield

        def level3():
            norm_transpose(env, X, zT)
            with ExitStack() as s:
                qT = env.sb(s, "qT", [P, TOKENS])
                project(env, qT, env.w("L3x_q"), zT, env.w("L3x_qb"))
                single_cross_attention(env, "L3x_", X, ctxT, qT, mask, 128 ** -0.5)
            yield
            norm_transpose(env, X, zT)
            self_attention(env, "L3a_", X, zT, zT, 8 ** -0.5, causal=True, biases=False, rope="pair")
            yield
            with ExitStack() as s:
                acc = env.sb(s, "acc", [P, TILES, D])
                gates = env.sb(s, "gates", [P, TILES, 8])
                gatesT = env.sb(s, "gatesT", [8, TOKENS])
                norm_transpose(env, X, zT)
                route(env, gates, gatesT, zT, env.w("L3f_r"), 8, None, 1e-12, 1.0)
                experts(env, acc, zT, gates, gatesT, dram["L3f_experts"], env.w("L3f_b2"), 8, 256, ACT.Relu)
                add_to(env, X, (acc,))
            yield

        n = 0
        for level in (level0, level1, level2, level3):
            for _ in level():
                n += 1
                if n >= STOP:
                    break
            if n >= STOP:
                break

        with nc.Block() as block:
            @block.sync
            def _(sp):
                sp.dma_start(out.rearrange("(t b) s d -> (b s) t d", b=PER_TILE), X[:, :, :]).then_inc(stored, 16)
                sp.wait_ge(stored, 16)


def kernel(**inputs):
    import concourse.bacc as _bacc
    from concourse.bass_utils import run_bass_kernel_spmd as _run

    nc = _bacc.Bacc("TRN2", target_bir_lowering=False, num_devices=1)
    weights, tables = packed_weights(inputs), constants()

    def columns(parts):
        where, at = {}, 0
        for name, a in parts.items():
            where[name] = (at, at + a.shape[1])
            at += a.shape[1]
        return where, np.concatenate(list(parts.values()), axis=1)

    wcols, weights = columns(weights)
    ccols, tables = columns(tables)
    ctxT = np.asarray(inputs["ctx_1024"]).transpose(2, 0, 1)
    arrays = {
        "x": inputs["x"], "weights": weights, "constants": tables, "buckets": bucket_rows(),
        "mask": np.asarray(inputs["mask_SxS2_bk0"]).astype(np.int64),
        "ctxT": ctxT,
        "L1f_experts": packed_experts(inputs["L1_ffn_fc1_w"], inputs["L1_ffn_fc1_b"], inputs["L1_ffn_fc2_w"]),
        "L2f_experts": packed_experts(inputs["L2_ffn_w1"], inputs["L2_ffn_b1"], inputs["L2_ffn_w2"]),
        "L3f_experts": packed_experts(inputs["L3_ffn_W1"], inputs["L3_ffn_b1"], inputs["L3_ffn_W2"]),
    }
    arrays = {k: np.ascontiguousarray(v) for k, v in arrays.items()}
    dram = {k: nc.dram_tensor(k + "_dram", v.shape, mybir.dt.from_np(v.dtype), kind="ExternalInput").ap()
            for k, v in arrays.items()}
    out = nc.dram_tensor("out_dram", (BATCH, SEQ, D), F32, kind="ExternalOutput").ap()
    perceiver(nc, dram, wcols, ccols, dram["x"], out)
    r = _run(nc, [{k + "_dram": v for k, v in arrays.items()}], core_ids=[0])
    return r.results[0]["out_dram"]
```

```python
from contextlib import ExitStack

import numpy as np

import concourse.bass as bass
from concourse import mybir

F32 = mybir.dt.float32
BF16 = mybir.dt.bfloat16
ALU = mybir.AluOpType
ACT = mybir.ActivationFunctionType
AX = mybir.AxisListType

P = 128
D = 128
BATCH = 32
SEQ = 32
KEYS = 257
TOKENS = BATCH * SEQ
TILES = TOKENS // P
PER_TILE = P // SEQ
BANK = 512
GROUP = BANK // P
GROUPS = TILES // GROUP
KCH = 86
KSIZES = (86, 86, 85)
MASKED = -1e30
LN_EPS = 1e-5
QMAX = 127.0
ROUND = 12582912.0
DROP = 0.8

FIRST_SEM, LAST_SEM = 110, 250
MOST_SEMS = 40
FIRST = 1
WARM_UP = 2
LOADED = 16


def constants():
    p = np.arange(P)
    c = {}
    c["ident"] = np.eye(P)
    c["ones"] = np.ones((P, P))
    c["upto"] = (p[:, None] <= p[None, :])
    for dk in (8, 16):
        rows = 4 * dk
        c[f"spread{dk}"] = ((p[:, None] % rows) // dk == np.arange(4)[None, :])
        c[f"own_head{dk}"] = (p[:, None] // SEQ == np.arange(rows)[None, :] // dk)
    c["block_of"] = (p[:, None] // SEQ == np.arange(4)[None, :])
    c["fold"] = (p[:, None] % SEQ == np.arange(SEQ)[None, :])
    c["causal"] = np.where(np.arange(SEQ)[None, :] > p[:, None] % SEQ, MASKED, 0.0)
    same = p[:, None] // SEQ == p[None, :] // SEQ
    c["past"] = same & (p[:, None] <= p[None, :])
    c["first_wins"] = np.broadcast_to(16.0 - np.arange(16), (P, 16))
    c["slot_number"] = np.broadcast_to(np.arange(P) + 1.0, (P, P))
    c["minus_half"] = np.full((P, TILES), -0.5)
    c["own_row"] = np.broadcast_to(np.eye(8).reshape(1, 64), (P, 64))
    c["batch_of_row"] = (p[:, None] == (32 * (np.arange(BATCH) // 8) + np.arange(BATCH) % 8)[None, :])
    t = np.arange(SEQ, dtype=np.float32)
    inv = (1.0 / 10000.0 ** (np.arange(0, 32, 2, dtype=np.float32) / 32)).astype(np.float32)
    ang = (inv[(p % 32) % 16][:, None] * t[None, :]).astype(np.float32)
    c["cos_half"] = np.cos(ang)
    c["sin_half"] = np.sin(ang) * np.where((p % 32) < 16, -1.0, 1.0)[:, None]
    inv = (10000.0 ** (-np.arange(0, 8, 2, dtype=np.float32) / 8)).astype(np.float32)
    ang = (inv[(p % 8) // 2][:, None] * t[None, :]).astype(np.float32)
    c["cos_pair"] = np.cos(ang)
    c["sin_pair"] = np.sin(ang) * np.where(p % 2 == 0, -1.0, 1.0)[:, None]
    return {k: np.ascontiguousarray(v, dtype=np.float32) for k, v in c.items()}


def bucket_rows():
    n = np.maximum(np.arange(SEQ)[:, None] - np.arange(SEQ)[None, :], 0)
    nf = np.maximum(n, 1).astype(np.float32)
    large = 16 + (np.log(nf / 16) / np.log(8.0) * 16).astype(np.int32)
    b = np.where(n < 16, n, np.minimum(large, 31))
    hot = b[None] == np.arange(32)[:, None, None]
    return np.ascontiguousarray(np.tile(hot, (1, 1, PER_TILE)).reshape(32, SEQ * P), dtype=np.float32)


HALF_SWAP = np.concatenate([np.arange(16, 32), np.arange(16)])
PAIR_SWAP = np.arange(P) ^ 1


def packed_weights(w):
    def mat(a):
        return np.asarray(a)

    def col(a):
        return mat(a).reshape(-1, P).T

    def row(a):
        return np.broadcast_to(mat(a).reshape(1, -1), (P, mat(a).size))

    c = {}
    kv = mat(w["L0_xattn_Wkv_w"])
    kvb = mat(w["L0_xattn_Wkv_b"])
    c["L0x_q"] = mat(w["L0_xattn_Wq_w"])
    c["L0x_k"] = kv[:, :, :16].transpose(1, 0, 2).reshape(D, D)
    c["L0x_v"] = kv[:, :, 16:].transpose(1, 0, 2).reshape(D, D)
    c["L0x_o"] = mat(w["L0_xattn_Wo_w"])
    c["L0x_qb"] = col(w["L0_xattn_Wq_b"])
    c["L0x_kb"] = kvb[:, :16].reshape(D, 1)
    c["L0x_vbc"] = kvb[:, 16:].reshape(D, 1)
    c["L0x_ob"] = row(w["L0_xattn_Wo_b"])
    qkv, qkvb = mat(w["L0_attn_qkv_w"]), mat(w["L0_attn_qkv_b"])
    for i, n in enumerate("qkv"):
        c["L0a_" + n] = qkv[:, i * D:(i + 1) * D]
    c["L0a_qb"], c["L0a_kb"], c["L0a_vb"] = col(qkvb[:D]), col(qkvb[D:2 * D]), row(qkvb[2 * D:])
    c["L0a_o"], c["L0a_ob"] = mat(w["L0_attn_out_w"]), row(w["L0_attn_out_b"])
    c["L0f_T"] = mat(w["L0_ffn_rhs"]).T
    c["L1x_q"] = mat(w["L1_xattn_Wq"])
    c["L1x_k"], c["L1x_v"] = mat(w["L1_xattn_Wkv"])[:, :D], mat(w["L1_xattn_Wkv"])[:, D:]
    c["L1a_qk"], c["L1a_qkb"] = mat(w["L1_attn_Wqk"]), col(w["L1_attn_bqk"])
    c["L1a_gamma"], c["L1a_beta"] = mat(w["L1_attn_gamma"]).T, mat(w["L1_attn_beta"]).T
    c["L1a_v"], c["L1a_vb"] = mat(w["L1_attn_Wv"]), row(w["L1_attn_bv"])
    c["L1a_rel"] = np.concatenate([mat(w["L1_attn_rel_emb"]), np.zeros((P - 32, 1), np.float32)])
    for n in "qkvo":
        c["L1f_" + n] = mat(w[f"L1_ffn_{n}_w"])
        c[f"L1f_{n}b"] = (col if n in "qk" else row)(w[f"L1_ffn_{n}_b"])
        c["L2f_" + n] = mat(w[f"L2_ffn_w{n}"])
        c[f"L2f_{n}b"] = (col if n in "qk" else row)(w[f"L2_ffn_b{n}"])
    for i in "12":
        c[f"L1f_ln{i}w"], c[f"L1f_ln{i}b"] = col(w[f"L1_ffn_ln{i}_w"]), col(w[f"L1_ffn_ln{i}_b"])
        c[f"L2f_ln{i}w"], c[f"L2f_ln{i}b"] = col(w[f"L2_ffn_ln{i}_g"]), col(w[f"L2_ffn_ln{i}_b"])
    c["L1f_r"], c["L2f_r"], c["L3f_r"] = mat(w["L1_ffn_router_w"]), mat(w["L2_ffn_wr"]), mat(w["L3_ffn_gate"])
    for n, a in (("L1f_b2", "L1_ffn_fc2_b"), ("L2f_b2", "L2_ffn_b2"), ("L3f_b2", "L3_ffn_b2")):
        b2 = mat(w[a])
        c[n] = np.concatenate([b2, np.zeros((P - b2.shape[0], D), np.float32)])
    order = np.concatenate([np.arange(0, 256), np.arange(384, 512), np.arange(256, 384)])
    c["L2x_ihx"] = mat(w["L2_xattn_W_ih"])[order, :D].T
    c["L2x_iha"] = mat(w["L2_xattn_W_ih"])[order, D:].T
    c["L2x_hh"] = mat(w["L2_xattn_W_hh"])[order].T
    c["L2x_bih"], c["L2x_bhh"] = col(mat(w["L2_xattn_b_ih"])[order]), col(mat(w["L2_xattn_b_hh"])[order])
    c["L2x_q"] = mat(w["L2_xattn_Wq"])
    c["L2x_oc"], c["L2x_oh"] = mat(w["L2_xattn_Wout"])[:, :D].T, mat(w["L2_xattn_Wout"])[:, D:].T
    c["L2x_ob"] = col(w["L2_xattn_b_out"])
    c["L2a_down"], c["L2a_k"], c["L2a_v"] = (mat(w["L2_attn_" + n]) for n in ("W_kv_down", "W_k_up", "W_v_up"))
    c["L2a_q"], c["L2a_o"] = mat(w["L2_attn_W_q"]), mat(w["L2_attn_W_o"])
    for n, a in (("qr", "L2_attn_W_q_rope"), ("kr", "L2_attn_W_k_rope")):
        c["L2a_" + n] = np.tile(mat(w[a]), (1, 4))
        c[f"L2a_{n}s"] = np.tile(mat(w[a])[:, HALF_SWAP], (1, 4))
    for n in "qkv":
        c["L3x_" + ("kT" if n == "k" else n)] = mat(w[f"L3_xattn_W{n}"]).T if n == "k" else mat(w[f"L3_xattn_W{n}"])
        c[f"L3x_{n}b"] = (row if n == "v" else col)(w[f"L3_xattn_b{n}"])
        c["L3a_" + n] = mat(w[f"L3_attn_W{n}"]).T
    for n in "qk":
        c[f"L3a_{n}s"] = mat(w[f"L3_attn_W{n}"]).T[:, PAIR_SWAP]
    c["L3a_o"] = mat(w["L3_attn_Wo"]).T
    return c


def packed_experts(w1, b1, w2):
    w1, b1, w2 = np.asarray(w1), np.asarray(b1), np.asarray(w2)
    e, _, f = w1.shape
    n = f // P
    w2 = w2.reshape(e, n, P, D).transpose(0, 2, 1, 3).reshape(e, P, n * D)
    return np.concatenate([w1, w2, b1.reshape(e, n, P).transpose(0, 2, 1)], axis=2)


def chunked_rows(ctx):
    rows = np.zeros((BATCH, 3 * KCH, D), np.float32)
    rows[:, :KEYS] = ctx
    return rows.reshape(BATCH, 3, KCH, D).transpose(2, 0, 1, 3)


class Env:

    def __init__(self, nc, stack):
        self.nc, self.stack, self.n, self.next_sem = nc, stack, 0, FIRST_SEM

    def sb(self, stack, name, shape, dt=F32):
        self.n += 1
        return stack.enter_context(self.nc.sbuf_tensor(f"{name}_{self.n}", shape, dt))

    def sem(self, stack, name):
        self.n += 1
        self.next_sem += 1
        return stack.enter_context(self.nc.semaphore(f"{name}_{self.n}", num=self.next_sem - 1))

    def stage(self):
        if self.next_sem > LAST_SEM - MOST_SEMS:
            with self.nc.Block() as block:
                @block.sync
                def _(sp):
                    sp.sem_clear(range(FIRST_SEM, LAST_SEM))
            self.next_sem = FIRST_SEM

    def w(self, name):
        a, b = self.wcols[name]
        return self.W[:, a:b]

    def c(self, name):
        a, b = self.ccols[name]
        return self.C[:, a:b]

    def bank(self, b, n=BANK):
        return self.PS[:, b, 0:n]


def head_start(env, semaphores):
    with env.nc.Block() as block:
        @block.sync
        def _(sp):
            for sem in semaphores:
                sp.sem_inc(sem, FIRST)


def keep_busy(env, n, bank=7):
    for _ in range(n):
        env.nc.tensor.matmul(env.bank(bank), env.c("ident"), env.C[:, 0:BANK], start=True, stop=True)


def over(ap, axis, shape):
    return ap.unsqueeze(axis).broadcast_to(shape)


def norm_transpose(env, src, turned, keep=None, scale=None, shift=None, onward=None):
    nc = env.nc
    env.stage()
    with ExitStack() as s:
        z = keep if keep is not None else env.sb(s, "normed", [P, TILES, D])
        stats = env.sb(s, "stats", [P, TILES, 6])
        mv = env.sb(s, "mean_var", [P, TILES, 2])
        var_eps = env.sb(s, "var_eps", [P, TILES])
        rstd = env.sb(s, "rstd", [P, TILES])
        have_var = env.sem(s, "have_var")
        have_rstd = env.sem(s, "have_rstd")
        tile_normed = env.sem(s, "tile_normed")
        tile_turned = env.sem(s, "tile_turned")
        half_turned = env.sem(s, "half_turned")
        half_projected = env.sem(s, "half_projected")
        halves = (range(TILES // 2), range(TILES // 2, TILES))
        with nc.Block() as block:
            @block.vector
            def _(dve):
                for h in halves:
                    for t in h:
                        nc.vector.bn_stats(stats[:, t, :], src[:, t, :])
                    dve.drain()
                    for t in h:
                        nc.vector.bn_aggr(mv[:, t, :], stats[:, t, :])
                    dve.drain()
                    r = slice(h[0], h[-1] + 1)
                    nc.vector.tensor_scalar(var_eps[:, r], mv[:, r, 1], LN_EPS, None, ALU.add).then_inc(have_var, 1)
                for n, h in enumerate(halves):
                    dve.wait_ge(have_rstd, n + 1)
                    for t in h:
                        nc.vector.tensor_scalar(z[:, t, :], src[:, t, :], mv[:, t, 0:1], rstd[:, t:t + 1],
                                                ALU.subtract, ALU.mult).then_inc(tile_normed, 1)

            @block.gpsimd
            def _(pool):
                for n, h in enumerate(halves):
                    r = slice(h[0], h[-1] + 1)
                    pool.wait_ge(have_var, n + 1)
                    nc.gpsimd.tensor_tensor(rstd[:, r], var_eps[:, r], env.c("minus_half")[:, r],
                                            ALU.pow).then_inc(have_rstd, 1)

            if turned is None:
                return

            @block.tensor
            def _(pe):
                keep_busy(env, WARM_UP)
                for t in range(TILES):
                    pe.wait_ge(tile_normed, t + 1)
                    nc.tensor.transpose(env.PS[:, t // 4, (t % 4) * P:(t % 4 + 1) * P], z[:, t, :],
                                        env.c("ident")).then_inc(tile_turned, 1)
                if onward:
                    for h in range(2):
                        pe.wait_ge(half_turned, h + 1)
                        nc.tensor.matmul(env.bank(2 + h), onward[1], turned[:, h * BANK:(h + 1) * BANK],
                                         start=True, stop=True).then_inc(half_projected, 1)

            @block.scalar
            def _(act):
                for h in range(2):
                    act.wait_ge(tile_turned, 4 * (h + 1))
                    if scale is None:
                        nc.scalar.copy(turned[:, h * BANK:(h + 1) * BANK], env.bank(h)).then_inc(half_turned, 1)
                    else:
                        nc.scalar.activation(turned[:, h * BANK:(h + 1) * BANK], env.bank(h), ACT.Identity,
                                             bias=shift, scale=scale).then_inc(half_turned, 1)
                if onward:
                    out, _, bias = onward
                    for h in range(2):
                        act.wait_ge(half_projected, h + 1)
                        nc.scalar.activation(out[:, h * BANK:(h + 1) * BANK], env.bank(2 + h), ACT.Identity,
                                             bias=0.0 if bias is None else bias)


def self_attention(env, layer, R, qsrc, kvsrc, scale, causal=False, biases=True, rope=None, qk_rope=False):
    nc = env.nc
    env.stage()
    nb = GROUP * PER_TILE
    early = not (rope or qk_rope)
    V0 = 6 if early else 4
    w = lambda n: env.w(layer + n)
    spread, block_of, ident = env.c("spread8"), env.c("block_of"), env.c("ident")
    PS = env.PS
    with ExitStack() as s:
        two = range(GROUPS)
        q = [env.sb(s, f"q{g}", [P, BANK]) for g in two]
        kbd = [env.sb(s, f"k_spread{g}", [P, nb, 4, SEQ]) for g in two]
        kb4 = env.sb(s, "k_bias_spread", [P, 4])
        v = [env.sb(s, f"v_own{g}", [P, GROUP, PER_TILE, 4, 4, 8]) for g in two]
        sc = [env.sb(s, f"scores{g}", [P, 4, GROUP, 4, SEQ]) for g in two]
        probsT = [env.sb(s, f"probsT{g}", [P, 4, GROUP, P]) for g in two]
        top = [env.sb(s, f"top{g}", [P, 4, GROUP, 4]) for g in two]
        total = [env.sb(s, f"total{g}", [P, 4, GROUP, 4]) for g in two]
        att = [env.sb(s, f"att{g}", [P, GROUP, D]) for g in two]
        attT = [env.sb(s, f"attT{g}", [P, BANK]) for g in two]
        if rope or qk_rope:
            rot = env.sb(s, "rot", [P, nb, SEQ])
            rot2 = env.sb(s, "rot2", [P, nb, SEQ])
            krot = env.sb(s, "k_rotated", [P, nb, SEQ])
        if qk_rope:
            qr = [env.sb(s, f"q_rope{g}", [P, BANK]) for g in two]
            kr = [env.sb(s, f"k_rope{g}", [P, nb, SEQ]) for g in two]
            shared = [env.sb(s, f"shared_scores{g}", [P, GROUP, SEQ]) for g in two]
        names = ("kb_spread", "projected", "q_ready", "k_rotated", "k_ready", "v_projected", "v_ready", "scored",
                 "shifted", "exped", "turned", "probsT_ready", "weighed", "att_ready", "att_turned", "attT_ready",
                 "out_projected", "rope_projected", "rope_ready", "rope_scored", "shared_ready")
        S = {n: env.sem(s, n) for n in names}

        def banked(b):
            return PS[:, b, :].rearrange("p (b q) -> p b q", q=SEQ)

        with nc.Block() as block:
            @block.tensor
            def _(pe):
                def project_group(g):
                    cols = slice(g * BANK, (g + 1) * BANK)
                    nc.tensor.matmul(PS[:, 4 * g, :], w("q"), qsrc[:, cols], start=True, stop=True)
                    last = nc.tensor.matmul(PS[:, 4 * g + 1, :], w("k"), kvsrc[:, cols], start=True, stop=True)
                    if rope:
                        nc.tensor.matmul(PS[:, 4 * g + 2, :], w("qs"), qsrc[:, cols], start=True, stop=True)
                        last = nc.tensor.matmul(PS[:, 4 * g + 3, :], w("ks"), kvsrc[:, cols], start=True, stop=True)
                    last.then_inc(S["projected"], 1)

                def rope_group(g):
                    cols = slice(g * BANK, (g + 1) * BANK)
                    pe.wait_ge(S["q_ready"], g + 1)
                    pe.wait_ge(S["k_ready"], g + 1)
                    for i, (name, src) in enumerate((("qr", qsrc), ("qrs", qsrc), ("kr", kvsrc), ("krs", kvsrc))):
                        last = nc.tensor.matmul(PS[:, 4 * g + i, :], w(name), src[:, cols], start=True, stop=True)
                    last.then_inc(S["rope_projected"], 1)
                    pe.wait_ge(S["rope_ready"], g + 1)
                    r = slice(0, 32)
                    for t in range(GROUP):
                        for b in range(PER_TILE):
                            n = t * PER_TILE + b
                            last = nc.tensor.matmul(PS[32 * b:32 * b + 32, 4 * g, t * SEQ:(t + 1) * SEQ],
                                                    qr[g][r, n * SEQ:(n + 1) * SEQ], kr[g][r, n, :],
                                                    start=True, stop=True)
                    last.then_inc(S["rope_scored"], 1)

                def values(g):
                    mine = w("v").rearrange("p (c h e) -> p h c e", c=4, h=4)
                    for n in range(nb):
                        at = g * BANK + n * SEQ
                        for h in range(4):
                            last = nc.tensor.matmul(PS[32 * h:32 * h + 32, V0 + g, n * 32:(n + 1) * 32],
                                                    kvsrc[:, at:at + SEQ], mine[:, h, :, :], start=True, stop=True)
                    last.then_inc(S["v_projected"], 1)

                def scores(g):
                    pe.wait_ge(S["q_ready"], g + 1)
                    pe.wait_ge(S["k_ready"], g + 1)
                    if qk_rope:
                        pe.wait_ge(S["shared_ready"], g + 1)
                    for t in range(GROUP):
                        for c in range(4):
                            r = slice(32 * c, 32 * c + 32)
                            for b in range(PER_TILE):
                                n = t * PER_TILE + b
                                o = PS[32 * b:32 * b + 32, 4 * g + c, t * P:(t + 1) * P]
                                last = nc.tensor.matmul(o, q[g][r, n * SEQ:(n + 1) * SEQ], kbd[g][r, n, :, :],
                                                        start=True, stop=True)
                    last.then_inc(S["scored"], 1)

                def turn(g):
                    pe.wait_ge(S["exped"], g + 1)
                    for c in range(4):
                        for t in range(GROUP):
                            last = nc.tensor.transpose(PS[:, 4 * g + c, t * P:(t + 1) * P], sc[g][:, c, t, :, :],
                                                       ident)
                        last.then_inc(S["turned"], 1)

                def weigh(g):
                    pe.wait_ge(S["probsT_ready"], 2 * (g + 1))
                    for t in range(GROUP):
                        for c in range(4):
                            for b in range(PER_TILE):
                                last = nc.tensor.matmul(PS[32 * b:32 * b + 32, 4 * g, t * P + 32 * c:t * P + 32 * c + 32],
                                                        probsT[g][:, c, t, 32 * b:32 * b + 32], v[g][:, t, b, c, :, :],
                                                        start=True, stop=True)
                    last.then_inc(S["weighed"], 1)

                def finish(g):
                    pe.wait_ge(S["att_ready"], g + 1)
                    for t in range(GROUP):
                        last = nc.tensor.transpose(PS[:, 4 * g + 1, t * P:(t + 1) * P], att[g][:, t, :], ident)
                    last.then_inc(S["att_turned"], 1)
                    pe.wait_ge(S["attT_ready"], g + 1)
                    for t in range(GROUP):
                        last = nc.tensor.matmul(PS[:, 4 * g + 2, t * P:(t + 1) * P], attT[g][:, t * P:(t + 1) * P],
                                                w("o"), start=True, stop=True)
                    last.then_inc(S["out_projected"], 1)

                project_group(0)
                values(0)
                values(1)
                if qk_rope:
                    rope_group(0)
                if early:
                    project_group(1)
                scores(0)
                pe.wait_ge(S["v_ready"], 2)
                if not early:
                    project_group(1)
                if qk_rope:
                    rope_group(1)
                scores(1)
                turn(0)
                weigh(0)
                turn(1)
                finish(0)
                weigh(1)
                finish(1)

            @block.scalar
            def _(act):
                def keys(g):
                    if rope:
                        act.wait_ge(S["k_rotated"], g + 1)
                    else:
                        act.wait_ge(S["projected"], g + 1)
                    for j in range(4):
                        last = nc.scalar.activation(kbd[g][:, :, j, :], krot[:, :, :] if rope else banked(4 * g + 1),
                                                    ACT.Identity, scale=spread[:, j:j + 1],
                                                    bias=kb4[:, j:j + 1] if biases else 0.0)
                    last.then_inc(S["k_ready"], 1)

                def values(g):
                    act.wait_ge(S["v_projected"], g + 1)
                    for j in range(4):
                        last = nc.scalar.activation(v[g][:, :, :, :, j, :].rearrange("p t b c e -> p (t b c) e"),
                                                    PS[:, V0 + g, :].rearrange("p (n e) -> p n e", e=8),
                                                    ACT.Copy, scale=block_of[:, j:j + 1])
                    last.then_inc(S["v_ready"], 1)

                def exp(g):
                    act.wait_ge(S["shifted"], g + 1)
                    nc.scalar.activation(sc[g][:, :, :, :, :], sc[g][:, :, :, :, :], ACT.Exp, scale=scale
                                         ).then_inc(S["exped"], 1)

                def turned(g):
                    act.wait_ge(S["turned"], 4 * g + 2)
                    nc.scalar.copy(probsT[g][:, 0:2, :, :],
                                   PS[:, 4 * g:4 * g + 2, :].rearrange("p c (t r) -> p c t r", t=GROUP)
                                   ).then_inc(S["probsT_ready"], 1)
                    act.wait_ge(S["turned"], 4 * g + 4)
                    nc.scalar.copy(probsT[g][:, 2:4, :, :],
                                   PS[:, 4 * g + 2:4 * g + 4, :].rearrange("p c (t r) -> p c t r", t=GROUP)
                                   ).then_inc(S["probsT_ready"], 1)

                def finish(g):
                    act.wait_ge(S["att_turned"], g + 1)
                    nc.scalar.copy(attT[g][:, :], PS[:, 4 * g + 1, :]).then_inc(S["attT_ready"], 1)

                if biases:
                    act.wait_ge(S["kb_spread"], 1)
                keys(0)
                values(0)
                values(1)
                keys(1)
                exp(0)
                turned(0)
                exp(1)
                turned(1)
                finish(0)
                finish(1)

            @block.vector
            def _(dve):
                def rotate(out, plain, swapped, cos, sin):
                    nc.vector.tensor_tensor(rot[:, :, :], banked(plain), over(env.c(cos), 1, [P, nb, SEQ]), ALU.mult)
                    nc.vector.tensor_tensor(rot2[:, :, :], banked(swapped), over(env.c(sin), 1, [P, nb, SEQ]),
                                            ALU.mult)
                    dve.drain()
                    return nc.vector.tensor_tensor(out, rot[:, :, :], rot2[:, :, :], ALU.add)

                def queries(g):
                    dve.wait_ge(S["projected"], g + 1)
                    if rope:
                        if g > 0:
                            dve.wait_ge(S["k_ready"], g)
                        rotate(krot[:, :, :], 4 * g + 1, 4 * g + 3, "cos_pair", "sin_pair").then_inc(S["k_rotated"], 1)
                        dve.drain()
                        rotate(q[g][:, :].rearrange("p (b q) -> p b q", q=SEQ), 4 * g, 4 * g + 2,
                               "cos_pair", "sin_pair").then_inc(S["q_ready"], 1)
                    elif biases:
                        nc.vector.tensor_scalar(q[g][:, :], PS[:, 4 * g, :], w("qb"), None, ALU.add
                                                ).then_inc(S["q_ready"], 1)
                    else:
                        nc.vector.tensor_copy(q[g][:, :], PS[:, 4 * g, :]).then_inc(S["q_ready"], 1)
                    if qk_rope:
                        dve.wait_ge(S["rope_projected"], g + 1)
                        rotate(qr[g][:, :].rearrange("p (b q) -> p b q", q=SEQ), 4 * g, 4 * g + 1,
                               "cos_half", "sin_half")
                        dve.drain()
                        rotate(kr[g][:, :, :], 4 * g + 2, 4 * g + 3, "cos_half", "sin_half"
                               ).then_inc(S["rope_ready"], 1)
                        dve.wait_ge(S["rope_scored"], g + 1)
                        nc.vector.tensor_tensor(shared[g][:, :, :],
                                                PS[:, 4 * g, 0:GROUP * SEQ].rearrange("p (t k) -> p t k", k=SEQ),
                                                over(env.c("causal"), 1, [P, GROUP, SEQ]), ALU.add
                                                ).then_inc(S["shared_ready"], 1)

                def softmax(g):
                    dve.wait_ge(S["scored"], g + 1)
                    raw = PS[:, 4 * g:4 * g + 4, :].rearrange("p c (t h k) -> p (c t) h k", h=4, k=SEQ)
                    mine = sc[g][:, :, :, :, :].rearrange("p c t h k -> p (c t) h k")
                    if qk_rope:
                        for t in range(GROUP):
                            nc.vector.tensor_tensor(sc[g][:, :, t, :, :],
                                                    PS[:, 4 * g:4 * g + 4, t * P:(t + 1) * P].rearrange(
                                                        "p c (h k) -> p c h k", k=SEQ),
                                                    shared[g][:, t, :].unsqueeze(1).unsqueeze(1)
                                                    .broadcast_to([P, 4, 4, SEQ]), ALU.add)
                        dve.drain()
                        raw = mine
                    elif causal:
                        nc.vector.tensor_tensor(sc[g][:, :, :, :, :].rearrange("p c t h k -> p (c t h) k"),
                                                PS[:, 4 * g:4 * g + 4, :].rearrange("p c (n k) -> p (c n) k", k=SEQ),
                                                over(env.c("causal"), 1, [P, 16 * GROUP, SEQ]), ALU.add)
                        dve.drain()
                        raw = mine
                    tops = top[g][:, :, :, :].rearrange("p c t h -> p (c t) h")
                    nc.vector.tensor_reduce(tops, raw, AX.X, ALU.max)
                    dve.drain()
                    nc.vector.tensor_tensor(mine, raw, over(tops, 3, [P, 4 * GROUP, 4, SEQ]), ALU.subtract
                                            ).then_inc(S["shifted"], 1)

                def sums(g):
                    dve.wait_ge(S["exped"], g + 1)
                    nc.vector.tensor_reduce(total[g][:, :, :, :], sc[g][:, :, :, :, :], AX.X, ALU.add)
                    dve.drain()
                    nc.vector.reciprocal(total[g][:, :, :, :], total[g][:, :, :, :])

                def normalise(g):
                    dve.drain()
                    dve.wait_ge(S["weighed"], g + 1)
                    for c in range(4):
                        last = nc.vector.tensor_tensor(
                            att[g][:, :, 32 * c:32 * c + 32].rearrange("p t (h e) -> p t h e", h=4),
                            PS[:, 4 * g, :].rearrange("p (t c h e) -> p t c h e", t=GROUP, c=4, h=4)[:, :, c, :, :],
                            over(total[g][:, c, :, :], 3, [P, GROUP, 4, 8]), ALU.mult)
                    if biases:
                        dve.drain()
                        last = nc.vector.tensor_tensor(att[g][:, :, :], att[g][:, :, :],
                                                       over(w("vb"), 1, [P, GROUP, D]), ALU.add)
                    last.then_inc(S["att_ready"], 1)

                def add(g):
                    dve.wait_ge(S["out_projected"], g + 1)
                    here = R[:, g * GROUP:(g + 1) * GROUP, :]
                    nc.vector.tensor_tensor(here, here, PS[:, 4 * g + 2, :].rearrange("p (t d) -> p t d", t=GROUP),
                                            ALU.add)
                    if biases:
                        dve.drain()
                        nc.vector.tensor_tensor(here, here, over(w("ob"), 1, [P, GROUP, D]), ALU.add)

                if biases:
                    nc.vector.tensor_scalar(kb4[:, :], spread, w("kb"), None, ALU.mult).then_inc(S["kb_spread"], 1)
                queries(0)
                if early:
                    queries(1)
                softmax(0)
                if not early:
                    queries(1)
                if early:
                    softmax(1)
                    sums(0)
                else:
                    sums(0)
                    softmax(1)
                normalise(0)
                sums(1)
                add(0)
                normalise(1)
                add(1)


def cross_attention(env, layer, X, ctxT, qT, dk, scale, biases):
    nc = env.nc
    env.stage()
    rows = 4 * dk
    n_c = D // rows
    per_batch = n_c // 2
    units = PER_TILE * per_batch
    w = lambda n: env.w(layer + n)
    spread, own, fold, ident = env.c(f"spread{dk}"), env.c(f"own_head{dk}"), env.c("fold"), env.c("ident")
    PS = env.PS
    KT, V, PT, REST = 6, 7, 4, 5
    OT_COLS, RT_COLS, OUT_COLS = slice(256, 384), slice(384, 416), slice(KEYS, KEYS + D)
    with ExitStack() as s:
        one = env.sb(s, "ctx_batch", [P, KEYS])
        kT = env.sb(s, "kT", [P, KEYS])
        v = [env.sb(s, f"v{i}", [KCH, 3, D]) for i in range(PER_TILE)]
        qbd = [env.sb(s, f"q_spread{i}", [P, 4, SEQ]) for i in range(2)]
        probs = [env.sb(s, f"probs{i}", [P, 2, KEYS]) for i in range(2)]
        probsT = env.sb(s, "probsT", [KCH, 3, 2 * P])
        ntop = [env.sb(s, f"minus_top{i}", [P, 2]) for i in range(2)]
        total = [env.sb(s, f"total{i}", [P, n_c]) for i in range(PER_TILE)]
        inv = env.sb(s, "inv", [P, n_c])
        scaled = env.sb(s, "scaled_spread", [P, 4])
        inv_own = env.sb(s, "inv_own", [P, n_c, rows])
        oh = env.sb(s, "own_out", [P, 4, SEQ])
        o = env.sb(s, "unscaled", [P, SEQ])
        attT = env.sb(s, "attT", [P, P])
        names = ("ctx_copied", "kv_projected", "kT_ready", "q_ready", "v_ready", "scored", "top_ready", "exped",
                 "turned", "probsT_ready", "weighed", "inv_made", "inv_ready", "inv_turned", "batch_read", "attT_ready",
                 "out_projected", "tile_added")
        S = {n: env.sem(s, n) for n in names}
        head_start(env, [S[n] for n in ("kv_projected", "tile_added", "batch_read")])

        def unit(t, i):
            return t * units + i, t * PER_TILE + i // per_batch, i // per_batch % PER_TILE, i % per_batch

        with nc.Block() as block:
            @block.vector
            def _(dve):
                nc.vector.tensor_scalar(scaled[:, :], spread, scale, None, ALU.mult)

        with nc.Block() as block:
            @block.gpsimd
            def _(pool):
                def batch(k, y):
                    pool.wait_ge(S["kv_projected"], FIRST + k)
                    nc.gpsimd.tensor_copy(one[:, :], ctxT[:, k, :]).then_inc(S["ctx_copied"], 1)
                    nc.gpsimd.tensor_tensor(qbd[y][:, :, :], over(qT[:, bass.ds(k * SEQ, SEQ)], 1, [P, 4, SEQ]),
                                            over(scaled[:, :], 2, [P, 4, SEQ]), ALU.mult).then_inc(S["q_ready"], 1)

                def inverse(k):
                    pool.wait_ge(S["inv_made"], k + 1)
                    nc.gpsimd.tensor_tensor(inv_own[:, :, :], over(inv[:, :], 2, [P, n_c, rows]),
                                            over(own, 1, [P, n_c, rows]), ALU.mult).then_inc(S["inv_ready"], 1)

                batch(0, 0)
                batch(1, 1)
                with pool.Fori(0, BATCH // 2 - 1) as pair:
                    for y in range(2):
                        batch(pair * 2 + y + 2, y)
                        inverse(pair * 2 + y)
                inverse(BATCH - 2)
                inverse(BATCH - 1)

            @block.tensor
            def _(pe):
                def keys_values(k):
                    pe.wait_ge(S["ctx_copied"], k + 1)
                    nc.tensor.matmul(PS[:, KT, 0:KEYS], w("k"), one[:, :], start=True, stop=True)
                    for i in range(3):
                        last = nc.tensor.matmul(PS[0:KSIZES[i], V, i * P:(i + 1) * P],
                                                one[:, i * KCH:i * KCH + KSIZES[i]], w("v"), start=True, stop=True)
                    last.then_inc(S["kv_projected"], 1)

                def scores(k, j, u, parity):
                    if u == 0:
                        pe.wait_ge(S["kT_ready"], k + 1)
                        pe.wait_ge(S["q_ready"], k + 1)
                    for c in range(2):
                        r = slice(rows * (2 * u + c), rows * (2 * u + c + 1))
                        last = nc.tensor.matmul(PS[:, 2 * parity + c, 0:KEYS], qbd[j % 2][r, :, :], kT[r, :],
                                                start=True, stop=True)
                    last.then_inc(S["scored"], 1)

                def turn(n, k, u, parity):
                    pe.wait_ge(S["exped"], n * 2 + 2)
                    if u == 0:
                        pe.wait_ge(S["batch_read"], FIRST + k)
                    for i in range(3):
                        for c in range(2):
                            o_cols = (i % 2) * 2 * P + c * P
                            last = nc.tensor.transpose(PS[0:KSIZES[i], PT + i // 2, o_cols:o_cols + P],
                                                       probs[parity][:, c, i * KCH:i * KCH + KSIZES[i]], ident)
                        if i > 0:
                            last.then_inc(S["turned"], 1)

                def weigh(n, k, j, u):
                    if u == 0:
                        pe.wait_ge(S["v_ready"], k * 2 + 2)
                    pe.wait_ge(S["probsT_ready"], n * 2 + 2)
                    for i in range(3):
                        for c in range(2):
                            r = slice(rows * (2 * u + c), rows * (2 * u + c + 1))
                            last = nc.tensor.matmul(PS[r, REST, OT_COLS], v[j][0:KSIZES[i], i, r],
                                                    probsT[0:KSIZES[i], i, c * P:(c + 1) * P],
                                                    start=i == 0, stop=i == 2)
                    last.then_inc(S["weighed"], 1)
                    if u == per_batch - 1:
                        pe.wait_ge(S["inv_ready"], k + 1)
                        for c in range(n_c):
                            last = nc.tensor.matmul(PS[rows * c:rows * (c + 1), REST, RT_COLS], inv_own[:, c, :], fold,
                                                    start=True, stop=True)
                        last.then_inc(S["inv_turned"], 1)

                def step(t, i, ahead=True):
                    n, k, j, u = unit(t, i)
                    if ahead:
                        _, nk, nj, nu = unit(t, i + 2)
                        if nu == 0:
                            pe.wait_ge(S["v_ready"], nk * 2)
                            if i == per_batch:
                                pe.wait_ge(S["tile_added"], FIRST + t)
                            keys_values(nk)
                    turn(n, k, u, i % 2)
                    if ahead:
                        scores(nk, nj, nu, i % 2)
                    if i == units:
                        finish(t)
                    weigh(n, k, j, u)

                def finish(t):
                    pe.wait_ge(S["attT_ready"], t + 1)
                    if biases:
                        out = nc.tensor.matmul(PS[:, KT, OUT_COLS], attT[:, :], w("o"), start=True, stop=True)
                    else:
                        out = nc.tensor.transpose(PS[:, KT, OUT_COLS], attT[:, :], ident)
                    out.then_inc(S["out_projected"], 1)

                for i in range(2):
                    _, k, j, u = unit(0, i)
                    if u == 0:
                        if k > 0:
                            pe.wait_ge(S["v_ready"], k * 2)
                        keys_values(k)
                    scores(k, j, u, i)
                keep_busy(env, WARM_UP, REST)
                step(0, 0)
                with pe.Fori(0, TILES - 1) as t:
                    for i in range(1, units + 1):
                        step(t, i)
                for i in range(1, units):
                    step(TILES - 1, i, ahead=i < units - 2)
                finish(TILES - 1)

            @block.scalar
            def _(act):
                def keys(k):
                    act.wait_ge(S["kv_projected"], FIRST + k + 1)
                    nc.scalar.activation(kT[:, :], PS[:, KT, 0:KEYS], ACT.Identity,
                                         bias=w("kb") if biases else 0.0).then_inc(S["kT_ready"], 1)

                def values(j):
                    for n, i0, i1 in ((KCH, 0, 2), (KSIZES[2], 2, 3)):
                        nc.scalar.copy(v[j][0:n, i0:i1, :], PS[0:n, V, i0 * P:i1 * P].rearrange("p (i d) -> p i d", d=D)
                                       ).then_inc(S["v_ready"], 1)

                def exp(n, j, u, parity):
                    act.wait_ge(S["top_ready"], n + 1)
                    for c in range(2):
                        nc.scalar.activation(probs[parity][:, c, :], PS[:, 2 * parity + c, 0:KEYS], ACT.Exp,
                                             bias=ntop[parity][:, c:c + 1],
                                             accum_out=total[j][:, 2 * u + c:2 * u + c + 1]
                                             ).then_inc(S["exped"], 1)

                def step(t, i, ahead=True):
                    n = unit(t, i)[0]
                    if ahead:
                        _, nk, nj, nu = unit(t, i + 2)
                        if nu == 0:
                            keys(nk)
                            values(nj)
                    act.wait_ge(S["turned"], n * 2 + 2)
                    nc.scalar.copy(probsT[0:KSIZES[2], 2, :], PS[0:KSIZES[2], REST, 0:2 * P]
                                   ).then_inc(S["probsT_ready"], 1)
                    if ahead:
                        exp(n + 2, nj, nu, i % 2)

                for i in range(2):
                    n, k, j, u = unit(0, i)
                    if u == 0:
                        keys(k)
                        values(j)
                    exp(n, j, u, i)
                step(0, 0)
                with act.Fori(0, TILES - 1) as t:
                    for i in range(1, units + 1):
                        step(t, i)
                for i in range(1, units):
                    step(TILES - 1, i, ahead=i < units - 2)

            @block.vector
            def _(dve):
                def maximum(n, parity):
                    dve.wait_ge(S["scored"], n + 1)
                    nc.vector.tensor_reduce(ntop[parity][:, :], PS[:, 2 * parity:2 * parity + 2, 0:KEYS], AX.X, ALU.max,
                                            negate=True).then_inc(S["top_ready"], 1)

                def step(t, i, ahead=True):
                    n, k, j, u = unit(t, i)
                    ends = u == per_batch - 1
                    if ends:
                        dve.wait_ge(S["exped"], n * 2 + 2)
                        nc.vector.reciprocal(inv[:, :], total[j][:, :]).then_inc(S["inv_made"], 1)
                    dve.wait_ge(S["turned"], n * 2 + 1)
                    nc.vector.tensor_copy(probsT[:, 0:2, :], PS[0:KCH, PT, :].rearrange("p (i r) -> p i r", i=2)
                                          ).then_inc(S["probsT_ready"], 1)
                    if ahead:
                        maximum(n + 2, i % 2)
                    if i == units:
                        add(t)
                    if ends:
                        dve.wait_ge(S["weighed"], n + 1)
                        dve.wait_ge(S["inv_turned"], k + 1)
                        nc.vector.tensor_tensor(oh[:, :, :], PS[:, REST, OT_COLS].rearrange("p (h q) -> p h q", h=4),
                                                over(spread, 2, [P, 4, SEQ]), ALU.mult)
                        dve.drain()
                        nc.vector.tensor_reduce(o[:, :], oh[:, :, :].rearrange("p h q -> p q h"), AX.X, ALU.add)
                        dve.drain()
                        nc.vector.tensor_tensor(attT[:, j * SEQ:(j + 1) * SEQ], PS[:, REST, RT_COLS], o[:, :],
                                                ALU.mult).then_inc(S["batch_read"], 1)
                        if j == PER_TILE - 1:
                            dve.drain()
                            if biases:
                                nc.vector.tensor_scalar(attT[:, :], attT[:, :], w("vbc"), None, ALU.add)
                                dve.drain()
                            dve.sem_inc(S["attT_ready"], 1)

                def add(t):
                    here = X[:, t, :] if isinstance(t, int) else X[:, bass.ds(t, 1), :].rearrange("p o d -> p (o d)")
                    dve.wait_ge(S["out_projected"], t + 1)
                    nc.vector.tensor_tensor(here, here, PS[:, KT, OUT_COLS], ALU.add)
                    dve.drain()
                    dve.sem_inc(S["tile_added"], 1)
                    if biases:
                        nc.vector.tensor_tensor(here, here, w("ob"), ALU.add)

                maximum(0, 0)
                maximum(1, 1)
                step(0, 0)
                with dve.Fori(0, TILES - 1) as t:
                    for i in range(1, units + 1):
                        step(t, i)
                for i in range(1, units):
                    step(TILES - 1, i, ahead=i < units - 2)
                add(TILES - 1)


def single_cross_attention(env, layer, X, ctxT, ctx_rows, rows_loaded, qT, mask, scale):
    nc = env.nc
    env.stage()
    w = lambda n: env.w(layer + n)
    ident = env.c("ident")
    PS = env.PS
    Q, QB = (0, 1), 2
    SCORES, TURNED, SUMS, OUT = (0, 1), 2, 3, 4
    with ExitStack() as s:
        kq = env.sb(s, "queries_times_wk", [P, TOKENS])
        qb = env.sb(s, "queries_times_bk", [P, TILES])
        sc = env.sb(s, "scores", [P, KEYS])
        probs = env.sb(s, "probs", [P, KEYS])
        probsT = env.sb(s, "probsT", [KCH, 3, P])
        ntop = env.sb(s, "minus_top", [P, 1])
        total = [env.sb(s, f"total{i}", [P, 1]) for i in range(2)]
        inv = env.sb(s, "inv", [P, 1])
        cx = env.sb(s, "ctx_sum", [P, D])
        cxT = env.sb(s, "ctx_sumT", [P, D])
        names = ("kq_done", "qb_done", "scored", "top_ready", "exped", "turned", "probsT_ready",
                 "weighed", "cx_ready", "cx_turned", "cxT_ready", "projected", "tile_added")
        S = {n: env.sem(s, n) for n in names}
        with nc.Block() as block:
            @block.tensor
            def _(pe):
                for h in range(2):
                    nc.tensor.matmul(PS[:, Q[h], :], w("kT"), qT[:, h * BANK:(h + 1) * BANK], start=True, stop=True
                                     ).then_inc(S["kq_done"], 1)
                for t in range(TILES):
                    last = nc.tensor.matmul(PS[:, QB, t:t + 1], qT[:, t * P:(t + 1) * P], w("kb"),
                                            start=True, stop=True)
                last.then_inc(S["qb_done"], 1)

            @block.scalar
            def _(act):
                act.wait_ge(S["kq_done"], 1)
                nc.scalar.activation(kq[:, 0:BANK], PS[:, Q[0], :], ACT.Copy, scale=scale)

            @block.vector
            def _(dve):
                dve.wait_ge(S["kq_done"], 2)
                nc.vector.tensor_scalar(kq[:, BANK:2 * BANK], PS[:, Q[1], :], scale, None, ALU.mult)
                dve.wait_ge(S["qb_done"], 1)
                nc.vector.tensor_scalar(qb[:, :], PS[:, QB, 0:TILES], scale, None, ALU.mult)

        with nc.Block() as block:
            @block.tensor
            def _(pe):
                def scores(t, y):
                    for j in range(PER_TILE):
                        r = slice(32 * j, 32 * j + 32)
                        last = nc.tensor.matmul(PS[r, SCORES[y], 0:KEYS], kq[:, t * P + 32 * j:t * P + 32 * j + 32],
                                                ctxT[:, t * PER_TILE + j, :], start=True, stop=True)
                    last.then_inc(S["scored"], 1)

                def step(t, y, ahead=True):
                    pe.wait_ge(S["exped"], t + 1)
                    for i in range(3):
                        last = nc.tensor.transpose(PS[0:KSIZES[i], TURNED, i * P:(i + 1) * P],
                                                   probs[:, i * KCH:i * KCH + KSIZES[i]], ident)
                    last.then_inc(S["turned"], 1)
                    if ahead:
                        scores(t + 1, 1 - y)
                    pe.wait_ge(S["probsT_ready"], t + 1)
                    for i in range(3):
                        for j in range(PER_TILE):
                            r = slice(32 * j, 32 * j + 32)
                            last = nc.tensor.matmul(PS[r, SUMS, 0:D], probsT[0:KSIZES[i], i, r],
                                                    ctx_rows[0:KSIZES[i], t * PER_TILE + j, i, :],
                                                    start=i == 0, stop=i == 2)
                    last.then_inc(S["weighed"], 1)
                    pe.wait_ge(S["cx_ready"], t + 1)
                    if t > 0:
                        pe.wait_ge(S["tile_added"], t)
                    nc.tensor.transpose(PS[:, OUT, 0:D], cx[:, :], ident).then_inc(S["cx_turned"], 1)
                    pe.wait_ge(S["cxT_ready"], t + 1)
                    nc.tensor.matmul(PS[:, OUT, D:2 * D], cxT[:, :], w("v"), start=True, stop=True
                                     ).then_inc(S["projected"], 1)

                pe.wait_ge(rows_loaded, LOADED)
                scores(0, 0)
                for t in range(TILES):
                    step(t, t % 2, ahead=t < TILES - 1)

            @block.scalar
            def _(act):
                def step(t, y):
                    act.wait_ge(S["top_ready"], t + 1)
                    nc.scalar.activation(probs[:, :], sc[:, :], ACT.Exp, bias=ntop[:, :],
                                         accum_out=total[y][:, :]).then_inc(S["exped"], 1)
                    act.wait_ge(S["weighed"], t + 1)
                    nc.scalar.copy(cx[:, :], PS[:, SUMS, 0:D]).then_inc(S["cx_ready"], 1)
                    act.wait_ge(S["cx_turned"], t + 1)
                    nc.scalar.copy(cxT[:, :], PS[:, OUT, 0:D]).then_inc(S["cxT_ready"], 1)

                for t in range(TILES):
                    step(t, t % 2)

            @block.vector
            def _(dve):
                def top(t, y):
                    dve.wait_ge(S["scored"], t + 1)
                    nc.vector.scalar_tensor_tensor(sc[:, :], PS[:, SCORES[y], 0:KEYS], qb[:, t:t + 1], mask[:, :],
                                                   ALU.add, ALU.add)
                    dve.drain()
                    nc.vector.tensor_reduce(ntop[:, :], sc[:, :], AX.X, ALU.max, negate=True
                                            ).then_inc(S["top_ready"], 1)

                def step(t, y, ahead=True):
                    dve.wait_ge(S["turned"], t + 1)
                    nc.vector.tensor_copy(probsT[:, 0:2, :],
                                          PS[0:KCH, TURNED, 0:2 * P].rearrange("p (i r) -> p i r", r=P))
                    nc.vector.tensor_copy(probsT[0:KSIZES[2], 2, :], PS[0:KSIZES[2], TURNED, 2 * P:3 * P])
                    dve.drain()
                    dve.sem_inc(S["probsT_ready"], 1)
                    nc.vector.reciprocal(inv[:, :], total[y][:, :])
                    if ahead:
                        top(t + 1, 1 - y)
                    else:
                        dve.drain()
                    dve.wait_ge(S["projected"], t + 1)
                    nc.vector.scalar_tensor_tensor(X[:, t, :], PS[:, OUT, D:2 * D], inv[:, :], X[:, t, :],
                                                   ALU.mult, ALU.add)
                    dve.drain()
                    dve.sem_inc(S["tile_added"], 1)
                    nc.vector.tensor_tensor(X[:, t, :], X[:, t, :], w("vb"), ALU.add)

                top(0, 0)
                for t in range(TILES):
                    step(t, t % 2, ahead=t < TILES - 1)


def int8_matmul(env, X, z):
    nc = env.nc
    env.stage()
    PS = env.PS
    WT = env.w("L0f_T")
    ident = env.c("ident")
    with ExitStack() as s:
        qz = env.sb(s, "z_rounded", [P, TILES, D])
        zs = env.sb(s, "z_scale", [P, TILES])
        zi = env.sb(s, "z_inverse", [P, TILES])
        qw = env.sb(s, "w_rounded", [P, D])
        ws = env.sb(s, "w_scale", [P, 2])
        diag = env.sb(s, "w_scale_diag", [P, P])
        wrow = env.sb(s, "w_scale_row", [P, P])
        qwT = env.sb(s, "w_turned", [P, D], BF16)
        qzT = env.sb(s, "z_turned", [P, TOKENS], BF16)
        prod = env.sb(s, "product", [P, TILES, D])
        names = ("w_rounded", "w_turned", "z_rounded", "z_turned", "copied", "multiplied")
        S = {n: env.sem(s, n) for n in names}
        with nc.Block() as block:
            @block.vector
            def _(dve):
                def rounded(out, values, inverse):
                    nc.vector.tensor_tensor(out, values, inverse, ALU.mult)
                    dve.drain()
                    nc.vector.tensor_scalar(out, out, ROUND, ROUND, ALU.add, ALU.subtract)
                    dve.drain()
                    return nc.vector.tensor_scalar(out, out, QMAX, -QMAX, ALU.min, ALU.max)

                nc.vector.tensor_reduce(ws[:, 0:1], WT, AX.X, ALU.max, apply_absolute_value=True)
                nc.vector.tensor_reduce(zs[:, :], z[:, :, :], AX.X, ALU.max, apply_absolute_value=True)
                dve.drain()
                nc.vector.tensor_scalar(ws[:, 0:1], ws[:, 0:1], 1e-12, 1.0 / QMAX, ALU.max, ALU.mult)
                nc.vector.tensor_scalar(zs[:, :], zs[:, :], 1e-12, 1.0 / QMAX, ALU.max, ALU.mult)
                dve.drain()
                nc.vector.reciprocal(ws[:, 1:2], ws[:, 0:1])
                nc.vector.reciprocal(zi[:, :], zs[:, :])
                nc.vector.tensor_scalar(diag[:, :], ident, ws[:, 0:1], None, ALU.mult)
                dve.drain()
                rounded(qw[:, :], WT, ws[:, 1:2].broadcast_to([P, D])).then_inc(S["w_rounded"], 1)
                rounded(qz[:, :, :], z[:, :, :], over(zi[:, :], 2, [P, TILES, D])).then_inc(S["z_rounded"], 1)
                dve.wait_ge(S["w_turned"], 1)
                nc.vector.tensor_copy(wrow[:, :], PS[:, 4, 0:P])
                nc.vector.tensor_copy(qwT[:, :], PS[:, 4, P:2 * P]).then_inc(S["copied"], 1)
                dve.drain()
                for h in range(2):
                    dve.wait_ge(S["multiplied"], h + 1)
                    half = slice(4 * h, 4 * h + 4)
                    nc.vector.tensor_tensor(prod[:, half, :], PS[:, 2 + h, :].rearrange("p (t d) -> p t d", t=4),
                                            over(zs[:, half], 2, [P, 4, D]), ALU.mult)
                dve.drain()
                nc.vector.tensor_tensor(prod[:, :, :], prod[:, :, :], over(wrow[:, :], 1, [P, TILES, D]), ALU.mult)
                dve.drain()
                nc.vector.tensor_tensor(X[:, :, :], X[:, :, :], prod[:, :, :], ALU.add)

            @block.tensor
            def _(pe):
                pe.wait_ge(S["w_rounded"], 1)
                nc.tensor.matmul(PS[:, 4, 0:P], env.c("ones"), diag[:, :], start=True, stop=True)
                nc.tensor.transpose(PS[:, 4, P:2 * P], qw[:, :], ident).then_inc(S["w_turned"], 1)
                pe.wait_ge(S["z_rounded"], 1)
                for t in range(TILES):
                    nc.tensor.transpose(PS[:, t // 4, (t % 4) * P:(t % 4 + 1) * P], qz[:, t, :], ident
                                        ).then_inc(S["z_turned"], 1)
                for t in range(TILES):
                    if t % 4 == 0:
                        pe.wait_ge(S["copied"], 2 + t // 4)
                    last = nc.tensor.matmul(PS[:, 2 + t // 4, (t % 4) * P:(t % 4 + 1) * P],
                                            qzT[:, t * P:(t + 1) * P], qwT[:, :], start=True, stop=True)
                    if t % 4 == 3:
                        last.then_inc(S["multiplied"], 1)

            @block.scalar
            def _(act):
                act.wait_ge(S["copied"], 1)
                for h in range(2):
                    act.wait_ge(S["z_turned"], 4 * (h + 1))
                    nc.scalar.copy(qzT[:, h * BANK:(h + 1) * BANK], env.bank(h)).then_inc(S["copied"], 1)


def laplacian_attention(env, X, zT, bucket_dram):
    nc = env.nc
    env.stage()
    PS = env.PS
    mu, std = float(np.sqrt(0.5)), float(np.sqrt(0.25 * np.pi))
    w = lambda n: env.w("L1a_" + n)
    with ExitStack() as s:
        hot = env.sb(s, "buckets", [32, SEQ, P])
        bias = env.sb(s, "bias", [P, SEQ])
        qk = env.sb(s, "qk", [P, TOKENS])
        q = env.sb(s, "q", [P, TOKENS])
        k = env.sb(s, "k", [P, TOKENS])
        v = env.sb(s, "v", [P, TILES, D])
        sim = env.sb(s, "sim", [P, TILES, P])
        near = env.sb(s, "near_zero", [P, TILES, P])
        cum = env.sb(s, "gelu", [P, TILES, P])
        names = ("buckets_loaded", "bias_summed", "qk_projected", "qk_swished", "q_ready", "v_projected",
                 "v_biased", "v_ready", "scored", "sim_ready", "gelu_ready", "weights_ready", "weighed")
        S = {n: env.sem(s, n) for n in names}
        with nc.Block() as block:
            @block.sync
            def _(sp):
                sp.dma_start(hot[:, :, :], bucket_dram.rearrange("n (q p) -> n q p", q=SEQ)
                             ).then_inc(S["buckets_loaded"], 16)

            @block.tensor
            def _(pe):
                for h in range(2):
                    nc.tensor.matmul(env.bank(h), w("qk"), zT[:, h * BANK:(h + 1) * BANK], start=True, stop=True
                                     ).then_inc(S["qk_projected"], 1)
                for t in range(TILES):
                    last = nc.tensor.matmul(PS[:, 2 + t // 4, (t % 4) * P:(t % 4 + 1) * P],
                                            zT[:, t * P:(t + 1) * P], w("v"), start=True, stop=True)
                last.then_inc(S["v_projected"], 1)
                pe.wait_ge(S["buckets_loaded"], LOADED)
                for i in range(SEQ):
                    last = nc.tensor.matmul(PS[:, 4, i:i + 1], hot[:, i, :], w("rel")[0:32], start=True, stop=True)
                last.then_inc(S["bias_summed"], 1)
                pe.wait_ge(S["q_ready"], 1)
                for t in range(TILES):
                    last = nc.tensor.matmul(PS[:, 6 + t // 4, (t % 4) * P:(t % 4 + 1) * P],
                                            k[:, t * P:(t + 1) * P], q[:, t * P:(t + 1) * P], start=True, stop=True)
                last.then_inc(S["scored"], 1)
                pe.wait_ge(S["weights_ready"], 1)
                pe.wait_ge(S["v_ready"], 1)
                for t in range(TILES):
                    last = nc.tensor.matmul(PS[:, t // 4, (t % 4) * P:(t % 4 + 1) * P], sim[:, t, :], v[:, t, :],
                                            start=True, stop=True)
                last.then_inc(S["weighed"], 1)

            @block.scalar
            def _(act):
                for h in range(2):
                    act.wait_ge(S["qk_projected"], h + 1)
                    nc.scalar.activation(qk[:, h * BANK:(h + 1) * BANK], env.bank(h), ACT.Silu, bias=w("qkb")
                                         ).then_inc(S["qk_swished"], 1)
                act.wait_ge(S["v_biased"], 1)
                nc.scalar.activation(v[:, :, :], v[:, :, :], ACT.Silu).then_inc(S["v_ready"], 1)
                act.wait_ge(S["sim_ready"], 1)
                nc.scalar.activation(cum[:, :, :], near[:, :, :], ACT.Gelu).then_inc(S["gelu_ready"], 1)

            @block.vector
            def _(dve):
                dve.wait_ge(S["v_projected"], 1)
                nc.vector.tensor_tensor(v[:, :, :], PS[:, 2:4, :].rearrange("p h (t d) -> p (h t) d", t=4),
                                        over(w("vb"), 1, [P, TILES, D]), ALU.add).then_inc(S["v_biased"], 1)
                dve.wait_ge(S["qk_swished"], 2)
                for out, i in ((q, 0), (k, 1)):
                    nc.vector.tensor_scalar(out[:, :], qk[:, :], w("gamma")[:, i:i + 1], w("beta")[:, i:i + 1],
                                            ALU.mult, ALU.add)
                dve.drain()
                dve.sem_inc(S["q_ready"], 1)
                dve.wait_ge(S["bias_summed"], 1)
                nc.vector.tensor_scalar(bias[:, :], PS[:, 4, 0:SEQ], float(D ** 0.5), -mu, ALU.mult, ALU.add)
                dve.drain()
                dve.wait_ge(S["scored"], 1)
                nc.vector.scalar_tensor_tensor(sim[:, :, :].rearrange("p t (b q) -> p (t b) q", q=SEQ),
                                               PS[:, 6:8, :].rearrange("p h (b q) -> p (h b) q", q=SEQ), 1.0 / SEQ,
                                               over(bias[:, :], 1, [P, BATCH, SEQ]), ALU.mult, ALU.add)
                dve.drain()
                nc.vector.tensor_scalar(sim[:, :, :], sim[:, :, :], 1.0 / std, None, ALU.mult)
                dve.drain()
                nc.vector.tensor_scalar(near[:, :, :], sim[:, :, :], 0.0, 1e-20, ALU.is_equal, ALU.mult)
                dve.drain()
                nc.vector.tensor_tensor(near[:, :, :], near[:, :, :], sim[:, :, :], ALU.add
                                        ).then_inc(S["sim_ready"], 1)
                dve.drain()
                nc.vector.reciprocal(sim[:, :, :], near[:, :, :])
                dve.wait_ge(S["gelu_ready"], 1)
                dve.drain()
                nc.vector.tensor_tensor(sim[:, :, :], sim[:, :, :], cum[:, :, :], ALU.mult)
                dve.drain()
                nc.vector.tensor_tensor(sim[:, :, :], sim[:, :, :], over(env.c("past"), 1, [P, TILES, P]), ALU.mult
                                        ).then_inc(S["weights_ready"], 1)
                dve.wait_ge(S["weighed"], 1)
                nc.vector.tensor_tensor(X[:, :, :], X[:, :, :], PS[:, 0:2, :].rearrange("p h (t d) -> p (h t) d", t=4),
                                        ALU.add)


def route(env, gates, gatesT, zT, router, n_experts, capacity, floor, factor, places=None):
    nc = env.nc
    env.stage()
    PS = env.PS
    E = n_experts
    full = [P, TILES, E]
    with ExitStack() as s:
        lg = env.sb(s, "logits", full)
        tmp = env.sb(s, "masked_logits", full)
        m = env.sb(s, "best_two", [P, 2, TILES, E])
        pr = env.sb(s, "probs", full)
        st = env.sb(s, "stats", [P, TILES, 6])
        run = env.sb(s, "running", [P, 2, 2 * TILES, E])
        names = ("logits_done", "shifted", "exped", "hot_ready", "summed", "gates_ready", "gates_turned")
        S = {n: env.sem(s, n) for n in names}
        with nc.Block() as block:
            @block.tensor
            def _(pe):
                for t in range(TILES):
                    last = nc.tensor.matmul(PS[:, 0, t * E:(t + 1) * E], zT[:, t * P:(t + 1) * P], router,
                                            start=True, stop=True)
                last.then_inc(S["logits_done"], 1)
                if capacity is not None:
                    pe.wait_ge(S["hot_ready"], 1)
                    flat = m[:, :, :, :].rearrange("p n t e -> p (n t e)")
                    nc.tensor.matmul(PS[:, 1, 0:2 * TILES * E], env.c("upto"), flat, start=True, stop=True)
                    nc.tensor.matmul(PS[:, 2, 0:2 * TILES * E], env.c("ones"), flat, start=True, stop=True
                                     ).then_inc(S["summed"], 1)
                pe.wait_ge(S["gates_ready"], 1)
                for t in range(TILES):
                    last = nc.tensor.transpose(PS[0:E, 3 + t // 4, (t % 4) * P:(t % 4 + 1) * P], gates[:, t, :],
                                               env.c("ident"))
                last.then_inc(S["gates_turned"], 1)

            @block.scalar
            def _(act):
                act.wait_ge(S["shifted"], 1)
                nc.scalar.activation(pr[:, :, :], pr[:, :, :], ACT.Exp).then_inc(S["exped"], 1)

            @block.vector
            def _(dve):
                def st_over(i):
                    return st[:, :, i:i + 1].broadcast_to(full)

                def best(out, values):
                    nc.vector.tensor_reduce(st[:, :, 0], values, AX.X, ALU.max)
                    dve.drain()
                    nc.vector.tensor_tensor(out, values, st_over(0), ALU.is_equal)
                    dve.drain()
                    nc.vector.tensor_tensor(out, out, over(env.c("first_wins")[:, 0:E], 1, full), ALU.mult)
                    dve.drain()
                    nc.vector.tensor_reduce(st[:, :, 1], out, AX.X, ALU.max)
                    dve.drain()
                    nc.vector.tensor_tensor(out, out, st_over(1), ALU.is_equal)
                    dve.drain()

                dve.wait_ge(S["logits_done"], 1)
                nc.vector.tensor_copy(lg[:, :, :], PS[:, 0, 0:TILES * E].rearrange("p (t e) -> p t e", e=E))
                dve.drain()
                best(m[:, 0, :, :], lg[:, :, :])
                nc.vector.tensor_tensor(pr[:, :, :], lg[:, :, :], st_over(0), ALU.subtract).then_inc(S["shifted"], 1)
                nc.vector.scalar_tensor_tensor(tmp[:, :, :], m[:, 0, :, :], MASKED, lg[:, :, :], ALU.mult, ALU.add)
                dve.drain()
                best(m[:, 1, :, :], tmp[:, :, :])
                dve.sem_inc(S["hot_ready"], 1)
                dve.wait_ge(S["exped"], 1)
                nc.vector.tensor_reduce(st[:, :, 2], pr[:, :, :], AX.X, ALU.add)
                dve.drain()
                nc.vector.reciprocal(st[:, :, 3], st[:, :, 2])
                dve.drain()
                nc.vector.tensor_tensor(pr[:, :, :], pr[:, :, :], st_over(3), ALU.mult)
                if capacity is not None:
                    n = 2 * TILES
                    dve.wait_ge(S["summed"], 1)
                    totals = PS[:, 2, 0:n * E].rearrange("p (n e) -> p n e", e=E)
                    nc.vector.memset(run[:, 0, 0:1, :], 0.0)
                    nc.vector.tensor_copy(run[:, 0, 1:n, :], totals[:, 0:n - 1, :])
                    src = 0
                    for shift in (1, 2, 4, 8):
                        dve.drain()
                        nc.vector.tensor_copy(run[:, 1 - src, 0:shift, :], run[:, src, 0:shift, :])
                        nc.vector.tensor_tensor(run[:, 1 - src, shift:n, :], run[:, src, shift:n, :],
                                                run[:, src, 0:n - shift, :], ALU.add)
                        src = 1 - src
                    dve.drain()
                    nc.vector.tensor_tensor(run[:, src, :, :], run[:, src, :, :],
                                            PS[:, 1, 0:n * E].rearrange("p (n e) -> p n e", e=E), ALU.add)
                    dve.drain()
                    hot = m[:, :, :, :].rearrange("p n t e -> p (n t) e")
                    nc.vector.scalar_tensor_tensor(hot, run[:, src, :, :], float(capacity), hot,
                                                   ALU.is_le, ALU.mult)
                dve.drain()
                if places is not None:
                    nc.vector.tensor_tensor(run[:, src, :, :], run[:, src, :, :], hot, ALU.mult)
                    dve.drain()
                    nc.vector.tensor_tensor(places[:, :, :], run[:, src, 0:TILES, :], run[:, src, TILES:n, :], ALU.add)
                nc.vector.tensor_tensor(tmp[:, :, :], m[:, 0, :, :], m[:, 1, :, :], ALU.add)
                dve.drain()
                nc.vector.tensor_tensor(pr[:, :, :], pr[:, :, :], tmp[:, :, :], ALU.mult)
                dve.drain()
                nc.vector.tensor_reduce(st[:, :, 4], pr[:, :, :], AX.X, ALU.add)
                dve.drain()
                nc.vector.tensor_scalar(st[:, :, 4], st[:, :, 4], floor, None, ALU.max)
                dve.drain()
                nc.vector.reciprocal(st[:, :, 5], st[:, :, 4])
                dve.drain()
                nc.vector.scalar_tensor_tensor(gates[:, :, :], pr[:, :, :], factor, st_over(5), ALU.mult, ALU.mult
                                               ).then_inc(S["gates_ready"], 1)
                dve.wait_ge(S["gates_turned"], 1)
                nc.vector.tensor_copy(gatesT[0:E, :], PS[0:E, 3:5, :].rearrange("p h c -> p (h c)"))


def experts(env, acc, zT, gates, gatesT, dram, b2, n_experts, hidden, func):
    nc = env.nc
    env.stage()
    PS = env.PS
    n_f = hidden // P
    cols = hidden + n_f * D + n_f
    units = 2 * n_f
    with ExitStack() as s:
        wt = [env.sb(s, f"expert{i}", [P, cols]) for i in range(2)]
        h = [env.sb(s, f"hidden{i}", [P, n_f, TOKENS]) for i in range(2)]
        gc = [env.sb(s, f"gate_col{i}", [P, TILES]) for i in range(2)]
        names = ("b2_done", "acc_begun", "fc1_done", "hidden_ready", "fc2_done", "added", "gate_copied")
        S = {n: env.sem(s, n) for n in names}
        loaded = [env.sem(s, f"expert_loaded{i}") for i in range(2)]
        head_start(env, [S[n] for n in ("fc2_done", "hidden_ready", "added")])
        with nc.Block() as block:
            @block.sync
            def _(sp):
                for x in range(2):
                    sp.dma_start(wt[x][:, :], dram[x, :, :]).then_inc(loaded[x], 16)
                with sp.Fori(0, n_experts // 2 - 1) as i:
                    for x in range(2):
                        sp.wait_ge(S["fc2_done"], FIRST + (i * 2 + x + 1) * TILES)
                        sp.dma_start(wt[x][:, :], dram[i * 2 + 2 + x, :, :]).then_inc(loaded[x], 16)

            @block.tensor
            def _(pe):
                for t in range(TILES):
                    last = nc.tensor.matmul(PS[:, 4 + t // 4, (t % 4) * P:(t % 4 + 1) * P],
                                            gatesT[0:n_experts, t * P:(t + 1) * P], b2[0:n_experts],
                                            start=True, stop=True)
                last.then_inc(S["b2_done"], 1)
                pe.wait_ge(S["acc_begun"], 1)
                with pe.Fori(0, n_experts // 2) as i:
                    for x in range(2):
                        e = i * 2 + x
                        pe.wait_ge(loaded[x], i * 16 + 16)
                        for u in range(units):
                            half, f = u // n_f, u % n_f
                            if u >= 4:
                                pe.wait_ge(S["hidden_ready"], FIRST + e * units + u - 3)
                            elif x == 0:
                                pe.wait_ge(S["hidden_ready"], FIRST + i * 2 * units)
                            else:
                                pe.wait_ge(S["hidden_ready"], FIRST + (i * 2 + 1) * units - 3 + u)
                            nc.tensor.matmul(PS[:, u % 4, :], wt[x][:, f * P:(f + 1) * P],
                                             zT[:, half * BANK:(half + 1) * BANK], start=True, stop=True
                                             ).then_inc(S["fc1_done"], 1)
                        for t in range(TILES):
                            if t % (TILES // 2) == 0:
                                pe.wait_ge(S["hidden_ready"], FIRST + e * units + (1 + t // (TILES // 2)) * n_f)
                            if t >= 4:
                                pe.wait_ge(S["added"], FIRST + e * TILES + t - 3)
                            else:
                                pe.wait_ge(S["added"], FIRST + e * TILES)
                            for f in range(n_f):
                                last = nc.tensor.matmul(PS[:, 4 + t % 4, 0:D], h[x][:, f, t * P:(t + 1) * P],
                                                        wt[x][:, hidden + f * D:hidden + (f + 1) * D],
                                                        start=f == 0, stop=f == n_f - 1)
                            last.then_inc(S["fc2_done"], 1)

            @block.scalar
            def _(act):
                with act.Fori(0, n_experts // 2) as i:
                    for x in range(2):
                        e = i * 2 + x
                        act.wait_ge(loaded[x], i * 16 + 16)
                        act.wait_ge(S["fc2_done"], FIRST + i * 2 * TILES)
                        for u in range(units):
                            half, f = u // n_f, u % n_f
                            act.wait_ge(S["fc1_done"], e * units + u + 1)
                            nc.scalar.activation(h[x][:, f, half * BANK:(half + 1) * BANK], PS[:, u % 4, :], func,
                                                 bias=wt[x][:, hidden + n_f * D + f:hidden + n_f * D + f + 1]
                                                 ).then_inc(S["hidden_ready"], 1)

            @block.gpsimd
            def _(pool):
                with pool.Fori(0, n_experts // 2) as i:
                    for x in range(2):
                        pool.wait_ge(S["added"], FIRST + i * 2 * TILES)
                        nc.gpsimd.tensor_copy(gc[x][:, :], gates[:, :, bass.ds(i * 2 + x, 1)].rearrange("p t o -> p (t o)")
                                              ).then_inc(S["gate_copied"], 1)

            @block.vector
            def _(dve):
                dve.wait_ge(S["b2_done"], 1)
                nc.vector.tensor_copy(acc[:, :, :], PS[:, 4:6, :].rearrange("p h (t d) -> p (h t) d", t=4)
                                      ).then_inc(S["acc_begun"], 1)
                dve.drain()
                with dve.Fori(0, n_experts // 2) as i:
                    for x in range(2):
                        e = i * 2 + x
                        dve.wait_ge(S["gate_copied"], e + 1)
                        for t in range(TILES):
                            dve.wait_ge(S["fc2_done"], FIRST + e * TILES + t + 1)
                            nc.vector.scalar_tensor_tensor(acc[:, t, :], PS[:, 4 + t % 4, 0:D], gc[x][:, t:t + 1],
                                                           acc[:, t, :], ALU.mult, ALU.add).then_inc(S["added"], 1)
                        dve.drain()


def dispatched_experts(env, acc, z, scale, shift, gates, gatesT, places, dram, b2, n_experts, hidden, func):
    nc = env.nc
    env.stage()
    PS = env.PS
    n_f = hidden // P
    cols = hidden + n_f * D + n_f
    XIN, Y, HIDDEN, BACK, OUT = 0, 1, 2, (3, 4), (5, 6)
    half_tiles = TILES // 2
    with ExitStack() as s:
        wt = [env.sb(s, f"expert{i}", [P, cols]) for i in range(2)]
        slot_of = [env.sb(s, f"slot_of{i}", [P, TILES, P]) for i in range(2)]
        slot_ofT = [env.sb(s, f"slot_ofT{i}", [P, TOKENS]) for i in range(2)]
        xinT = env.sb(s, "slots_inT", [P, P])
        h = env.sb(s, "hidden", [P, n_f, P])
        y = env.sb(s, "slots_out", [P, D])
        gated = [env.sb(s, f"gated{i}", [P, half_tiles, D]) for i in range(2)]
        names = ("b2_done", "acc_begun", "slots_known", "xin_done", "xin_ready", "turned", "first_turned_copied",
                 "second_turned_copied", "fc1_done", "hidden_ready", "fc2_done", "y_ready", "sent_back", "gated",
                 "added")
        S = {n: env.sem(s, n) for n in names}
        loaded = [env.sem(s, f"expert_loaded{i}") for i in range(2)]
        head_start(env, [S[n] for n in ("gated", "added")])

        def pairs(engine, step):
            with engine.Fori(0, n_experts // 2 - 1) as pair:
                for x in range(2):
                    step(pair, pair * 2 + x, x, 2)
            step(n_experts // 2 - 1, n_experts - 2, 0, 1)
            step(n_experts // 2 - 1, n_experts - 1, 1, 0)

        with nc.Block() as block:
            @block.sync
            def _(sp):
                for x in range(2):
                    sp.dma_start(wt[x][:, :], dram[x, :, :]).then_inc(loaded[x], 16)
                with sp.Fori(0, n_experts // 2 - 1) as i:
                    for x in range(2):
                        sp.wait_ge(S["fc2_done"], i * 2 + x + 1)
                        sp.dma_start(wt[x][:, :], dram[i * 2 + 2 + x, :, :]).then_inc(loaded[x], 16)

            @block.tensor
            def _(pe):
                def dispatch(e, x):
                    pe.wait_ge(S["slots_known"], e + 1)
                    for t in range(TILES):
                        last = nc.tensor.matmul(PS[:, XIN, 0:P], z[:, t, :], slot_of[x][:, t, :],
                                                start=t == 0, stop=t == TILES - 1)
                    last.then_inc(S["xin_done"], 1)

                def turn(x):
                    for t in range(TILES):
                        last = nc.tensor.transpose(PS[:, BACK[t // half_tiles], t % half_tiles * P:(t % half_tiles + 1) * P],
                                                   slot_of[x][:, t, :], env.c("ident"))
                        if t % half_tiles == half_tiles - 1:
                            last.then_inc(S["turned"], 1)

                def fc1(e, x, pair):
                    pe.wait_ge(loaded[x], pair * 16 + 16)
                    pe.wait_ge(S["xin_ready"], e + 1)
                    for f in range(n_f):
                        last = nc.tensor.matmul(PS[:, HIDDEN, f * P:(f + 1) * P], wt[x][:, f * P:(f + 1) * P],
                                                xinT[:, :], start=True, stop=True)
                    last.then_inc(S["fc1_done"], 1)

                def step(pair, e, x, after):
                    if after:
                        dispatch(e + 1, 1 - x)
                    pe.wait_ge(S["hidden_ready"], e + 1)
                    for f in range(n_f):
                        last = nc.tensor.matmul(PS[:, Y, 0:D], h[:, f, :], wt[x][:, hidden + f * D:hidden + (f + 1) * D],
                                                start=f == 0, stop=f == n_f - 1)
                    last.then_inc(S["fc2_done"], 1)
                    pe.wait_ge(S["first_turned_copied"], e + 1)
                    pe.wait_ge(S["second_turned_copied"], e + 1)
                    if after:
                        turn(1 - x)
                        fc1(e + 1, 1 - x, pair + x)
                    pe.wait_ge(S["y_ready"], e + 1)
                    pe.wait_ge(S["gated"], FIRST + e * 2)
                    for t in range(TILES):
                        last = nc.tensor.matmul(PS[:, OUT[t // half_tiles], t % half_tiles * P:(t % half_tiles + 1) * P],
                                                slot_ofT[x][:, t * P:(t + 1) * P], y[:, :], start=True, stop=True)
                        if t % half_tiles == half_tiles - 1:
                            last.then_inc(S["sent_back"], 1)

                for t in range(TILES):
                    last = nc.tensor.matmul(PS[:, OUT[t // half_tiles], (t % half_tiles) * P:(t % half_tiles + 1) * P],
                                            gatesT[0:n_experts, t * P:(t + 1) * P], b2[0:n_experts],
                                            start=True, stop=True)
                last.then_inc(S["b2_done"], 1)
                dispatch(0, 0)
                turn(0)
                fc1(0, 0, 0)
                pe.wait_ge(S["acc_begun"], 1)
                pairs(pe, step)

            @block.scalar
            def _(act):
                def arrive(e, x):
                    act.wait_ge(S["xin_done"], e + 1)
                    nc.scalar.activation(xinT[:, :], PS[:, XIN, 0:P], ACT.Identity, bias=shift, scale=scale
                                         ).then_inc(S["xin_ready"], 1)
                    act.wait_ge(S["turned"], e * 2 + 1)
                    nc.scalar.copy(slot_ofT[x][:, 0:BANK], env.bank(BACK[0])).then_inc(S["first_turned_copied"], 1)
                    act.wait_ge(S["fc1_done"], e + 1)
                    for f in range(n_f):
                        at = hidden + n_f * D + f
                        last = nc.scalar.activation(h[:, f, :], PS[:, HIDDEN, f * P:(f + 1) * P], func,
                                                    bias=wt[x][:, at:at + 1])
                    act.drain()
                    act.sem_inc(S["hidden_ready"], 1)

                def step(pair, e, x, after):
                    if after:
                        arrive(e + 1, 1 - x)

                arrive(0, 0)
                pairs(act, step)

            @block.vector
            def _(dve):
                def know_slots(e, x):
                    mine = places[:, :, bass.ds(e, 1)] if not isinstance(e, int) else places[:, :, e:e + 1]
                    nc.vector.tensor_tensor(slot_of[x][:, :, :], mine.broadcast_to([P, TILES, P]),
                                            over(env.c("slot_number"), 1, [P, TILES, P]), ALU.is_equal
                                            ).then_inc(S["slots_known"], 1)

                def second_back(e, x):
                    dve.wait_ge(S["turned"], e * 2 + 2)
                    nc.vector.tensor_copy(slot_ofT[x][:, BANK:2 * BANK], env.bank(BACK[1])
                                          ).then_inc(S["second_turned_copied"], 1)

                def step(pair, e, x, after):
                    dve.wait_ge(S["fc2_done"], e + 1)
                    nc.vector.tensor_copy(y[:, :], PS[:, Y, 0:D]).then_inc(S["y_ready"], 1)
                    if after:
                        second_back(e + 1, 1 - x)
                    if after == 2:
                        know_slots(e + 2, x)
                    for half in range(2):
                        r = slice(half * half_tiles, (half + 1) * half_tiles)
                        gate = gates[:, r, bass.ds(e, 1)] if not isinstance(e, int) else gates[:, r, e:e + 1]
                        dve.wait_ge(S["sent_back"], e * 2 + half + 1)
                        dve.wait_ge(S["added"], FIRST + e * 2)
                        nc.vector.tensor_tensor(gated[half][:, :, :], env.bank(OUT[half]).rearrange("p (t d) -> p t d", d=D),
                                                gate.broadcast_to([P, half_tiles, D]), ALU.mult).then_inc(S["gated"], 1)

                know_slots(0, 0)
                know_slots(1, 1)
                dve.wait_ge(S["b2_done"], 1)
                nc.vector.tensor_copy(acc[:, :, :], PS[:, OUT[0]:OUT[1] + 1, :].rearrange("p h (t d) -> p (h t) d", t=4))
                dve.drain()
                dve.sem_inc(S["acc_begun"], 1)
                second_back(0, 0)
                pairs(dve, step)

            @block.gpsimd
            def _(pool):
                def step(pair, e, x, after):
                    for half in range(2):
                        mine = acc[:, half * half_tiles:(half + 1) * half_tiles, :]
                        pool.wait_ge(S["gated"], FIRST + e * 2 + half + 1)
                        nc.gpsimd.tensor_tensor(mine, mine, gated[half][:, :, :], ALU.add).then_inc(S["added"], 1)

                pairs(pool, step)


def add_to(env, X, others):
    nc = env.nc
    with nc.Block() as block:
        @block.vector
        def _(dve):
            for o in others:
                nc.vector.tensor_tensor(X[:, :, :], X[:, :, :], o[:, :, :], ALU.add)
                dve.drain()


def context_lstm(env, X, zT, ctxT):
    nc = env.nc
    env.stage()
    PS = env.PS
    w = lambda n: env.w("L2x_" + n)
    ident = env.c("ident")
    own_row = env.c("own_row").rearrange("p (i m) -> p i m", i=8)
    batch_of_row = env.c("batch_of_row")
    GATES, CTX, OUT = (0, 7), 5, 6
    TURNED, SCORES = (1, 2), (3, 4)
    HALF = 4
    with ExitStack() as s:
        keysT = env.sb(s, "scored_ctxT", [P, BATCH, KEYS])
        rows = env.sb(s, "projected_ctx", [P, BATCH, 2, D])
        lastrow = env.sb(s, "projected_ctx_last", [P, D])
        gx = env.sb(s, "gates_of_x", [P, SEQ + 1, 4, BATCH])
        w_a = env.sb(s, "w_attn", [P, 4 * P])
        w_h = env.sb(s, "w_hidden", [P, 4 * P])
        w_o = env.sb(s, "w_out_hidden", [P, P])
        gb = env.sb(s, "gate_bias", [P, 4])
        outs = env.sb(s, "outs", [P, BATCH, SEQ])
        attn = env.sb(s, "attn", [P, BATCH])
        h2 = env.sb(s, "h2", [P, BATCH])
        c2 = env.sb(s, "c2", [P, BATCH])
        gt = env.sb(s, "gates_tanh", [P, 4, BATCH])
        u = env.sb(s, "in_part", [P, BATCH])
        f = env.sb(s, "kept_part", [P, BATCH])
        tc = env.sb(s, "tanh_c", [P, BATCH])
        gate_spread = env.sb(s, "out_gate_spread", [P, 4, 8, 8])
        hbd = env.sb(s, "h_spread", [P, 4, 8, 8])
        ntop = [env.sb(s, f"minus_top{x}", [P, 1]) for x in range(2)]
        total = [env.sb(s, f"total{x}", [P, 1]) for x in range(2)]
        inv = [env.sb(s, f"inv{x}", [P, 1]) for x in range(2)]
        probs = [env.sb(s, f"probs{x}", [P, KEYS]) for x in range(2)]
        pT = [env.sb(s, f"probsT_spread{x}", [P, 2, 4, HALF, 8]) for x in range(2)]
        share = env.sb(s, "inv_of_row", [P, 4, 8])
        last_share = env.sb(s, "last_prob_of_row", [P, 4, 8])
        cx = env.sb(s, "ctx_sum", [P, D])
        names = ("weights_ready", "gx_done", "gx_ready", "keys_done", "keys_ready", "rows_done", "rows_ready",
                 "gates_done", "tanh_ready", "c_ready", "tanh_c_ready", "h_ready", "h_spread", "scored",
                 "top_ready", "exped", "turned", "pT_ready", "summed", "cx_ready", "share_ready",
                 "out_done", "attn_ready", "outs_turned")
        S = {n: env.sem(s, n) for n in names}
        head_start(env, [S["attn_ready"]])
        with nc.Block() as block:
            @block.vector
            def _(dve):
                nc.vector.tensor_scalar(w_h[:, 0:3 * P], w("hh")[:, 0:3 * P], 0.25, None, ALU.mult)
                nc.vector.tensor_scalar(w_h[:, 3 * P:4 * P], w("hh")[:, 3 * P:4 * P], 0.5, None, ALU.mult)
                nc.vector.tensor_scalar(w_a[:, 0:3 * P], w("iha")[:, 0:3 * P], 0.5, None, ALU.mult)
                nc.vector.tensor_copy(w_a[:, 3 * P:4 * P], w("iha")[:, 3 * P:4 * P])
                nc.vector.tensor_scalar(w_o[:, :], w("oh"), 0.5, None, ALU.mult)
                nc.vector.tensor_tensor(gb[:, :], w("bih"), w("bhh"), ALU.add)
                dve.drain()
                nc.vector.tensor_scalar(gb[:, 0:3], gb[:, 0:3], 0.5, None, ALU.mult).then_inc(S["weights_ready"], 1)
                nc.vector.memset(attn[:, :], 0.0)
                nc.vector.memset(h2[:, :], 0.0)
                nc.vector.memset(c2[:, :], 0.0)
                nc.vector.memset(gx[:, SEQ, :, :], 0.0)
                nc.vector.memset(PS[:, SCORES[0], :], 0.0)
                nc.vector.memset(PS[:, SCORES[1], :], 0.0)
                nc.vector.memset(PS[:, CTX, :], 0.0)
                dve.drain()
                dve.sem_inc(S["rows_ready"], 1)
                for n in range(BATCH // 2):
                    dve.wait_ge(S["rows_done"], n + 1)
                    nc.vector.tensor_copy(rows[:, 2 * n:2 * n + 2, :, :].rearrange("p b c d -> p (b c d)"),
                                          PS[:, 6 + n % 2, :]).then_inc(S["rows_ready"], 1)
                dve.wait_ge(S["rows_done"], BATCH // 2 + 1)
                nc.vector.tensor_copy(lastrow[:, :], PS[:, CTX, 0:D])

            @block.tensor
            def _(pe):
                for n in range(BATCH // 2):
                    for b in (2 * n, 2 * n + 1):
                        if b >= 3:
                            pe.wait_ge(S["keys_ready"], b - 2)
                        nc.tensor.matmul(PS[:, b % 3, 0:KEYS], w("q"), ctxT[:, b, :], start=True, stop=True
                                         ).then_inc(S["keys_done"], 1)
                    if n >= 2:
                        pe.wait_ge(S["rows_ready"], n)
                    for x in range(4):
                        last = nc.tensor.matmul(PS[:, 6 + n % 2, x * D:(x + 1) * D],
                                                ctxT[:, 2 * n + x // 2, x % 2 * P:(x % 2 + 1) * P], w("oc"),
                                                start=True, stop=True)
                    last.then_inc(S["rows_done"], 1)
                for j in range(4):
                    last = nc.tensor.matmul(PS[32 * j:32 * j + 8, CTX, 0:D], ctxT[:, 8 * j:8 * j + 8, KEYS - 1],
                                            w("oc"), start=True, stop=True)
                last.then_inc(S["rows_done"], 1)
                pe.wait_ge(S["keys_ready"], BATCH)
                for i in range(4):
                    for half in range(2):
                        n = 2 * i + half
                        if n >= 3:
                            pe.wait_ge(S["gx_ready"], n - 2)
                        nc.tensor.matmul(PS[:, n % 3, :], w("ihx")[:, i * P:(i + 1) * P],
                                         zT[:, half * BANK:(half + 1) * BANK], start=True, stop=True
                                         ).then_inc(S["gx_done"], 1)

            @block.scalar
            def _(act):
                for b in range(BATCH):
                    act.wait_ge(S["keys_done"], b + 1)
                    nc.scalar.activation(keysT[:, b, :], PS[:, b % 3, 0:KEYS], ACT.Copy, scale=0.5
                                         ).then_inc(S["keys_ready"], 1)
                act.wait_ge(S["weights_ready"], 1)
                for i in range(4):
                    for half in range(2):
                        n = 2 * i + half
                        b = slice(half * BATCH // 2, (half + 1) * BATCH // 2)
                        act.wait_ge(S["gx_done"], n + 1)
                        nc.scalar.activation(gx[:, 0:SEQ, i, b].rearrange("p t b -> p b t"),
                                             PS[:, n % 3, :].rearrange("p (b t) -> p b t", t=SEQ), ACT.Identity,
                                             bias=gb[:, i:i + 1], scale=0.5 if i < 3 else 1.0
                                             ).then_inc(S["gx_ready"], 1)

        STEPS = 8

        def steps_of(turn):
            return [turn * STEPS + i for i in range(STEPS)]

        with nc.Block() as block:
            @block.tensor
            def _(pe):
                def by_columns(bank, cols, lhsT, rhs, start, stop):
                    for c in range(4):
                        r = slice(32 * c, 32 * c + 32)
                        last = nc.tensor.matmul(PS[r, bank, cols], lhsT[:, r], rhs, start=start, stop=stop)
                    return last

                def gates_of_x(t, bank):
                    nc.tensor.matmul(PS[:, bank, 0:4 * BATCH], ident,
                                     gx[:, bass.ds(t, 1), :, :].rearrange("p o g b -> p (o g b)"),
                                     start=True, stop=False)

                def gates_of(weights, state, i, bank, last=False):
                    return by_columns(bank, slice(i * BATCH, (i + 1) * BATCH), weights[:, i * P:(i + 1) * P],
                                      state[:, :], False, last)

                gates_of_x(0, GATES[0])
                for i in range(4):
                    gates_of(w_h, h2, i, GATES[0])
                with pe.Fori(0, SEQ // STEPS) as turn:
                    for t, (now, then) in zip(steps_of(turn), (GATES, GATES[::-1]) * (STEPS // 2)):
                        pe.wait_ge(S["attn_ready"], FIRST + t)
                        for i in range(4):
                            last = gates_of(w_a, attn, i, now, last=i == 3)
                        last.then_inc(S["gates_done"], 1)
                        gates_of_x(t + 1, then)
                        nc.tensor.matmul(PS[:, TURNED[0], :], ident, zT[:, 0:BANK],
                                         start=True, stop=True)
                        for x in range(2):
                            pe.wait_ge(S["h_spread"], t * 2 + x + 1)
                            for i in range(HALF):
                                for j in range(4):
                                    last = nc.tensor.matmul(PS[32 * j:32 * j + 8, SCORES[x], 0:KEYS],
                                                            hbd[:, j, HALF * x + i, :],
                                                            keysT[:, 8 * j + HALF * x + i, :],
                                                            start=i == 0, stop=i == HALF - 1)
                            last.then_inc(S["scored"], 1)
                        for x in range(2):
                            pe.wait_ge(S["exped"], t * 2 + x + 1)
                            for c in range(2):
                                last = nc.tensor.transpose(PS[:, TURNED[x], c * P:(c + 1) * P],
                                                           probs[x][:, c * P:(c + 1) * P], ident)
                            last.then_inc(S["turned"], 1)
                            if x == 0:
                                pe.wait_ge(S["h_ready"], t + 1)
                            gates_of(w_h, h2, 2 * x, then)
                            gates_of(w_h, h2, 2 * x + 1, then)
                            if x == 0:
                                by_columns(OUT, slice(0, BATCH), w_o[:, :], h2[:, :], True, False)
                            for c in range(2):
                                pe.wait_ge(S["pT_ready"], t * 4 + 2 * x + c + 1)
                                for i in range(HALF):
                                    for j in range(4):
                                        last = nc.tensor.matmul(PS[32 * j:32 * j + 8, CTX, 0:D], pT[x][:, c, j, i, :],
                                                                rows[:, 8 * j + HALF * x + i, c, :],
                                                                start=x + i + c == 0, stop=x * c * i == HALF - 1)
                        last.then_inc(S["summed"], 1)
                        pe.wait_ge(S["share_ready"], t + 1)
                        by_columns(OUT, slice(0, BATCH), lastrow[:, :],
                                   last_share[:, :, :].rearrange("p j i -> p (j i)"), False, False)
                        pe.wait_ge(S["cx_ready"], t + 1)
                        by_columns(OUT, slice(0, BATCH), cx[:, :], share[:, :, :].rearrange("p j i -> p (j i)"),
                                   False, True).then_inc(S["out_done"], 1)
                nc.tensor.matmul(PS[:, GATES[0], 0:1], ident, gx[:, SEQ, 0, 0:1], start=False, stop=True)

            @block.scalar
            def _(act):
                with act.Fori(0, SEQ // STEPS) as turn:
                    for t, now in zip(steps_of(turn), GATES * (STEPS // 2)):
                        act.wait_ge(S["gates_done"], t + 1)
                        nc.scalar.activation(gt[:, :, :].rearrange("p g b -> p (g b)"), PS[:, now, 0:4 * BATCH], ACT.Tanh
                                             ).then_inc(S["tanh_ready"], 1)
                        act.wait_ge(S["c_ready"], t + 1)
                        nc.scalar.activation(tc[:, :], c2[:, :], ACT.Tanh, scale=0.5).then_inc(S["tanh_c_ready"], 1)
                        for x in range(2):
                            act.wait_ge(S["top_ready"], t * 2 + x + 1)
                            nc.scalar.activation(probs[x][:, :], PS[:, SCORES[x], 0:KEYS], ACT.Exp, bias=ntop[x][:, :],
                                                 accum_out=total[x][:, :]).then_inc(S["exped"], 1)
                        act.wait_ge(S["out_done"], t + 1)
                        nc.scalar.activation(attn[:, :], PS[:, OUT, 0:BATCH], ACT.Tanh, bias=w("ob")
                                             ).then_inc(S["attn_ready"], 1)
                        act.drain()
                        nc.scalar.copy(outs[:, :, bass.ds(t, 1)].rearrange("p b o -> p (b o)"), attn[:, :])

            @block.vector
            def _(dve):
                def by_row(values):
                    return values.rearrange("p (j i) -> p j i", i=8)

                def spread_rows(out, values, x):
                    mine = own_row[:, HALF * x:HALF * (x + 1), :]
                    return nc.vector.tensor_tensor(out, values.unsqueeze(3).broadcast_to([P, 4, HALF, 8]),
                                                   over(mine, 1, [P, 4, HALF, 8]), ALU.mult)

                with dve.Fori(0, SEQ // STEPS) as turn:
                    for t in steps_of(turn):
                        dve.wait_ge(S["tanh_ready"], t + 1)
                        nc.vector.scalar_tensor_tensor(u[:, :], gt[:, 0, :], 1.0, gt[:, 3, :], ALU.add, ALU.mult)
                        nc.vector.scalar_tensor_tensor(f[:, :], gt[:, 1, :], 1.0, c2[:, :], ALU.add, ALU.mult)
                        dve.drain()
                        nc.vector.scalar_tensor_tensor(c2[:, :], f[:, :], 0.5, u[:, :], ALU.mult, ALU.add
                                                       ).then_inc(S["c_ready"], 1)
                        nc.vector.scalar_tensor_tensor(gate_spread[:, :, :, :], by_row(gt[:, 2, :]).unsqueeze(3)
                                                       .broadcast_to([P, 4, 8, 8]), 1.0,
                                                       over(own_row, 1, [P, 4, 8, 8]), ALU.add, ALU.mult)
                        dve.drain()
                        dve.wait_ge(S["tanh_c_ready"], t + 1)
                        for x in range(2):
                            i = slice(HALF * x, HALF * (x + 1))
                            nc.vector.tensor_tensor(hbd[:, :, i, :], gate_spread[:, :, i, :],
                                                    by_row(tc[:, :])[:, :, i].unsqueeze(3)
                                                    .broadcast_to([P, 4, HALF, 8]), ALU.mult
                                                    ).then_inc(S["h_spread"], 1)
                        nc.vector.scalar_tensor_tensor(h2[:, :], gt[:, 2, :], 1.0, tc[:, :], ALU.add, ALU.mult
                                                       ).then_inc(S["h_ready"], 1)
                        for x in range(2):
                            dve.wait_ge(S["scored"], t * 2 + x + 1)
                            nc.vector.tensor_reduce(ntop[x][:, :], PS[:, SCORES[x], 0:KEYS], AX.X, ALU.max, negate=True
                                                    ).then_inc(S["top_ready"], 1)
                        for x in range(2):
                            dve.wait_ge(S["turned"], t * 2 + x + 1)
                            for c in range(2):
                                cols = PS[:, TURNED[x], c * P:(c + 1) * P].rearrange("p (j i) -> p j i", i=32)
                                spread_rows(pT[x][:, c, :, :, :], cols[:, :, HALF * x:HALF * (x + 1)], x
                                            ).then_inc(S["pT_ready"], 1)
                            nc.vector.reciprocal(inv[x][:, :], total[x][:, :])
                            dve.drain()
                            i = slice(HALF * x, HALF * (x + 1))
                            of_row = batch_of_row.rearrange("p (j i) -> p j i", i=8)[:, :, i]
                            nc.vector.tensor_scalar(share[:, :, i], of_row, inv[x][:, :], None, ALU.mult)
                            dve.drain()
                            last = nc.vector.tensor_scalar(last_share[:, :, i], share[:, :, i],
                                                           probs[x][:, KEYS - 1:KEYS], None, ALU.mult)
                        last.then_inc(S["share_ready"], 1)
                        dve.wait_ge(S["summed"], t + 1)
                        nc.vector.tensor_copy(cx[:, :], PS[:, CTX, 0:D]).then_inc(S["cx_ready"], 1)

        with nc.Block() as block:
            @block.tensor
            def _(pe):
                flat = outs[:, :, :].rearrange("p b t -> p (b t)")
                for t in range(TILES):
                    last = nc.tensor.transpose(PS[:, 6 + t // 4, (t % 4) * P:(t % 4 + 1) * P],
                                               flat[:, t * P:(t + 1) * P], ident)
                last.then_inc(S["outs_turned"], 1)

            @block.vector
            def _(dve):
                dve.wait_ge(S["outs_turned"], 1)
                nc.vector.tensor_tensor(X[:, :, :], X[:, :, :], PS[:, 6:8, :].rearrange("p h (t d) -> p (h t) d", t=4),
                                        ALU.add)


def perceiver(nc, dram, wcols, ccols, x_in, out):
    with ExitStack() as top:
        env = Env(nc, top)
        env.wcols, env.ccols = wcols, ccols
        env.W = env.sb(top, "weights", [P, dram["weights"].shape[1]])
        env.C = env.sb(top, "constants", [P, dram["constants"].shape[1]])
        env.PS = top.enter_context(nc.psum_tensor("banks", [P, 8, BANK], F32))
        X = env.sb(top, "X", [P, TILES, D])
        zT = env.sb(top, "zT", [P, TOKENS])
        ctxT = env.sb(top, "ctxT", [P, BATCH, KEYS])
        mask_in = env.sb(top, "mask_words", [P, KEYS, 2], mybir.dt.int32)
        mask = env.sb(top, "mask", [P, KEYS])
        x_loaded, ctx_loaded, rest_loaded, rows_loaded, stored = (
            top.enter_context(nc.semaphore(n))
            for n in ("x_loaded", "ctx_loaded", "rest_loaded", "rows_loaded", "stored"))

        with nc.Block() as block:
            @block.sync
            def _(sp):
                first = wcols["L0x_ob"][1]
                sp.dma_start(X[:, :, :], x_in.rearrange("(t b) s d -> (b s) t d", b=PER_TILE)).then_inc(x_loaded, 16)
                sp.dma_start(env.C[:, :], dram["constants"]).then_inc(x_loaded, 16)
                sp.dma_start(env.W[:, 0:first], dram["weights"][:, 0:first]).then_inc(x_loaded, 16)
                sp.dma_start(ctxT[:, :, :], dram["ctxT"]).then_inc(ctx_loaded, 16)
                sp.dma_start(env.W[:, first:], dram["weights"][:, first:]).then_inc(rest_loaded, 16)
                for j in range(PER_TILE):
                    sp.dma_start(mask_in[32 * j:32 * j + 32, :, :].rearrange("p k w -> p (k w)"),
                                 dram["mask"].bitcast(mybir.dt.int32)).then_inc(rest_loaded, 16)
                sp.wait_ge(x_loaded, 3 * LOADED)

        def level0():
            with ExitStack() as s:
                qT = env.sb(s, "qT", [P, TOKENS])
                norm_transpose(env, X, zT, onward=(qT, env.w("L0x_q"), env.w("L0x_qb")))
                with nc.Block() as block:
                    @block.sync
                    def _(sp):
                        sp.wait_ge(ctx_loaded, LOADED)
                cross_attention(env, "L0x_", X, ctxT, qT, 16, 16 ** -0.5, True)
            with nc.Block() as block:
                @block.vector
                def _(dve):
                    dve.wait_ge(rest_loaded, 5 * LOADED)
                    nc.vector.tensor_scalar(mask[:, :], mask_in[:, :, 0], -1.0, -MASKED, ALU.add, ALU.mult)
            norm_transpose(env, X, zT)
            self_attention(env, "L0a_", X, zT, zT, 8 ** -0.5, causal=True)
            with ExitStack() as s:
                z = env.sb(s, "z", [P, TILES, D])
                norm_transpose(env, X, None, keep=z)
                int8_matmul(env, X, z)

        def level1():
            with ExitStack() as s:
                qT = env.sb(s, "qT", [P, TOKENS])
                norm_transpose(env, X, zT, onward=(qT, env.w("L1x_q"), None))
                cross_attention(env, "L1x_", X, ctxT, qT, 8, 8 ** -0.5, False)
            norm_transpose(env, X, zT)
            laplacian_attention(env, X, zT, dram["buckets"])
            mixture("L1f_", 16, 512, 2 * TOKENS // 16, ACT.Gelu, 8 ** -0.5, True)

        def mixture(layer, n, hidden, capacity, func, scale, causal):
            eps = float(np.finfo(np.float32).eps)
            with ExitStack() as s:
                Y = env.sb(s, "Y", [P, TILES, D])
                acc = env.sb(s, "acc", [P, TILES, D])
                gates = env.sb(s, "gates", [P, TILES, n])
                gatesT = env.sb(s, "gatesT", [n, TOKENS])
                norm_transpose(env, X, None, keep=Y)
                norm_transpose(env, Y, zT, scale=env.w(layer + "ln1w"), shift=env.w(layer + "ln1b"))
                self_attention(env, layer, Y, zT, zT, scale, causal=causal)
                scale2, shift2, rest = env.w(layer + "ln2w"), env.w(layer + "ln2b"), (env.w(layer + "b2"), n, hidden, func)
                if capacity <= P:
                    z = env.sb(s, "z", [P, TILES, D])
                    places = env.sb(s, "places", [P, TILES, n])
                    norm_transpose(env, Y, zT, keep=z, scale=scale2, shift=shift2)
                    route(env, gates, gatesT, zT, env.w(layer + "r"), n, capacity, eps, DROP, places)
                    dispatched_experts(env, acc, z, scale2, shift2, gates, gatesT, places, dram[layer + "experts"], *rest)
                else:
                    norm_transpose(env, Y, zT, scale=scale2, shift=shift2)
                    route(env, gates, gatesT, zT, env.w(layer + "r"), n, capacity, eps, DROP)
                    experts(env, acc, zT, gates, gatesT, dram[layer + "experts"], *rest)
                add_to(env, X, (Y, acc))

        def level2():
            norm_transpose(env, X, zT)
            context_lstm(env, X, zT, ctxT)
            with ExitStack() as s:
                latent = env.sb(s, "latentT", [P, TOKENS])
                norm_transpose(env, X, zT, onward=(latent, env.w("L2a_down"), None))
                self_attention(env, "L2a_", X, zT, latent, 40 ** -0.5, causal=True, biases=False, qk_rope=True)
            mixture("L2f_", 8, 512, TOKENS // 4, ACT.Relu, 8 ** -0.5, False)

        def level3():
            with ExitStack() as s:
                ctx_rows = env.sb(s, "ctx_rows", [KCH, BATCH, 3, D])
                with nc.Block() as block:
                    @block.sync
                    def _(sp):
                        sp.dma_start(ctx_rows[:, :, :, :], dram["ctx_rows"]).then_inc(rows_loaded, 16)
                qT = env.sb(s, "qT", [P, TOKENS])
                norm_transpose(env, X, zT, onward=(qT, env.w("L3x_q"), env.w("L3x_qb")))
                single_cross_attention(env, "L3x_", X, ctxT, ctx_rows, rows_loaded, qT, mask, 128 ** -0.5)
            norm_transpose(env, X, zT)
            self_attention(env, "L3a_", X, zT, zT, 8 ** -0.5, causal=True, biases=False, rope="pair")
            with ExitStack() as s:
                acc = env.sb(s, "acc", [P, TILES, D])
                gates = env.sb(s, "gates", [P, TILES, 8])
                gatesT = env.sb(s, "gatesT", [8, TOKENS])
                norm_transpose(env, X, zT)
                route(env, gates, gatesT, zT, env.w("L3f_r"), 8, None, 1e-12, 1.0)
                experts(env, acc, zT, gates, gatesT, dram["L3f_experts"], env.w("L3f_b2"), 8, 256, ACT.Relu)
                add_to(env, X, (acc,))

        for level in (level0, level1, level2, level3):
            level()

        with nc.Block() as block:
            @block.sync
            def _(sp):
                sp.dma_start(out.rearrange("(t b) s d -> (b s) t d", b=PER_TILE), X[:, :, :]).then_inc(stored, 16)
                sp.wait_ge(stored, 16)


def kernel(**inputs):
    import concourse.bacc as _bacc
    from concourse.bass_utils import run_bass_kernel_spmd as _run

    nc = _bacc.Bacc("TRN2", target_bir_lowering=False, num_devices=1)
    weights, tables = packed_weights(inputs), constants()

    def columns(parts):
        where, at = {}, 0
        for name, a in parts.items():
            where[name] = (at, at + a.shape[1])
            at += a.shape[1]
        return where, np.concatenate(list(parts.values()), axis=1)

    wcols, weights = columns(weights)
    ccols, tables = columns(tables)
    ctx = np.asarray(inputs["ctx_1024"])
    ctxT, ctx_rows = ctx.transpose(2, 0, 1), chunked_rows(ctx)
    arrays = {
        "x": inputs["x"], "weights": weights, "constants": tables, "buckets": bucket_rows(),
        "mask": np.asarray(inputs["mask_SxS2_bk0"]).astype(np.int64),
        "ctxT": ctxT, "ctx_rows": ctx_rows,
        "L1f_experts": packed_experts(inputs["L1_ffn_fc1_w"], inputs["L1_ffn_fc1_b"], inputs["L1_ffn_fc2_w"]),
        "L2f_experts": packed_experts(inputs["L2_ffn_w1"], inputs["L2_ffn_b1"], inputs["L2_ffn_w2"]),
        "L3f_experts": packed_experts(inputs["L3_ffn_W1"], inputs["L3_ffn_b1"], inputs["L3_ffn_W2"]),
    }
    arrays = {k: np.ascontiguousarray(v) for k, v in arrays.items()}
    dram = {k: nc.dram_tensor(k + "_dram", v.shape, mybir.dt.from_np(v.dtype), kind="ExternalInput").ap()
            for k, v in arrays.items()}
    out = nc.dram_tensor("out_dram", (BATCH, SEQ, D), F32, kind="ExternalOutput").ap()
    perceiver(nc, dram, wcols, ccols, dram["x"], out)
    r = _run(nc, [{k + "_dram": v for k, v in arrays.items()}], core_ids=[0])
    return r.results[0]["out_dram"]
```
